# Optimizing a Trainium2 kernel written in Bass

```python
import numpy as np
import jax
import jax.numpy as jnp

def _softmax(x, axis=-1):
    return jax.nn.softmax(x, axis=axis)

def _gelu(x):
    return jax.nn.gelu(x, approximate=True)

def _silu(x):
    return jax.nn.silu(x)

def _sigmoid(x):
    return jax.nn.sigmoid(x)

def _layernorm(x, axis=-1, eps=1e-05):
    m = jnp.mean(x, axis=axis, keepdims=True)
    v = jnp.var(x, axis=axis, keepdims=True)
    return (x - m) / jnp.sqrt(v + eps)

def _scatter_add(tgt, idx, src, axis=0):
    return tgt.at[idx].add(src)

def _segment_sum(src, seg, n):
    return jax.ops.segment_sum(src, seg, n)
kernel_name = 'mk_gnn_preln_d4_gnn_r64_845fe5'

def setup_inputs(seed: int=0):
    np.random.seed(seed)
    _w = jnp.asarray

    def _rec_inputs():
        import jax
        import jax.numpy as jnp
        _gk = jax.random.key(seed)
        x = -0.0005121 + 1.001 * jax.random.normal(jax.random.fold_in(_gk, 1), (100000, 32), jnp.float32)
        src = jax.random.randint(jax.random.fold_in(_gk, 2), (25000,), 0, 100000, jnp.int32)
        dst = jax.random.randint(jax.random.fold_in(_gk, 3), (25000,), 0, 100000, jnp.int32)
        _o = jnp.argsort(dst, stable=True)
        src = src[_o]
        dst = dst[_o]
        edge_attr_32 = -0.00010739 + 0.99994 * jax.random.normal(jax.random.fold_in(_gk, 12), (25000, 32), jnp.float32)
        edge_attr_4 = jax.random.uniform(jax.random.fold_in(_gk, 13), (25000, 4), jnp.float32, 0.0, 1)
        edge_type_8 = jax.random.randint(jax.random.fold_in(_gk, 15), (25000,), 0, 8, jnp.int32)
        return (x, src, dst, edge_attr_32, edge_attr_4, edge_type_8)
    x, src, dst, edge_attr_32, edge_attr_4, edge_type_8 = _rec_inputs()

    def _L0_gnn_setup():
        import jax, jax.numpy as jnp
        import numpy as np
        N_NODES = 100000
        N_EDGES = 25000
        D_IN, D_HID, D_OUT = (32, 64, 32)

        def sage_conv(x, edge_index, W_l, b_l, W_r, num_segments):
            src, dst = (edge_index[0], edge_index[1])
            agg = jax.ops.segment_sum(x[src], dst, num_segments=num_segments)
            return agg @ W_l.T + b_l + x @ W_r.T
        key = jax.random.key(seed)
        ks = jax.random.split(key, 8)
        x = jax.random.normal(ks[0], (N_NODES, D_IN), dtype=jnp.float32)
        edge_index = jax.random.randint(ks[1], (2, N_EDGES), 0, N_NODES, dtype=jnp.int64)
        s_in = 1.0 / np.sqrt(D_IN)
        s_hid = 1.0 / np.sqrt(D_HID)
        W_l_in = jax.random.normal(ks[2], (D_HID, D_IN), dtype=jnp.float32) * s_in
        b_l_in = jnp.zeros((D_HID,), dtype=jnp.float32)
        W_r_in = jax.random.normal(ks[3], (D_HID, D_IN), dtype=jnp.float32) * s_in
        W_l_out = jax.random.normal(ks[4], (D_OUT, D_HID), dtype=jnp.float32) * s_hid
        b_l_out = jnp.zeros((D_OUT,), dtype=jnp.float32)
        W_r_out = jax.random.normal(ks[5], (D_OUT, D_HID), dtype=jnp.float32) * s_hid
        return {'x': x, 'edge_index': edge_index, 'W_l_in': W_l_in, 'b_l_in': b_l_in, 'W_r_in': W_r_in, 'W_l_out': W_l_out, 'b_l_out': b_l_out, 'W_r_out': W_r_out}
    _L0_gnn_all = _L0_gnn_setup()
    _L0_gnn_in = {k: v for k, v in _L0_gnn_all.items() if k in ('W_l_in', 'b_l_in', 'W_r_in', 'W_l_out', 'b_l_out', 'W_r_out')}
    del _L0_gnn_all

    def _L1_gnn_setup():
        import jax, jax.numpy as jnp
        import numpy as np
        N_NODES = 100000
        N_EDGES = 25000
        IN_F = 32
        HID = 128

        def _gcn_norm(edge_index, n_nodes):
            loops = jnp.arange(n_nodes, dtype=edge_index.dtype)
            src = jnp.concatenate([edge_index[0], loops])
            dst = jnp.concatenate([edge_index[1], loops])
            ones = jnp.ones(src.shape[0], dtype=jnp.float32)
            deg = jax.ops.segment_sum(ones, dst, num_segments=n_nodes)
            deg_inv_sqrt = jnp.where(deg > 0, jax.lax.rsqrt(deg), 0.0)
            norm = deg_inv_sqrt[src] * deg_inv_sqrt[dst]
            return (src, dst, norm)

        def _gcn_conv(x, src, dst, norm, W, b, n_nodes):
            h = x @ W
            msg = h[src] * norm[:, None]
            out = jax.ops.segment_sum(msg, dst, num_segments=n_nodes)
            return out + b
        key = jax.random.key(seed)
        ks = jax.random.split(key, 8)
        x = jax.random.normal(ks[0], (N_NODES, IN_F), dtype=jnp.float32)
        edge_index = jax.random.randint(ks[1], (2, N_EDGES), 0, N_NODES, dtype=jnp.int64)
        W1 = jax.random.normal(ks[2], (IN_F, HID), dtype=jnp.float32) / np.sqrt(IN_F)
        b1 = jnp.zeros((HID,), dtype=jnp.float32)
        W2 = jax.random.normal(ks[3], (HID, HID), dtype=jnp.float32) / np.sqrt(HID)
        b2 = jnp.zeros((HID,), dtype=jnp.float32)
        W3 = jax.random.normal(ks[4], (HID, IN_F), dtype=jnp.float32) / np.sqrt(HID)
        b3 = jnp.zeros((IN_F,), dtype=jnp.float32)
        return {'x': x, 'edge_index': edge_index, 'W1': W1, 'b1': b1, 'W2': W2, 'b2': b2, 'W3': W3, 'b3': b3}
    _L1_gnn_all = _L1_gnn_setup()
    _L1_gnn_in = {k: v for k, v in _L1_gnn_all.items() if k in ('W1', 'b1', 'W2', 'b2', 'W3', 'b3')}
    del _L1_gnn_all

    def _L2_gnn_setup():
        import jax, jax.numpy as jnp
        import numpy as np
        N_NODES = 100000
        N_EDGES = 6250
        D = 32
        EH = 128
        STEPS = 6

        def _gru_cell(x, h, wih, whh, bih, bhh):
            gi = x @ wih.T + bih
            gh = h @ whh.T + bhh
            ir, iz, inn = jnp.split(gi, 3, axis=-1)
            hr, hz, hn = jnp.split(gh, 3, axis=-1)
            r = jax.nn.sigmoid(ir + hr)
            z = jax.nn.sigmoid(iz + hz)
            n = jnp.tanh(inn + r * hn)
            return (1.0 - z) * n + z * h
        key = jax.random.key(seed)
        ks = jax.random.split(key, 12)
        s = 0.05
        return {'n_feat': jax.random.normal(ks[0], (N_NODES, D), jnp.float32), 'e_feat': jax.random.normal(ks[1], (N_EDGES, D), jnp.float32), 'src': jax.random.randint(ks[2], (N_EDGES,), 0, N_NODES, jnp.int32), 'dst': jax.random.randint(ks[3], (N_EDGES,), 0, N_NODES, jnp.int32), 'lin0_w': jax.random.normal(ks[4], (D, D), jnp.float32) * s, 'lin0_b': jnp.zeros((D,), jnp.float32), 'en1_w': jax.random.normal(ks[5], (EH, D), jnp.float32) * s, 'en1_b': jnp.zeros((EH,), jnp.float32), 'en2_w': jax.random.normal(ks[6], (D * D, EH), jnp.float32) * s, 'en2_b': jnp.zeros((D * D,), jnp.float32), 'conv_bias': jnp.zeros((D,), jnp.float32), 'gru_wih': jax.random.normal(ks[7], (3 * D, D), jnp.float32) * s, 'gru_whh': jax.random.normal(ks[8], (3 * D, D), jnp.float32) * s, 'gru_bih': jnp.zeros((3 * D,), jnp.float32), 'gru_bhh': jnp.zeros((3 * D,), jnp.float32)}
    _L2_gnn_all = _L2_gnn_setup()
    _L2_gnn_in = {k: v for k, v in _L2_gnn_all.items() if k in ('lin0_w', 'lin0_b', 'en1_w', 'en1_b', 'en2_w', 'en2_b', 'conv_bias', 'gru_wih', 'gru_whh', 'gru_bih', 'gru_bhh')}
    del _L2_gnn_all

    def _L3_gnn_setup():
        import jax, jax.numpy as jnp
        import numpy as np
        N = 50000
        E = 12500
        IN = 32
        H = 32
        OUT = 32
        R = 8
        Q = 4

        def _xavier(key, shape):
            gain = 5.0 / 3.0
            fan_in, fan_out = (shape[-2], shape[-1])
            limit = gain * np.sqrt(6.0 / (fan_in + fan_out))
            return jax.random.uniform(key, shape, jnp.float32, -limit, limit)

        def _layer(h, W, b, src, dst, etypes, tv):
            hp = jnp.einsum('ni,rqio->nrqo', h, W)
            msg = jnp.einsum('eq,eqo->eo', tv, hp[src, etypes])
            msg = msg + jnp.einsum('eq,eqo->eo', tv, b[etypes])
            return jax.ops.segment_sum(msg, dst, num_segments=h.shape[0])
        key = jax.random.key(seed)
        ks = jax.random.split(key, 7)
        feat = jax.random.normal(ks[0], (N, IN), jnp.float32)
        src = jax.random.randint(ks[1], (E,), 0, N, dtype=jnp.int32)
        dst = jax.random.randint(ks[2], (E,), 0, N, dtype=jnp.int32)
        etypes = jax.random.randint(ks[3], (E,), 0, R, dtype=jnp.int32)
        truth_value = jax.random.uniform(ks[4], (E, Q), jnp.float32)
        W1 = _xavier(ks[5], (R, Q, IN, H))
        W2 = _xavier(ks[6], (R, Q, H, OUT))
        b1 = jnp.zeros((R, Q, H), jnp.float32)
        b2 = jnp.zeros((R, Q, OUT), jnp.float32)
        return dict(feat=feat, truth_value=truth_value, W1=W1, b1=b1, W2=W2, b2=b2, src=src, dst=dst, etypes=etypes)
    _L3_gnn_all = _L3_gnn_setup()
    _L3_gnn_in = {k: v for k, v in _L3_gnn_all.items() if k in ('W1', 'b1', 'W2', 'b2')}
    del _L3_gnn_all
    return {'x': x, 'src': src, 'dst': dst, 'edge_attr_32': edge_attr_32, 'edge_attr_4': edge_attr_4, 'edge_type_8': edge_type_8, 'L0_gnn_W_l_in': _L0_gnn_in['W_l_in'], 'L0_gnn_b_l_in': _L0_gnn_in['b_l_in'], 'L0_gnn_W_r_in': _L0_gnn_in['W_r_in'], 'L0_gnn_W_l_out': _L0_gnn_in['W_l_out'], 'L0_gnn_b_l_out': _L0_gnn_in['b_l_out'], 'L0_gnn_W_r_out': _L0_gnn_in['W_r_out'], 'L1_gnn_W1': _L1_gnn_in['W1'], 'L1_gnn_b1': _L1_gnn_in['b1'], 'L1_gnn_W2': _L1_gnn_in['W2'], 'L1_gnn_b2': _L1_gnn_in['b2'], 'L1_gnn_W3': _L1_gnn_in['W3'], 'L1_gnn_b3': _L1_gnn_in['b3'], 'L2_gnn_lin0_w': _L2_gnn_in['lin0_w'], 'L2_gnn_lin0_b': _L2_gnn_in['lin0_b'], 'L2_gnn_en1_w': _L2_gnn_in['en1_w'], 'L2_gnn_en1_b': _L2_gnn_in['en1_b'], 'L2_gnn_en2_w': _L2_gnn_in['en2_w'], 'L2_gnn_en2_b': _L2_gnn_in['en2_b'], 'L2_gnn_conv_bias': _L2_gnn_in['conv_bias'], 'L2_gnn_gru_wih': _L2_gnn_in['gru_wih'], 'L2_gnn_gru_whh': _L2_gnn_in['gru_whh'], 'L2_gnn_gru_bih': _L2_gnn_in['gru_bih'], 'L2_gnn_gru_bhh': _L2_gnn_in['gru_bhh'], 'L3_gnn_W1': _L3_gnn_in['W1'], 'L3_gnn_b1': _L3_gnn_in['b1'], 'L3_gnn_W2': _L3_gnn_in['W2'], 'L3_gnn_b2': _L3_gnn_in['b2']}

def reference(x, src, dst, edge_attr_32, edge_attr_4, edge_type_8, L0_gnn_W_l_in, L0_gnn_b_l_in, L0_gnn_W_r_in, L0_gnn_W_l_out, L0_gnn_b_l_out, L0_gnn_W_r_out, L1_gnn_W1, L1_gnn_b1, L1_gnn_W2, L1_gnn_b2, L1_gnn_W3, L1_gnn_b3, L2_gnn_lin0_w, L2_gnn_lin0_b, L2_gnn_en1_w, L2_gnn_en1_b, L2_gnn_en2_w, L2_gnn_en2_b, L2_gnn_conv_bias, L2_gnn_gru_wih, L2_gnn_gru_whh, L2_gnn_gru_bih, L2_gnn_gru_bhh, L3_gnn_W1, L3_gnn_b1, L3_gnn_W2, L3_gnn_b2):
    import jax
    import jax.numpy as jnp

    def _L0_gnn_ref(x, edge_index, W_l_in, b_l_in, W_r_in, W_l_out, b_l_out, W_r_out):
        import jax, jax.numpy as jnp
        import numpy as np
        N_NODES = 100000
        N_EDGES = 25000
        D_IN, D_HID, D_OUT = (32, 64, 32)

        def sage_conv(x, edge_index, W_l, b_l, W_r, num_segments):
            src, dst = (edge_index[0], edge_index[1])
            agg = jax.ops.segment_sum(x[src], dst, num_segments=num_segments)
            return agg @ W_l.T + b_l + x @ W_r.T
        n = x.shape[0]
        h = sage_conv(x, edge_index, W_l_in, b_l_in, W_r_in, n)
        h = jax.nn.relu(h)
        out = sage_conv(h, edge_index, W_l_out, b_l_out, W_r_out, n)
        return out

    def _L1_gnn_ref(x, edge_index, W1, b1, W2, b2, W3, b3):
        import jax, jax.numpy as jnp
        import numpy as np
        N_NODES = 100000
        N_EDGES = 25000
        IN_F = 32
        HID = 128

        def _gcn_norm(edge_index, n_nodes):
            loops = jnp.arange(n_nodes, dtype=edge_index.dtype)
            src = jnp.concatenate([edge_index[0], loops])
            dst = jnp.concatenate([edge_index[1], loops])
            ones = jnp.ones(src.shape[0], dtype=jnp.float32)
            deg = jax.ops.segment_sum(ones, dst, num_segments=n_nodes)
            deg_inv_sqrt = jnp.where(deg > 0, jax.lax.rsqrt(deg), 0.0)
            norm = deg_inv_sqrt[src] * deg_inv_sqrt[dst]
            return (src, dst, norm)

        def _gcn_conv(x, src, dst, norm, W, b, n_nodes):
            h = x @ W
            msg = h[src] * norm[:, None]
            out = jax.ops.segment_sum(msg, dst, num_segments=n_nodes)
            return out + b
        n = x.shape[0]
        src, dst, norm = _gcn_norm(edge_index, n)
        h = jax.nn.relu(_gcn_conv(x, src, dst, norm, W1, b1, n))
        h = jax.nn.relu(_gcn_conv(h, src, dst, norm, W2, b2, n))
        h = jax.nn.relu(_gcn_conv(h, src, dst, norm, W3, b3, n))
        return h

    def _L2_gnn_ref(n_feat, e_feat, src, dst, lin0_w, lin0_b, en1_w, en1_b, en2_w, en2_b, conv_bias, gru_wih, gru_whh, gru_bih, gru_bhh):
        import jax, jax.numpy as jnp
        import numpy as np
        N_NODES = 100000
        N_EDGES = 6250
        D = 32
        EH = 128
        STEPS = 6

        def _gru_cell(x, h, wih, whh, bih, bhh):
            gi = x @ wih.T + bih
            gh = h @ whh.T + bhh
            ir, iz, inn = jnp.split(gi, 3, axis=-1)
            hr, hz, hn = jnp.split(gh, 3, axis=-1)
            r = jax.nn.sigmoid(ir + hr)
            z = jax.nn.sigmoid(iz + hz)
            n = jnp.tanh(inn + r * hn)
            return (1.0 - z) * n + z * h
        n_nodes = n_feat.shape[0]
        out = jax.nn.relu(n_feat @ lin0_w.T + lin0_b)
        h = out
        eh = jax.nn.relu(e_feat @ en1_w.T + en1_b)
        w_e = (eh @ en2_w.T + en2_b).reshape(-1, D, D)
        for _ in range(STEPS):
            msg = jnp.einsum('ei,eio->eo', out[src], w_e)
            agg = jax.ops.segment_sum(msg, dst, num_segments=n_nodes) + conv_bias
            m = jax.nn.relu(agg)
            h = _gru_cell(m, h, gru_wih, gru_whh, gru_bih, gru_bhh)
            out = h
        return out

    def _L3_gnn_ref(feat, truth_value, W1, b1, W2, b2, src, dst, etypes):
        import jax, jax.numpy as jnp
        import numpy as np
        N = 50000
        E = 12500
        IN = 32
        H = 32
        OUT = 32
        R = 8
        Q = 4

        def _xavier(key, shape):
            gain = 5.0 / 3.0
            fan_in, fan_out = (shape[-2], shape[-1])
            limit = gain * np.sqrt(6.0 / (fan_in + fan_out))
            return jax.random.uniform(key, shape, jnp.float32, -limit, limit)

        def _layer(h, W, b, src, dst, etypes, tv):
            hp = jnp.einsum('ni,rqio->nrqo', h, W)
            msg = jnp.einsum('eq,eqo->eo', tv, hp[src, etypes])
            msg = msg + jnp.einsum('eq,eqo->eo', tv, b[etypes])
            return jax.ops.segment_sum(msg, dst, num_segments=h.shape[0])
        x = jnp.tanh(_layer(feat, W1, b1, src, dst, etypes, truth_value))
        return _layer(x, W2, b2, src, dst, etypes, truth_value)
    edge_index = jnp.stack([src, dst])
    h = jnp.maximum(_layernorm(x, axis=-1), 0.0)
    x = x + _L0_gnn_ref(h, edge_index, L0_gnn_W_l_in, L0_gnn_b_l_in, L0_gnn_W_r_in, L0_gnn_W_l_out, L0_gnn_b_l_out, L0_gnn_W_r_out)
    h = jnp.maximum(_layernorm(x, axis=-1), 0.0)
    x = x + _L1_gnn_ref(h, edge_index, L1_gnn_W1, L1_gnn_b1, L1_gnn_W2, L1_gnn_b2, L1_gnn_W3, L1_gnn_b3)
    h = jnp.maximum(_layernorm(x, axis=-1), 0.0)
    x = x + _L2_gnn_ref(h, edge_attr_32, src, dst, L2_gnn_lin0_w, L2_gnn_lin0_b, L2_gnn_en1_w, L2_gnn_en1_b, L2_gnn_en2_w, L2_gnn_en2_b, L2_gnn_conv_bias, L2_gnn_gru_wih, L2_gnn_gru_whh, L2_gnn_gru_bih, L2_gnn_gru_bhh)
    h = jnp.maximum(_layernorm(x, axis=-1), 0.0)
    x = x + _L3_gnn_ref(h, edge_attr_4, L3_gnn_W1, L3_gnn_b1, L3_gnn_W2, L3_gnn_b2, src, dst, edge_type_8)
    return x

_drawn_inputs = setup_inputs


def setup_inputs(seed=0):
    import zlib

    import numpy as np

    out = dict(_drawn_inputs(seed))
    spreads = {'L0_gnn_b_l_in': (0.0, 0.1),
     'L0_gnn_b_l_out': (0.0, 0.1),
     'L1_gnn_b1': (0.0, 0.1),
     'L1_gnn_b2': (0.0, 0.1),
     'L1_gnn_b3': (0.0, 0.1),
     'L2_gnn_lin0_b': (0.0, 0.8),
     'L2_gnn_en1_b': (0.0, 0.8),
     'L2_gnn_en2_b': (0.0, 0.8),
     'L2_gnn_conv_bias': (0.0, 0.631),
     'L2_gnn_gru_bih': (0.0, 0.1),
     'L2_gnn_gru_bhh': (0.0, 0.1),
     'L3_gnn_b1': (0.0, 0.306),
     'L3_gnn_b2': (0.0, 0.1)}
    factors = {'edge_attr_32': 8.0,
     'L2_gnn_lin0_w': 8.0,
     'L2_gnn_en1_w': 8.0,
     'L2_gnn_en2_w': 8.0,
     'L2_gnn_gru_wih': 4.255,
     'L2_gnn_gru_whh': 4.114}
    for name, (base, spread) in spreads.items():
        noise = np.random.default_rng([zlib.crc32(name.encode()), seed]).standard_normal(out[name].shape)
        drawn = base * np.exp(spread * noise) if base else spread * noise
        out[name] = jnp.asarray(drawn.astype(out[name].dtype))
    for name, factor in factors.items():
        out[name] = (out[name] * factor).astype(out[name].dtype)
    return out
```

```python
from contextlib import ExitStack

import numpy as np

import concourse.bass as bass
from concourse import mybir

P = 128
W = 512
Q = W // P
T = 4
D = 32
H0 = 64
H1 = 128
R = 8
STEPS = 6
TILES = Q * T
BIG = 1 << 22
CREDIT = 4

ALU = mybir.AluOpType
ACT = mybir.ActivationFunctionType
BF16 = mybir.dt.bfloat16
F32 = mybir.dt.float32
I32 = mybir.dt.int32
AX_X = mybir.AxisListType.X
SPACES = (0, 1)
S_, D_ = SPACES

MATS = ["ident", "center", "next_quarter", "prev_quarter"] + [f"spread{t}" for t in range(T)] + ["member_mean"]
WEIGHTS = (["l0_l0", "l0_l1", "l0_r0", "l0_r1", "l0_ol0", "l0_ol1", "l0_or0", "l0_or1"]
           + [f"w1_{t}" for t in range(T)] + ["w2"] + [f"w3_{t}" for t in range(T)]
           + ["lin0", "ir", "iz", "in", "hr", "hz", "hn", "en2b"])
BIASES = ["b_in", "b_out", "b1", "b2", "b3", "lin0_b", "en1_b", "conv_b", "ir", "iz", "in", "hr", "hz", "hn",
          "zero", "eps", "one", "two", "r", "z", "nr", "nz", "nn"]

NB_LOADED = BIASES.index("r")

SIGNALS = ("head xb ln_c ln_relu ln_sq ln_v ln_s ln_sd ln_r0 ln_a ln_b ln_y ln_r ln_t ln agg l0a l0b l0ra l0rb l0x l0y g c1a c1b c5r lin hn hs m gr gz ghn "
           "gin r z rh npre n u1 u2 mt hrm pr rd mf scan q_head q1 q1r qd q2 q3 q4 q5 q6 q7 "
           "b1 b1r bd bk bm b3 b3t b4 tab_end carry tab_sum tab_t tab_rm zz zt ztc rg rgm oh th "
           "of ot oc l0x_mm deg_sd deg_r ends_row ends_sd ends_r ends_bc ends_t ends_d scattered ehp eh wep weo").split()
SHARED = dict(
    b1="q1", b1r="q1r", bd="qd", bk="q2", bm="q3", b3="q4", b3t="q5", b4="q6",
    ends_row="q1", ends_sd="q1r", ends_r="qd", ends_bc="q2", ends_t="q3", ends_d="q4", deg_sd="q5", deg_r="q6",
    ehp="q1", eh="q1r", wep="q5", weo="q6",
    m="q_head", gin="qd", npre="q2", u1="q3", u2="q4",
    agg="q1", l0a="q2", l0b="qd", l0ra="q_head", l0rb="g", l0x="hs", l0x_mm="c1a", l0y="q3",
    c1b="q5", scattered="q1", zz="q5", zt="q6", ztc="q7", rg="q1", rgm="q1r", pr="q6", oh="c5r", th="lin",
    tab_sum="q1", tab_t="q1r", tab_rm="q7", tab_end="c1a", carry="lin")
LOADS = "ld_gs ld_gd ld_g4 ld_x ld_d ld_w ld_ea ld_tv ld_n".split()
STORES = "st_x st_tab st_tab4 st_we st_out st_d".split()
RING = 4


def shape_matrices():
    m = {"ident": np.eye(P), "center": np.eye(P) - np.kron(np.eye(T), np.full((D, D), 1.0 / D))}
    m["member_mean"] = np.zeros((P, P))
    m["member_mean"][:, 0:T] = np.kron(np.eye(T), np.full((D, 1), 1.0 / D))
    m["next_quarter"] = np.eye(P, k=D)
    m["prev_quarter"] = np.eye(P, k=-D)
    for t in range(T):
        s = np.zeros((P, P))
        s[t * D, :] = 1.0
        m[f"spread{t}"] = s
    return np.stack([m[k] for k in MATS], 1).astype(np.float32)


class Pass:

    def __init__(self, before, uses):
        self.base, self.uses = dict(before), {}
        for (kind, u), use in uses.items():
            self.use(before, kind, u, *use)

    def use(self, before, kind, u, per, blocks):
        key = (SHARED.get(kind, kind), u)
        assert key not in self.uses, (kind, u)
        self.base[key], self.uses[key] = before.get(key, 0), (per, blocks)
        before[key] = self.base[key] + per * blocks

    def n(self, kind, u, i, sub=0):
        key = (SHARED.get(kind, kind), u)
        return i * self.uses[key][0] + (self.base[key] + sub)

    def last(self, kind, u):
        key = (SHARED.get(kind, kind), u)
        per, blocks = self.uses[key]
        return self.base[key] + per * blocks - 1


def halves(n):
    return ((n + 1) // 2, n // 2)


LN = " ln_c ln_relu ln_sq ln_v ln_s ln_sd ln_r0 ln_a ln_b ln_y ln_r ln_t ln"
GRU = " gr gz ghn r z rh n u1 u2"
MSG = " mt hrm pr rd mf scan"
RG = " oh mt hrm zz zt ztc rg rgm rd mf scan"


def plan(EB, NP):
    before = {}
    out = {}

    def add(name, both="", s="", d="", times={}, blocks=(EB, EB), wide=False, gather=True, alternate=""):
        uses = {}
        for u, more in ((S_, s), (D_, d)):
            for k in (both + " " + more).split():
                uses[k, u] = (times.get(k, 1), blocks[u])
        for k in alternate.split():
            for par in (0, 1):
                uses[k, par] = (2, EB) if wide else (1, halves(EB)[par])
        out[name] = Pass(before, uses)

    K16 = {k: TILES for k in "pr rd zz zt ztc rg rgm".split()}
    Q4 = {k: T for k in "q_head q1 q1r qd q2 q3 q4 q5 q6 q7".split()}
    KW = {k: TILES // RING for k in ("ld_w",)}
    tab = "tab_sum tab_t tab_rm st_tab"

    def alternate_only(name, kinds, per=1):
        for k in kinds.split():
            for par in (0, 1):
                out[name].use(before, k, par, per, halves(EB)[par])

    def add_tab(name):
        add(name, s="tab_end carry", blocks=(1, 1))
        alternate_only(name, tab)

    def ring(p):
        for slot in range(RING):
            p.use(before, "ld_w", slot, TILES // RING, EB)

    add_tab("T_setup")
    before["st_tab", 0] = before["st_tab", 1] = 0
    alternate_only("T_setup", "deg_sd deg_r st_d")
    add("ENDS")
    alternate_only("ENDS", "ends_row ends_sd ends_r ends_bc ends_t ends_d st_d")
    add("P0", "head xb st_x" + LN, s="scan")
    add_tab("T0")
    add("P1", "head st_x ld_x agg l0a l0b l0ra l0rb l0x l0x_mm", s="l0y scan", alternate="ld_gs ld_gd")
    add_tab("T1")
    add("P2", "head xb st_x ld_x ld_d g" + LN, s="scan", alternate="ld_gs ld_gd")
    add_tab("T2")
    add("P3", "head ld_d c1a g", alternate="ld_gs ld_gd")
    n4 = tuple(T * h for h in halves(EB))
    add("T3", "ld_d b1 b1r bd bk bm b3 b3t b4 st_tab4", blocks=n4)
    add("P4", "ld_d g q_head q1 q1r qd q2 q3 q4 q5 q6 q7", s="scan", times=Q4, alternate="ld_gd", wide=True)
    add_tab("T4")
    add("WE", "ehp eh wep weo", s="ld_ea", times={"ehp": 2, "eh": 2, "wep": 2 * Q, "weo": 2 * Q})
    add("P5", "head ld_d ld_x c1a c1b c5r xb st_x lin hn hs" + LN, s=MSG, times=K16, alternate="ld_gs ld_gd")
    ring(out["P5"])
    add_tab("T5")
    for k in range(6, 5 + STEPS):
        add(f"P{k}", "head hs m gin npre" + GRU, s=MSG + " hn", times=K16, alternate="ld_gs ld_gd")
        ring(out[f"P{k}"])
        add_tab(f"T{k}")
    add("P11", "head ld_x xb hn st_x m gin npre" + GRU, s="ld_tv" + LN + RG, times=K16, alternate="ld_gs ld_gd")
    add_tab("T11")
    add("P12", s="head th ld_tv" + RG, times=K16, alternate="ld_gs")
    add_tab("T12")
    many = {k: 3 for k in LN.split()}
    many.update({k: STEPS for k in GRU.split()}, xb=3, hn=STEPS + 1)
    many.update({k: T for k in "q1 q1r q5 q6 q7".split()})
    add("N", "ld_n head l0a l0b l0ra l0rb l0x_mm c5r lin of ot oc st_out q1 q1r q5 q6 q7 xb hn" + LN + GRU,
        times=many, blocks=(NP, NP))
    add("P13", d="head ld_x of ot oc scattered", alternate="ld_gd")
    used = {key for q in out.values() for key in q.uses}
    return out, used




def gnn_kernel(nc, ins, out):
    GE = ins["edge_attr_T"].shape[1]
    EC = GE // T
    EB = EC // W
    NR = ins["x"].shape[0]
    NP = NR // (2 * W)
    NODES = NR * T
    SLOT_TILES = GE // P
    p_, used = plan(EB, NP)
    TAB = ["T_setup", "T0", "T1", "T2", "T4"] + [f"T{k}" for k in range(5, 13)]
    GRU_PASSES = [f"P{k}" for k in range(6, 5 + STEPS)]

    def dram(name, shape, dt=F32):
        return nc.dram_tensor(name, shape, dt, kind="Internal").ap()

    table = dram("table", (1 + EC, P))
    table4 = dram("table4", (1 + EC, T, P))
    last_of = dram("last_of", (NODES, 2))
    x_sp = dram("x_sp", (2, P, EC))
    d_sp = dram("d_sp", (2, P, EC))
    net = dram("net", (SLOT_TILES, P, D * D))
    prime = dram("prime", (16, P))

    with ExitStack() as ctx:
        def sb(name, shape, dt=F32):
            return ctx.enter_context(nc.sbuf_tensor(name, shape, dt))

        one = lambda name: ctx.enter_context(nc.semaphore(name))

        def sems(names, n=2):
            return {k: [ctx.enter_context(nc.semaphore(f"{k}{u}")) for u in range(n)] for k in names}

        sig = {k: [None, None] for k in SIGNALS}
        for k in SIGNALS:
            for u in (0, 1):
                if k not in SHARED and (k, u) in used:
                    sig[k][u] = one(f"{k}{u}")
        for k, other in SHARED.items():
            sig[k] = sig[other]
        dma = sems([k for k in LOADS + STORES if k not in ("ld_w", "st_we")])
        dma["ld_g0"] = sems(["ld_g0"], 4)["ld_g0"]
        dma.update(sems(["ld_w", "st_we"], RING))
        s_const, s_idx, s_bd, s_start, s_slot, s_settled = one("s_const"), one("s_idx"), one("s_blockdiag"), one("s_start"), one("s_slot"), one("s_settled")
        s_set, s_pset, s_aset = one("s_set_dve"), one("s_set_pe"), one("s_set_act")
        s_table, s_nodes, s_scat, s_own, s_end4 = one("s_table"), one("s_nodes"), one("s_scat"), one("s_own"), one("s_end4")
        s_tg = [one("s_tg0"), one("s_tg1")]
        s_sc = [one("s_sc0"), one("s_sc1")]

        keep = sb("keep", [P, EC], BF16)
        first = sb("first", [P, EC], BF16)
        scan = sb("scan", [P, EC + 1])
        h = [sb(f"h{u}", [P, EC]) for u in SPACES]
        G = [[sb(f"gathered{k}{u}", [P, W]) for u in SPACES] for k in (0, 1)]
        w = [[sb(f"w{k}{u}", [P, W]) for u in SPACES] for k in range(5)]
        xb = [sb(f"x_block{u}", [P, W]) for u in SPACES]
        db = [sb(f"d_block{u}", [P, W]) for u in SPACES]
        blocks4 = sb("blocks4", [P, T, W])
        hb = [blocks4[:, u, :] for u in SPACES]
        hn = [blocks4[:, 2 + u, :] for u in SPACES]
        attr_in = blocks4[0:D, :, :]
        h_rows, msg_rows = w[3][0], w[4][0]
        tab_in, tab_out = w[3], w[4]
        ring_all = sb("ring", [P, RING * D * D])
        ring = [ring_all[:, k * D * D:(k + 1) * D * D] for k in range(RING)]
        truth_in = ring_all[0:T, 0:T * W].rearrange("q (t e) -> q t e", t=T)
        mats = sb("mats", [P, len(MATS), P])
        wts = sb("wts", [P, len(WEIGHTS), P])
        bias = sb("bias", [P, len(BIASES)])
        spread_bf = sb("spread_bf", [P, T, P], BF16)
        en1 = sb("en1", [D, P])
        en2 = sb("en2", [P, D * D])
        rel_w = sb("rel_w", [P, 2, D * R])
        rel_b = sb("rel_b", [T, 2, D * R])
        tv = sb("tv", [P, SLOT_TILES, T])
        etype = sb("etype", [P, SLOT_TILES], I32)
        rel_id = sb("rel_id", [P, R])
        onehot = sb("onehot", [P, TILES, R])
        idx = {k: sb(f"idx_{k}", [P, SLOT_TILES], I32) for k in ("src", "dst", "run_end", "row")}
        slot_row = w[2][1][:, 0:SLOT_TILES]
        run_a, run_b = w[3][0][:, 0:SLOT_TILES], w[4][0][:, 0:SLOT_TILES]
        ends = sb("ends", [P, SLOT_TILES, 2])
        slot = [sb(f"idx_slot{k}", [P, TILES], I32) for k in (0, 1)]
        pair_slot = [sb(f"pair_slot{k}", [P, TILES, 2]) for k in (0, 1)]
        Z = [sb(f"z{k}", [P, P]) for k in (0, 1)]
        ZT = [sb(f"zt{k}", [P, P]) for k in (0, 1)]
        carry = sb("carry", [P, 1])
        first_end = sb("first_end", [P, 1])
        slot_d = [sb(f"idx_slot_d{k}", [P, TILES], I32) for k in (0, 1)]
        carry_mat = sb("carry_mat", [P, P])
        var, root, newton = ([sb(f"{name}{u}", [P, TILES]) for u in (0, 1)] for name in ("var", "root", "newton"))
        deg_small = [sb(f"deg_small{k}", [P, TILES]) for k in (0, 1)]
        ps = ctx.enter_context(nc.psum_tensor("ps", [P, 8, W], F32))
        pA, pB, pC, pD = ([ps[:, 4 * u + k, :] for u in SPACES] for k in range(4))
        member_mean = mats[:, len(MATS) - 1, 0:T]
        one_col = lambda name: bias[:, BIASES.index(name):BIASES.index(name) + 1]
        mat = {k: mats[:, i, :] for i, k in enumerate(MATS)}
        wt = {k: wts[:, i, :] for i, k in enumerate(WEIGHTS)}

        def settle(eng):
            eng.sem_inc(s_settled, 1)

        def ready(eng, kind, u, n):
            eng.wait_ge(sig[kind][u], n + 1 + CREDIT)
            if eng is nc.sync or eng is nc.gpsimd:
                settle(eng)

        def spent(eng, kind, u, n, depth=1):
            eng.wait_ge(sig[kind][u], n + 1 - depth + CREDIT)
            if eng is nc.sync or eng is nc.gpsimd:
                settle(eng)

        def landed(eng, kind, u, n):
            eng.wait_ge(dma[kind][u], 16 * (n + 1) if isinstance(n, int) else (n + 1) * 16)
            if eng is nc.sync or eng is nc.gpsimd:
                settle(eng)

        def stored(eng, kind, u, n):
            eng.wait_ge(dma[kind][u], 16 * (n + 1) if isinstance(n, int) else (n + 1) * 16)
            if eng is nc.sync or eng is nc.gpsimd:
                settle(eng)

        def sweep(eng, blocks, body):
            if blocks >= 2:
                with eng.Fori(0, blocks // 2) as j:
                    for par in (0, 1):
                        body(j * 2 + par, par, j)
            if blocks % 2:
                body(blocks - 1, 0, blocks // 2)

        def col(i):
            return bass.ts(i, W)

        def blk(t, i):
            return t[:, bass.ts(i, W)]

        end_of = {"P0": ("scan", "ln"), "P1": ("scan", "l0x"), "P2": ("scan", "g"), "P3": ("g", "g"), "P4": ("scan", "g"),
                  "P5": ("scan", "hs"), "P11": ("scan", "xb"), "P12": ("scan", None), "P13": (None, "oc")}
        end_of.update({k: ("scan", "hs") for k in GRU_PASSES})

        def pass_over(eng, name):
            for u in SPACES:
                if end_of[name][u]:
                    ready(eng, end_of[name][u], u, p_[name].last(end_of[name][u], u))

        block = ctx.enter_context(nc.Block())

        @block.sync
        def _(sp):
            for kind in SIGNALS:
                for u in (0, 1):
                    if kind not in SHARED and sig[kind][u]:
                        sp.sem_inc(sig[kind][u], CREDIT)
            at = 0
            for kind in STORES:
                for x in dma[kind]:
                    sp.dma_start(prime[at:at + 1, :], ins["mats"][at:at + 1, 0, :]).then_inc(x, 16)
                    at += 1
            for t in range(T):
                part = slice(t * D, t * D + D)
                sp.dma_start(h[0][part, :].bitcast(I32), ins["dst_fm"][t:t + 1, :].to_broadcast([D, EC])).then_inc(s_bd, 16)
                sp.dma_start(h[1][part, :].bitcast(I32), ins["dst_before_fm"][t:t + 1, :].to_broadcast([D, EC])).then_inc(s_bd, 16)
            for dst, name in ((mats, "mats"), (bias[:, 0:NB_LOADED], "biases"), (wts, "weights"), (en1, "en1"), (en2, "en2"),
                              (rel_w, "rel_w"), (rel_b, "rel_b"), (tv, "tv"), (etype, "etype"), (rel_id, "rel_id"),
                              (slot_row, "slot_row")):
                sp.dma_start(dst if dst is slot_row else dst[:], ins[name]).then_inc(s_const, 16)
            for k, name in (("src", "src"), ("dst", "dst"), ("row", "dst_after")):
                sp.dma_start(idx[k][:], ins[name]).then_inc(s_idx, 16)
            sp.wait_ge(s_set, 1)
            sp.dma_start(last_of.rearrange("(p n) two -> p (n two)", p=P), scan[:, 0:NODES * 2 // P]).then_inc(s_start, 16)
            sp.dma_start(table[0:1, :], scan[0:1, 0:P]).then_inc(s_start, 16)
            sp.dma_start(table4[0:1].rearrange("a t f -> a (t f)"), scan[0:1, 0:T * P]).then_inc(s_start, 16)

            def tables(name):
                q = p_[name]

                def body(i, par, j):
                    ready(sp, "tab_rm", par, q.n("tab_rm", par, j))
                    sp.dma_start(table[bass.ds(i * W + 1, W), :].rearrange("(q p) f -> p q f", p=P),
                                 tab_out[par][:].rearrange("p (q f) -> p q f", q=Q)).then_inc(dma["st_tab"][par], 16)
                sweep(sp, EB, body)
                for par in (0, 1):
                    stored(sp, "st_tab", par, q.last("st_tab", par) + 1)
                sp.sem_inc(s_table, 1)

            def d_rows(name, i, par, j):
                q = p_[name]
                spent(sp, "head", D_, q.n("head", D_, i), 2)
                sp.dma_start(G[par][D_][:].rearrange("p (q f) -> p q f", q=Q),
                             table[bass.ds(i * W + 1, W), :].rearrange("(q p) f -> p q f", p=P)
                             ).then_inc(dma["ld_gd"][par], 16)

            def pass_io(name, x_load=(), x_store=(), x_kind="xb", d_load=(), rows=True, tiles=False, tvs=False):
                q = p_[name]

                def body(i, par, j):
                    if rows:
                        d_rows(name, i, par, j)
                    for u in x_load:
                        spent(sp, end_of[name][u], u, q.n(end_of[name][u], u, i))
                        if u in x_store:
                            stored(sp, "st_x", u, q.n("st_x", u, i))
                        sp.dma_start(xb[u][:], x_sp[u, :, col(i)]).then_inc(dma["ld_x"][u], 16)
                    for u in d_load:
                        spent(sp, end_of[name][u], u, q.n(end_of[name][u], u, i))
                        sp.dma_start(db[u][:], d_sp[u, :, col(i)]).then_inc(dma["ld_d"][u], 16)
                    if tvs:
                        spent(sp, "mf", S_, q.n("mf", S_, i))
                        sp.dma_start(truth_in, ins["tv_T"][:, :, col(i)]).then_inc(dma["ld_tv"][S_], 16)
                    for u in x_store:
                        ready(sp, x_kind, u, q.n(x_kind, u, i))
                        sp.dma_start(x_sp[u, :, col(i)], xb[u][:]).then_inc(dma["st_x"][u], 16)
                    if tiles:
                        for k in range(TILES):
                            spent(sp, "rd", S_, q.n("rd", S_, i, k), RING)
                            sp.dma_start(ring[k % RING][:], net[bass.ds(i * TILES + k, 1), :, :].rearrange("a p f -> p (a f)")
                                         ).then_inc(dma["ld_w"][k % RING], 16)
                sweep(sp, EB, body)
                for u in x_store:
                    stored(sp, "st_x", u, q.last("st_x", u) + 1)

            q = p_["T_setup"]

            def body(i, par, j):
                ready(sp, "deg_r", par, q.n("deg_r", par, j))
                sp.dma_start(d_sp[D_, :, col(i)], w[1][par][:]).then_inc(dma["st_d"][par], 16)
            sweep(sp, EB, body)
            q2 = p_["ENDS"]

            def body(i, par, j):
                ready(sp, "ends_d", par, q2.n("ends_d", par, j))
                sp.dma_start(d_sp[S_, :, col(i)], w[1][par][:]).then_inc(dma["st_d"][par], 16)
            sweep(sp, EB, body)
            for par in (0, 1):
                stored(sp, "st_d", par, q2.last("st_d", par) + 1)

            pass_io("P0", x_store=SPACES, rows=False)
            tables("T0")
            pass_io("P1", x_load=SPACES, x_store=SPACES, x_kind="l0x")
            tables("T1")
            pass_io("P2", x_load=SPACES, x_store=SPACES, d_load=SPACES)
            tables("T2")
            pass_io("P3", d_load=SPACES)

            pass_over(sp, "P3")
            q = p_["T3"]
            for t in range(T):
                def body(i, par, j, t=t):
                    spent(sp, "bd", par, q.n("bd", par, j, t * halves(EB)[par]))
                    sp.dma_start(db[par][:], d_sp[S_, :, col(i)]).then_inc(dma["ld_d"][par], 16)
                    ready(sp, "b4", par, q.n("b4", par, j, t * halves(EB)[par]))
                    sp.dma_start(table4[bass.ds(i * W + 1, W), t, :].rearrange("(q p) f -> p q f", p=P),
                                 w[4][par][:].rearrange("p (q f) -> p q f", q=Q)).then_inc(dma["st_tab4"][par], 16)
                sweep(sp, EB, body)
            for par in (0, 1):
                stored(sp, "st_tab4", par, q.last("st_tab4", par) + 1)
            sp.sem_inc(s_table, 1)

            q = p_["P4"]

            def body(i, par, j):
                for u in SPACES:
                    spent(sp, "g", u, q.n("g", u, i))
                    sp.dma_start(db[u][:], d_sp[u, :, col(i)]).then_inc(dma["ld_d"][u], 16)
                for t in range(T):
                    spent(sp, "q_head", D_, q.n("q_head", D_, i, t), 2)
                    sp.dma_start(G[t % 2][D_][:].rearrange("p (q f) -> p q f", q=Q),
                                 table4[bass.ds(i * W + 1, W), t, :].rearrange("(q p) f -> p q f", p=P)
                                 ).then_inc(dma["ld_gd"][t % 2], 16)
            sweep(sp, EB, body)
            tables("T4")

            pass_over(sp, "P4")
            q = p_["WE"]

            def body(i, par, j):
                spent(sp, "ehp", 0, q.n("ehp", 0, i, 0))
                spent(sp, "ehp", 1, q.n("ehp", 1, i, 0))
                sp.dma_start(attr_in, ins["edge_attr_T"].rearrange("d (t e) -> d t e", t=T)[:, :, col(i)]
                             ).then_inc(dma["ld_ea"][0], 16)
                for t in range(T):
                    for k in range(Q):
                        ready(sp, "weo", t % 2, q.n("weo", t % 2, i, (t // 2) * Q + k))
                        slot_ = 2 * (t % 2) + k % 2
                        sp.dma_start(net[bass.ds(i * TILES + (k * T + t), 1), :, :].rearrange("a p f -> p (a f)"),
                                     ring[slot_]).then_inc(dma["st_we"][slot_], 16)
            sweep(sp, EB, body)
            for k in range(RING):
                stored(sp, "st_we", k, EB * TILES // RING)

            pass_io("P5", x_load=SPACES, x_store=SPACES, d_load=SPACES, tiles=True)
            tables("T5")
            for k, name in enumerate(GRU_PASSES):
                pass_io(name, tiles=True)
                tables(f"T{6 + k}")
            pass_io("P11", x_load=SPACES, x_store=SPACES, tvs=True)
            tables("T11")
            pass_io("P12", rows=False, tvs=True)
            tables("T12")

            q = p_["N"]
            pass_over(sp, "P12")
            with sp.Fori(0, NP) as i:
                for u in (0, 1):
                    spent(sp, "head", u, q.n("head", u, i))
                    sp.dma_start(G[0][u][:].rearrange("p (q f) -> p q f", q=Q),
                                 ins["x"][bass.ds(i * (2 * W) + u * W, W), :].rearrange("(p q) f -> p q f", q=Q)
                                 ).then_inc(dma["ld_n"][u], 16)
                for u in (0, 1):
                    ready(sp, "oc", u, q.n("oc", u, i))
                    sp.dma_start(out[bass.ds(i * (2 * W) + u * W, W), :].rearrange("(p q) f -> p q f", q=Q),
                                 db[u][:].rearrange("p (q f) -> p q f", q=Q)).then_inc(dma["st_out"][u], 16)
            for u in (0, 1):
                stored(sp, "st_out", u, NP)
            sp.sem_inc(s_nodes, 1)

            pass_io("P13", x_load=(D_,))

        @block.gpsimd
        def _(pool):
            slots = [0]

            def fetch(i, index, dst, rows, dests, done, base, per, sub):
                nc.gpsimd.tensor_copy(dst[:], index[:, bass.ds(i * TILES, TILES)]).then_inc(s_slot, 1)
                pool.wait_ge(s_slot, i * per + (base + sub + 1))
                settle(pool)
                for k in range(TILES):
                    pool.indirect_dma_start(dests(k), None, rows, bass.IndirectOffsetOnAxis(ap=dst[:, k:k + 1], axis=0)
                                            ).then_inc(done, 16)

            q = p_["T_setup"]
            pool.wait_ge(s_set, 18)
            pool.wait_ge(s_start, 48)

            def body(i, par, j):
                ready(pool, "tab_rm", par, q.n("tab_rm", par, j))
                nc.gpsimd.tensor_copy(slot[par][:], idx["run_end"][:, bass.ds(i * TILES, TILES)]).then_inc(s_slot, 1)
                nc.gpsimd.tensor_copy(pair_slot[par][:], ends[:, bass.ds(i * TILES, TILES), :]).then_inc(s_slot, 1)
                pool.wait_ge(s_slot, i * 2 + 2)
                settle(pool)
                for k in range(TILES):
                    pool.indirect_dma_start(last_of, bass.IndirectOffsetOnAxis(ap=slot[par][:, k:k + 1], axis=0),
                                            pair_slot[par][:, k, :], None, bounds_check=NODES - 1, oob_is_err=False
                                            ).then_inc(s_sc[par], 16)
                pool.wait_ge(s_sc[par], (j + 1) * (16 * TILES))
                settle(pool)
            sweep(pool, EB, body)
            slots[0] = 2 * EB
            q2 = p_["ENDS"]

            def body(i, par, j):
                spent(pool, "ends_row", par, q2.n("ends_row", par, j))
                spent(pool, "ends_sd", par, q2.n("ends_sd", par, j))
                fetch(i, idx["src"], slot[par], last_of, lambda k: pair_slot[par][:, k, :], s_tg[par], slots[0], 1, 0)
            sweep(pool, EB, body)
            slots[0] += EB

            for par in (0, 1):
                pool.wait_ge(s_tg[par], halves(EB)[par] * (16 * TILES))
            q3 = p_["P0"]
            x_rows = ins["x"].rearrange("r (t f) -> (r t) f", t=T)

            def body(i, par, j):
                for u, name in ((S_, "src"), (D_, "dst")):
                    spent(pool, "head", u, q3.n("head", u, i), 2)
                    fetch(i, idx[name], (slot if u == S_ else slot_d)[par], x_rows,
                          lambda k: G[par][u][:, k * D:k * D + D], dma["ld_g0"][2 * u + par], slots[0], 2, u)
            sweep(pool, EB, body)
            slots[0] += 2 * EB

            def gather(name, tables_before):
                q = p_[name]
                pool.wait_ge(s_table, tables_before)

                def body(i, par, j):
                    spent(pool, "head", S_, q.n("head", S_, i), 2)
                    fetch(i, idx["row"], slot[par], table.rearrange("r (t f) -> (r t) f", t=T),
                          lambda k: G[par][S_][:, k * D:k * D + D], dma["ld_gs"][par], slots[0], 1, 0)
                sweep(pool, EB, body)
                slots[0] += EB

            for k in (1, 2, 3):
                gather(f"P{k}", k)
            q4 = p_["P4"]
            pool.wait_ge(s_table, 4)

            def body(i, par, j):
                spent(pool, "q_head", S_, q4.n("q_head", S_, i), 2)
                nc.gpsimd.tensor_copy(slot[par][:], idx["row"][:, bass.ds(i * TILES, TILES)]).then_inc(s_slot, 1)
                pool.wait_ge(s_slot, i + (slots[0] + 1))
                settle(pool)
                for t in range(T):
                    spent(pool, "q_head", S_, q4.n("q_head", S_, i, t), 2)
                    for k in range(Q):
                        pool.indirect_dma_start(
                            G[t % 2][S_][:, k * P:k * P + P], None, table4.rearrange("r t f -> (r t) f"),
                            bass.IndirectOffsetOnAxis(ap=slot[par][:, k * T + t:k * T + t + 1], axis=0)
                        ).then_inc(dma["ld_g4"][t % 2], 16)
            sweep(pool, EB, body)
            slots[0] += EB
            for k in range(5, 13):
                gather(f"P{k}", k)

            q5 = p_["P13"]
            pool.wait_ge(s_nodes, 1)

            def body(i, par, j):
                nc.gpsimd.tensor_copy(slot[par][:], idx["run_end"][:, bass.ds(i * TILES, TILES)]).then_inc(s_slot, 1)
                pool.wait_ge(s_slot, i + (slots[0] + 1))
                settle(pool)
                ready(pool, "oc", D_, q5.n("oc", D_, i))
                for k in range(TILES):
                    pool.indirect_dma_start(out.rearrange("r (t f) -> (r t) f", t=T),
                                            bass.IndirectOffsetOnAxis(ap=slot[par][:, k:k + 1], axis=0),
                                            db[D_][:, k * D:k * D + D], None, bounds_check=NODES - 1, oob_is_err=False
                                            ).then_inc(s_scat, 16)
                pool.wait_ge(s_scat, (i + 1) * (16 * TILES))
                settle(pool)
                pool.sem_inc(sig["scattered"][D_], 1)
            sweep(pool, EB, body)

        @block.tensor
        def _(pe):
            mm = nc.tensor.matmul

            def turn(dst, src):
                for k in range(Q):
                    last = nc.tensor.transpose(dst[:, k * P:k * P + P], src[:, k * P:k * P + P], mat["ident"])
                return last

            def layer_norm(q, u, i, x, sub=0, x_sub=0, x_kind="xb"):
                ready(pe, x_kind, u, q.n(x_kind, u, i, x_sub))
                mm(pB[u], mat["center"], x, start=True, stop=True).then_inc(sig["ln_c"][u], 1)
                ready(pe, "ln_sq", u, q.n("ln_sq", u, i, sub))
                for k in range(Q):
                    last = mm(pC[u][:, k * T:k * T + T], w[0][u][:, k * P:k * P + P], member_mean, start=True, stop=True)
                last.then_inc(sig["ln_v"][u], 1)
                ready(pe, "ln_r", u, q.n("ln_r", u, i, sub))
                turn(pD[u], w[2][u]).then_inc(sig["ln_t"][u], 1)

            def head(q, u, i, par, j, load, ends):
                landed_n(pe, load, par, q, i, j)
                spent(pe, ends, u, q.n(ends, u, i))
                turn(pA[u], G[par][u]).then_inc(sig["head"][u], 1)

            def landed_n(eng, load, par, q, i, j):
                if load == "ld_gs":
                    eng.wait_ge(dma[load][par], (q.n(load, par, j) + 1) * (16 * TILES))
                else:
                    landed(eng, load, par, q.n(load, par, j))

            def gru(q, u, i, state):
                mm(pD[u], wt["hn"], state, start=True, stop=True).then_inc(sig["ghn"][u], 1)
                mm(pB[u], wt["hr"], state, start=True, stop=False)
                ready(pe, "m", u, q.n("m", u, i))
                mm(pB[u], wt["ir"], w[0][u][:], start=False, stop=True).then_inc(sig["gr"][u], 1)
                mm(pC[u], wt["hz"], state, start=True, stop=False)
                mm(pC[u], wt["iz"], w[0][u][:], start=False, stop=True).then_inc(sig["gz"][u], 1)
                mm(pA[u], wt["in"], w[0][u][:], start=True, stop=True).then_inc(sig["gin"][u], 1)

            def gru_alone(q, u, i, sub):
                ready(pe, "hn", u, q.n("hn", u, i, sub))
                mm(pB[u], wt["hr"], hn[u], start=True, stop=True).then_inc(sig["gr"][u], 1)
                mm(pC[u], wt["hz"], hn[u], start=True, stop=True).then_inc(sig["gz"][u], 1)
                mm(pD[u], wt["hn"], hn[u], start=True, stop=True).then_inc(sig["ghn"][u], 1)

            def to_rows(q, i, kind, src):
                ready(pe, kind, S_, q.n(kind, S_, i))
                turn(pB[S_], src).then_inc(sig["mt"][S_], 1)

            def edge_messages(q, i):
                to_rows(q, i, "hn", hn[S_])
                mm(pC[S_], wt["en2b"], hn[S_], start=True, stop=False)
                ready(pe, "rd", S_, q.n("rd", S_, i, TILES - 1))
                for k in range(Q):
                    last = mm(pC[S_][:, k * P:k * P + P], msg_rows[:, k * P:k * P + P], mat["ident"],
                              start=False, stop=(k == Q - 1))
                last.then_inc(sig["mf"][S_], 1)

            def relation_messages(q, i, kind, layer):
                to_rows(q, i, kind, hb[S_])
                landed(pe, "ld_tv", S_, q.n("ld_tv", S_, i))
                for k in range(TILES + 1):
                    if k < TILES:
                        ready(pe, "zz", S_, q.n("zz", S_, i, k))
                        spent(pe, "ztc", S_, q.n("ztc", S_, i, k), 2)
                        nc.tensor.transpose((pC, pB)[k % 2][S_][:, 0:P], Z[k % 2][:], mat["ident"]
                                            ).then_inc(sig["zt"][S_], 1)
                    if k:
                        m, dst = k - 1, (pD, pA)[(k - 1) % 2][S_][:, 0:D * R]
                        ready(pe, "ztc", S_, q.n("ztc", S_, i, m))
                        spent(pe, "rgm", S_, q.n("rgm", S_, i, m), 2)
                        mm(dst, ZT[m % 2][:], rel_w[:, layer, :], start=True, stop=False)
                        at = (m // T) * P
                        mm(dst, truth_in[:, m % T, at:at + P], rel_b[:, layer, :],
                           start=False, stop=True).then_inc(sig["rg"][S_], 1)
                ready(pe, "rd", S_, q.n("rd", S_, i, TILES - 1))
                turn(pA[S_], msg_rows).then_inc(sig["mf"][S_], 1)

            def tables(name, after):
                q = p_[name]
                if after:
                    pass_over(pe, after)
                mm(pA[0][:, 0:1], carry_mat[:], scan[:, EC:EC + 1], start=True, stop=True).then_inc(sig["tab_end"][0], 1)

                def body(i, par, j):
                    ready(pe, "tab_sum", par, q.n("tab_sum", par, j))
                    spent(pe, "tab_rm", par, q.n("tab_rm", par, j))
                    turn(pD[par], tab_in[par]).then_inc(sig["tab_t"][par], 1)
                sweep(pe, EB, body)

            pe.wait_ge(s_const, 16 * 11)
            pe.wait_ge(s_set, 5)
            mm(pA[0][:, 0:P], mat["prev_quarter"], w[0][0][:, 0:P], start=True, stop=True).then_inc(s_pset, 1)
            pe.wait_ge(s_set, 6)
            mm(pB[0][:, 0:P], mat["prev_quarter"], w[1][0][:, 0:P], start=True, stop=True).then_inc(s_pset, 1)
            pe.wait_ge(s_set, 10)
            for k, name in enumerate(("ir", "iz", "in")):
                mm(pC[0][:, k:k + 1], wt[name], w[2][0][:, 0:1], start=True, stop=True).then_inc(s_pset, 1)
            pe.wait_ge(s_set, 18)
            tables("T_setup", None)
            q = p_["ENDS"]

            def body(i, par, j):
                ready(pe, "ends_bc", par, q.n("ends_bc", par, j))
                spent(pe, "ends_d", par, q.n("ends_d", par, j))
                turn(pA[par], w[0][par]).then_inc(sig["ends_t"][par], 1)
            sweep(pe, EB, body)

            for par in (0, 1):
                ready(pe, "ends_d", par, q.last("ends_d", par))
            q = p_["P0"]

            def body(i, par, j, q=q):
                for u in SPACES:
                    pe.wait_ge(dma["ld_g0"][2 * u + par], (j + 1) * (16 * TILES))
                    spent(pe, end_of["P0"][u], u, q.n(end_of["P0"][u], u, i))
                    turn(pA[u], G[par][u]).then_inc(sig["head"][u], 1)
                for u in SPACES:
                    layer_norm(q, u, i, xb[u][:])
            sweep(pe, EB, body)
            tables("T0", "P0")

            q = p_["P1"]

            def sage(q, u, i, state, agg, messages):
                for k, (dst, kind) in enumerate(((pB, "l0a"), (pC, "l0b"))):
                    if agg:
                        mm(dst[u], wt[f"l0_l{k}"], w[0][u][:], start=True, stop=False)
                    mm(dst[u], wt[f"l0_r{k}"], state, start=not agg, stop=True).then_inc(sig[kind][u], 1)
                ready(pe, "l0ra", u, q.n("l0ra", u, i))
                ready(pe, "l0rb", u, q.n("l0rb", u, i))
                if messages:
                    mm(pA[u], wt["l0_ol0"], w[1][u][:], start=True, stop=False)
                    mm(pA[u], wt["l0_ol1"], w[2][u][:], start=False, stop=True).then_inc(sig["l0y"][u], 1)
                mm(pD[u], wt["l0_or0"], w[1][u][:], start=True, stop=False)
                mm(pD[u], wt["l0_or1"], w[2][u][:], start=False, stop=True).then_inc(sig["l0x_mm"][u], 1)

            def body(i, par, j, q=q):
                for u in SPACES:
                    head(q, u, i, par, j, ("ld_gs", "ld_gd")[u], end_of["P1"][u])
                for u in SPACES:
                    ready(pe, "agg", u, q.n("agg", u, i))
                    sage(q, u, i, blk(h[u], i), True, u == S_)
            sweep(pe, EB, body)
            tables("T1", "P1")

            q = p_["P2"]

            def body(i, par, j, q=q):
                for u in SPACES:
                    head(q, u, i, par, j, ("ld_gs", "ld_gd")[u], end_of["P2"][u])
                for u in SPACES:
                    layer_norm(q, u, i, xb[u][:])
            sweep(pe, EB, body)
            tables("T2", "P2")

            q = p_["P3"]

            def body(i, par, j, q=q):
                for u in SPACES:
                    head(q, u, i, par, j, ("ld_gs", "ld_gd")[u], end_of["P3"][u])
            sweep(pe, EB, body)
            pass_over(pe, "P3")

            q = p_["T3"]
            for t in range(T):
                def body(i, par, j, t=t, q=q):
                    spent(pe, "b4", par, q.n("b4", par, j, t * halves(EB)[par]))
                    mm(pA[par], wt[f"w1_{t}"], blk(h[S_], i), start=True, stop=True).then_inc(sig["b1"][par], 1)
                    landed(pe, "ld_d", par, q.n("ld_d", par, j, t * halves(EB)[par]))
                    mm(pB[par], mat[f"spread{t}"], db[par][:], start=True, stop=True
                       ).then_inc(sig["bd"][par], 1)
                    mm(pC[par], spread_bf[:, t, :], blk(keep, i), start=True, stop=True
                       ).then_inc(sig["bk"][par], 1)
                    ready(pe, "b3", par, q.n("b3", par, j, t * halves(EB)[par]))
                    turn(pD[par], w[3][par]).then_inc(sig["b3t"][par], 1)
                sweep(pe, EB, body)
            for par in (0, 1):
                ready(pe, "b4", par, q.last("b4", par))

            q = p_["P4"]

            def body(i, par, j, q=q):
                for t in range(T):
                    for u in SPACES:
                        if u == S_:
                            pe.wait_ge(dma["ld_g4"][t % 2], (i * 2 + (t // 2 + 1)) * (16 * Q))
                        else:
                            landed(pe, "ld_gd", t % 2, q.n("ld_gd", t % 2, i, t // 2))
                        spent(pe, "q3", u, q.n("q3", u, i, t))
                        turn(pA[u], G[t % 2][u]).then_inc(sig["q_head"][u], 1)
                        spent(pe, "q6", u, q.n("q6", u, i, t))
                        mm(pB[u], wt[f"w1_{t}"], blk(h[u], i), start=True, stop=True).then_inc(sig["q1"][u], 1)
                        spent(pe, "q4", u, q.n("q4", u, i, t))
                        landed(pe, "ld_d", u, q.n("ld_d", u, i))
                        mm(pC[u], mat[f"spread{t}"], db[u][:], start=True, stop=True).then_inc(sig["qd"][u], 1)
                    for u in SPACES:
                        ready(pe, "q4", u, q.n("q4", u, i, t))
                        mm(pB[u], wt["w2"], w[2][u][:], start=True, stop=True).then_inc(sig["q5"][u], 1)
                    for u in SPACES:
                        ready(pe, "q6", u, q.n("q6", u, i, t))
                        if t == 0:
                            spent(pe, "g", u, q.n("g", u, i))
                        mm(pD[u], wt[f"w3_{t}"], w[3][u][:], start=(t == 0), stop=(t == T - 1)
                           ).then_inc(sig["q7"][u], 1)
            sweep(pe, EB, body)
            tables("T4", "P4")

            q = p_["WE"]
            for par in (0, 1):
                ready(pe, "tab_rm", par, p_["T4"].last("tab_rm", par))

            def body(i, par, j, q=q):
                landed(pe, "ld_ea", 0, q.n("ld_ea", 0, i))
                for t in range(T):
                    u = t % 2
                    spent(pe, "eh", u, q.n("eh", u, i, t // 2))
                    mm(pA[u], en1[:], attr_in[:, t, :], start=True, stop=True).then_inc(sig["ehp"][u], 1)
                    ready(pe, "eh", u, q.n("eh", u, i, t // 2))
                    for k in range(Q):
                        spent(pe, "weo", u, q.n("weo", u, i, (t // 2) * Q + k))
                        lhs = w[0][u][:, k * P:k * P + P]
                        mm(pB[u], lhs, en2[:, 0:W], start=True, stop=True)
                        mm(pC[u], lhs, en2[:, W:2 * W], start=True, stop=True).then_inc(sig["wep"][u], 1)
            sweep(pe, EB, body)
            for u in (0, 1):
                ready(pe, "weo", u, q.last("weo", u))

            q = p_["P5"]

            def body(i, par, j, q=q):
                for u in SPACES:
                    head(q, u, i, par, j, ("ld_gs", "ld_gd")[u], end_of["P5"][u])
                for u in SPACES:
                    layer_norm(q, u, i, xb[u][:])
                for u in SPACES:
                    ready(pe, "ln", u, q.n("ln", u, i))
                    mm(pD[u], wt["lin0"], hb[u], start=True, stop=True).then_inc(sig["lin"][u], 1)
                edge_messages(q, i)
            sweep(pe, EB, body)
            tables("T5", "P5")

            for k, name in enumerate(GRU_PASSES):
                q = p_[name]

                def body(i, par, j, q=q):
                    for u in SPACES:
                        head(q, u, i, par, j, ("ld_gs", "ld_gd")[u], "hs")
                        if u == S_:
                            spent(pe, "scan", u, q.n("scan", u, i))
                        gru(q, u, i, blk(h[u], i))
                    edge_messages(q, i)
                sweep(pe, EB, body)
                tables(f"T{6 + k}", name)

            q = p_["P11"]

            def body(i, par, j, q=q):
                for u in SPACES:
                    head(q, u, i, par, j, ("ld_gs", "ld_gd")[u], end_of["P11"][u])
                    gru(q, u, i, blk(h[u], i))
                layer_norm(q, S_, i, xb[S_][:])
                relation_messages(q, i, "ln", 0)
            sweep(pe, EB, body)
            tables("T11", "P11")
            q = p_["P12"]

            def body(i, par, j, q=q):
                head(q, S_, i, par, j, "ld_gs", "scan")
                relation_messages(q, i, "th", 1)
            sweep(pe, EB, body)
            tables("T12", "P12")

            q = p_["N"]
            for par in (0, 1):
                ready(pe, "tab_rm", par, p_["T12"].last("tab_rm", par))
            with pe.Fori(0, NP) as i:
                for u in (0, 1):
                    landed(pe, "ld_n", u, q.n("ld_n", u, i))
                    spent(pe, "oc", u, q.n("oc", u, i))
                    turn(pA[u], G[0][u]).then_inc(sig["head"][u], 1)
                for u in (0, 1):
                    layer_norm(q, u, i, xb[u][:], 0, 0)
                for u in (0, 1):
                    ready(pe, "ln", u, q.n("ln", u, i, 0))
                    sage(q, u, i, hb[u], False, False)
                for u in (0, 1):
                    layer_norm(q, u, i, xb[u][:], 1, 1)
                for u in (0, 1):
                    ready(pe, "ln", u, q.n("ln", u, i, 1))
                for t in range(T):
                    for u in (0, 1):
                        mm(pA[u], wt[f"w1_{t}"], hb[u], start=True, stop=True).then_inc(sig["q1"][u], 1)
                    for u in (0, 1):
                        ready(pe, "q1r", u, q.n("q1r", u, i, t))
                        mm(pB[u], wt["w2"], w[1][u][:], start=True, stop=True).then_inc(sig["q5"][u], 1)
                    for u in (0, 1):
                        ready(pe, "q6", u, q.n("q6", u, i, t))
                        mm(pD[u], wt[f"w3_{t}"], w[2][u][:], start=(t == 0), stop=(t == T - 1)
                           ).then_inc(sig["q7"][u], 1)
                for u in (0, 1):
                    layer_norm(q, u, i, xb[u][:], 2, 2)
                for u in (0, 1):
                    ready(pe, "ln", u, q.n("ln", u, i, 2))
                    mm(pD[u], wt["lin0"], hb[u], start=True, stop=True).then_inc(sig["lin"][u], 1)
                for k in range(STEPS):
                    for u in (0, 1):
                        gru_alone(q, u, i, k)
                for u in (0, 1):
                    ready(pe, "of", u, q.n("of", u, i))
                    turn(pA[u], w[0][u]).then_inc(sig["ot"][u], 1)

            q = p_["P13"]

            def body(i, par, j, q=q):
                head(q, D_, i, par, j, "ld_gd", "oc")
                ready(pe, "of", D_, q.n("of", D_, i))
                turn(pB[D_], w[0][D_]).then_inc(sig["ot"][D_], 1)
            sweep(pe, EB, body)

        @block.scalar
        def _(act):
            f = nc.scalar.activation

            def layer_norm(q, u, i, sub=0):
                ready(act, "ln_c", u, q.n("ln_c", u, i, sub))
                f(w[0][u][:], pB[u], ACT.Square).then_inc(sig["ln_sq"][u], 1)
                f(w[1][u][:], pB[u], ACT.Relu).then_inc(sig["ln_relu"][u], 1)
                ready(act, "ln_s", u, q.n("ln_s", u, i, sub))
                f(root[u][:], var[u][:], ACT.Sqrt).then_inc(sig["ln_sd"][u], 1)

            def tables(name):
                q = p_[name]

                def body(i, par, j):
                    ready(act, "tab_t", par, q.n("tab_t", par, j))
                    stored(act, "st_tab", par, q.n("st_tab", par, j))
                    f(tab_out[par][:], pD[par], ACT.Copy).then_inc(sig["tab_rm"][par], 1)
                sweep(act, EB, body)

            def sage(q, u, i):
                for k, (src, dst, kind, out_kind) in enumerate(((pB, w[1], "l0a", "l0ra"), (pC, w[2], "l0b", "l0rb"))):
                    ready(act, kind, u, q.n(kind, u, i))
                    f(dst[u][:], src[u], ACT.Relu, bias=one_col("b_in")).then_inc(sig[out_kind][u], 1)

            def gru(q, u, i):
                ready(act, "gr", u, q.n("gr", u, i))
                f(w[1][u][:], pB[u], ACT.Sigmoid, bias=one_col("r")).then_inc(sig["r"][u], 1)
                ready(act, "gz", u, q.n("gz", u, i))
                f(w[2][u][:], pC[u], ACT.Sigmoid, bias=one_col("z")).then_inc(sig["z"][u], 1)

            def gru_new(q, u, i):
                ready(act, "npre", u, q.n("npre", u, i))
                f(w[1][u][:], w[4][u][:], ACT.Tanh, bias=one_col("in")).then_inc(sig["n"][u], 1)

            def rows(q, i):
                ready(act, "mt", S_, q.n("mt", S_, i))
                f(h_rows[:], pB[S_], ACT.Copy).then_inc(sig["hrm"][S_], 1)

            def relation(q, i):
                rows(q, i)
                for k in range(TILES):
                    ready(act, "zt", S_, q.n("zt", S_, i, k))
                    spent(act, "rg", S_, q.n("rg", S_, i, k), 2)
                    f(ZT[k % 2][:], (pC, pB)[k % 2][S_][:, 0:P], ACT.Copy).then_inc(sig["ztc"][S_], 1)

            act.wait_ge(s_const, 16 * 11)
            q = p_["T_setup"]

            def body(i, par, j, q=q):
                ready(act, "tab_sum", par, q.n("tab_sum", par, j))
                spent(act, "deg_r", par, q.n("deg_r", par, j))
                f(w[0][par][:], tab_in[par][:], ACT.Sqrt, bias=one_col("two")).then_inc(sig["deg_sd"][par], 1)
                ready(act, "tab_t", par, q.n("tab_t", par, j))
                f(ends[:, bass.ds(i * TILES, TILES), 1:2],
                  pD[par].rearrange("p (k f) -> p k f", f=D)[:, :, 0:1], ACT.Identity, bias=one_col("one")
                  ).then_inc(sig["tab_rm"][par], 1)
            sweep(act, EB, body)
            q = p_["ENDS"]

            def body(i, par, j, q=q):
                act.wait_ge(s_tg[par], (j + 1) * (16 * TILES))
                spent(act, "ends_bc", par, q.n("ends_bc", par, j))
                f(deg_small[par][:].rearrange("p (k a) -> p k a", a=1), pair_slot[par][:, :, 1:2], ACT.Sqrt, bias=one_col("one")
                  ).then_inc(sig["ends_sd"][par], 1)
                ready(act, "ends_t", par, q.n("ends_t", par, j))
                stored(act, "st_d", par, q.n("st_d", par, j))
                f(w[1][par][:], pA[par], ACT.Copy).then_inc(sig["ends_d"][par], 1)
            sweep(act, EB, body)

            q = p_["P0"]
            for par in (0, 1):
                stored(act, "st_d", par, p_["ENDS"].last("st_d", par) + 1)

            def body(i, par, j, q=q):
                for u in SPACES:
                    ready(act, "head", u, q.n("head", u, i))
                    stored(act, "st_x", u, q.n("st_x", u, i))
                    f(xb[u][:], pA[u], ACT.Copy).then_inc(sig["xb"][u], 1)
                for u in SPACES:
                    layer_norm(q, u, i)
            sweep(act, EB, body)
            tables("T0")

            q = p_["P1"]

            def body(i, par, j, q=q):
                for u in SPACES:
                    ready(act, "head", u, q.n("head", u, i))
                    f(w[0][u][:], pA[u], ACT.Copy).then_inc(sig["agg"][u], 1)
                for u in SPACES:
                    sage(q, u, i)
            sweep(act, EB, body)
            tables("T1")

            q = p_["P2"]

            def body(i, par, j, q=q):
                for u in SPACES:
                    layer_norm(q, u, i)
            sweep(act, EB, body)
            tables("T2")

            q = p_["T3"]
            for t in range(T):
                def body(i, par, j, t=t, q=q):
                    off = t * halves(EB)[par]
                    ready(act, "b1", par, q.n("b1", par, j, off))
                    f(w[1][par][:], pA[par], ACT.Relu, bias=one_col("b1")).then_inc(sig["b1r"][par], 1)
                    ready(act, "b3t", par, q.n("b3t", par, j, off))
                    stored(act, "st_tab4", par, q.n("st_tab4", par, j, off))
                    f(w[4][par][:], pD[par], ACT.Copy).then_inc(sig["b4"][par], 1)
                sweep(act, EB, body)

            q = p_["P4"]

            def body(i, par, j, q=q):
                for t in range(T):
                    for u in SPACES:
                        ready(act, "q1", u, q.n("q1", u, i, t))
                        f(w[1][u][:], pB[u], ACT.Relu, bias=one_col("b1")).then_inc(sig["q1r"][u], 1)
                    for u in SPACES:
                        ready(act, "q5", u, q.n("q5", u, i, t))
                        spent(act, "q7", u, q.n("q7", u, i, t))
                        f(w[3][u][:], pB[u], ACT.Relu, bias=one_col("b2")).then_inc(sig["q6"][u], 1)
            sweep(act, EB, body)
            tables("T4")

            q = p_["WE"]

            def body(i, par, j, q=q):
                for t in range(T):
                    u = t % 2
                    ready(act, "ehp", u, q.n("ehp", u, i, t // 2))
                    spent(act, "wep", u, q.n("wep", u, i, (t // 2) * Q))
                    f(w[0][u][:], pA[u], ACT.Relu, bias=one_col("en1_b")).then_inc(sig["eh"][u], 1)
                    if u == 0:
                        for k in range(Q):
                            ready(act, "wep", 0, q.n("wep", 0, i, (t // 2) * Q + k))
                            stored(act, "st_we", k % 2, i * (TILES // RING) + ((t // 2) * 2 + k // 2))
                            f(ring[k % 2][:], ps[:, 1:3, :].rearrange("p a f -> p (a f)"), ACT.Copy
                              ).then_inc(sig["weo"][0], 1)
            sweep(act, EB, body)

            q = p_["P5"]

            def body(i, par, j, q=q):
                for u in SPACES:
                    ready(act, "c1b", u, q.n("c1b", u, i))
                    f(w[2][u][:], w[1][u][:], ACT.Relu, bias=one_col("b3")).then_inc(sig["c5r"][u], 1)
                for u in SPACES:
                    layer_norm(q, u, i)
                for u in SPACES:
                    ready(act, "lin", u, q.n("lin", u, i))
                    f(hn[u], pD[u], ACT.Relu, bias=one_col("lin0_b")).then_inc(sig["hn"][u], 1)
                rows(q, i)
            sweep(act, EB, body)
            tables("T5")

            def gru_pass(q, more):
                def body(i, par, j):
                    for u in SPACES:
                        ready(act, "head", u, q.n("head", u, i))
                        f(w[0][u][:], pA[u], ACT.Relu, bias=one_col("conv_b")).then_inc(sig["m"][u], 1)
                        gru(q, u, i)
                    for u in SPACES:
                        gru_new(q, u, i)
                    more(i)
                sweep(act, EB, body)

            for k, name in enumerate(GRU_PASSES):
                gru_pass(p_[name], lambda i, q=p_[name]: rows(q, i))
                tables(f"T{6 + k}")

            def last_layer(i, q=p_["P11"]):
                layer_norm(q, S_, i)
                relation(q, i)
            gru_pass(p_["P11"], last_layer)
            tables("T11")
            q = p_["P12"]

            def body(i, par, j, q=q):
                ready(act, "head", S_, q.n("head", S_, i))
                f(hb[S_], pA[S_], ACT.Tanh).then_inc(sig["th"][S_], 1)
                relation(q, i)
            sweep(act, EB, body)
            tables("T12")

            q = p_["N"]
            with act.Fori(0, NP) as i:
                for u in (0, 1):
                    ready(act, "head", u, q.n("head", u, i))
                    f(xb[u][:], pA[u], ACT.Copy).then_inc(sig["xb"][u], 1)
                for u in (0, 1):
                    layer_norm(q, u, i, 0)
                for u in (0, 1):
                    sage(q, u, i)
                for u in (0, 1):
                    layer_norm(q, u, i, 1)
                for t in range(T):
                    for u in (0, 1):
                        ready(act, "q1", u, q.n("q1", u, i, t))
                        f(w[1][u][:], pA[u], ACT.Relu, bias=one_col("b1")).then_inc(sig["q1r"][u], 1)
                    for u in (0, 1):
                        ready(act, "q5", u, q.n("q5", u, i, t))
                        spent(act, "q7", u, q.n("q7", u, i, t))
                        f(w[2][u][:], pB[u], ACT.Relu, bias=one_col("b2")).then_inc(sig["q6"][u], 1)
                for u in (0, 1):
                    ready(act, "q7", u, q.n("q7", u, i, T - 1))
                    f(w[1][u][:], pD[u], ACT.Relu, bias=one_col("b3")).then_inc(sig["c5r"][u], 1)
                for u in (0, 1):
                    layer_norm(q, u, i, 2)
                for u in (0, 1):
                    ready(act, "lin", u, q.n("lin", u, i))
                    f(hn[u], pD[u], ACT.Relu, bias=one_col("lin0_b")).then_inc(sig["hn"][u], 1)
                for k in range(STEPS):
                    for u in (0, 1):
                        ready(act, "gr", u, q.n("gr", u, i, k))
                        f(w[1][u][:], pB[u], ACT.Sigmoid, bias=one_col("nr")).then_inc(sig["r"][u], 1)
                        ready(act, "gz", u, q.n("gz", u, i, k))
                        f(w[2][u][:], pC[u], ACT.Sigmoid, bias=one_col("nz")).then_inc(sig["z"][u], 1)
                    for u in (0, 1):
                        ready(act, "rh", u, q.n("rh", u, i, k))
                        f(w[1][u][:], w[3][u][:], ACT.Tanh, bias=one_col("nn")).then_inc(sig["n"][u], 1)
                for u in (0, 1):
                    ready(act, "ot", u, q.n("ot", u, i))
                    stored(act, "st_out", u, q.n("st_out", u, i))
                    f(db[u][:], pA[u], ACT.Copy).then_inc(sig["oc"][u], 1)

            q = p_["P13"]
            stored(act, "st_out", D_, NP)

            def body(i, par, j, q=q):
                ready(act, "ot", D_, q.n("ot", D_, i))
                spent(act, "scattered", D_, q.n("scattered", D_, i))
                f(db[D_][:], pB[D_], ACT.Copy).then_inc(sig["oc"][D_], 1)
            sweep(act, EB, body)

        @block.vector
        def _(dve):
            v = nc.vector

            def rank3(ap, n):
                return ap.rearrange("p (a b) -> p a b", b=n)

            def rsqrt(u, q, i, sub=0):
                ready(dve, "ln_sd", u, q.n("ln_sd", u, i, sub))
                v.reciprocal(root[u][:], root[u][:]).then_inc(sig["ln_r0"][u], 1)
                ready(dve, "ln_r0", u, q.n("ln_r0", u, i, sub))
                v.tensor_tensor(newton[u][:], root[u][:], root[u][:], ALU.mult).then_inc(sig["ln_a"][u], 1)
                ready(dve, "ln_a", u, q.n("ln_a", u, i, sub))
                v.scalar_tensor_tensor(newton[u][:], newton[u][:], -0.5, var[u][:], ALU.mult, ALU.mult
                                       ).then_inc(sig["ln_b"][u], 1)
                ready(dve, "ln_b", u, q.n("ln_b", u, i, sub))
                v.scalar_tensor_tensor(root[u][:], newton[u][:], 1.5, root[u][:], ALU.add, ALU.mult
                                       ).then_inc(sig["ln_y"][u], 1)
                ready(dve, "ln_y", u, q.n("ln_y", u, i, sub))

            def layer_norm(q, u, i, dst, sub=0):
                ready(dve, "ln_v", u, q.n("ln_v", u, i, sub))
                v.tensor_scalar(var[u][:], pC[u][:, 0:TILES], 1e-5, None, ALU.add).then_inc(sig["ln_s"][u], 1)
                rsqrt(u, q, i, sub)
                v.tensor_copy(rank3(w[2][u][:], D), root[u][:].rearrange("p (k a) -> p k a", a=1)
                              .to_broadcast([P, TILES, D])).then_inc(sig["ln_r"][u], 1)
                ready(dve, "ln_relu", u, q.n("ln_relu", u, i, sub))
                ready(dve, "ln_t", u, q.n("ln_t", u, i, sub))
                v.tensor_tensor(dst, w[1][u][:], pD[u], ALU.mult).then_inc(sig["ln"][u], 1)

            def run_sums(q, i, messages):
                spent(dve, "scan", S_, q.n("scan", S_, i))
                v.tensor_tensor_scan(scan[:, bass.ds(i * W + 1, W)], blk(keep, i), messages, scan[:, bass.ds(i * W, 1)],
                                     ALU.mult, ALU.add).then_inc(sig["scan"][S_], 1)

            def tables(name, after):
                q = p_[name]
                if after:
                    pass_over(dve, after)
                ready(dve, "tab_end", 0, q.n("tab_end", 0, 0))
                v.tensor_copy(carry[:], pA[0][:, 0:1]).then_inc(sig["carry"][0], 1)
                ready(dve, "carry", 0, q.n("carry", 0, 0))

                def body(i, par, j):
                    spent(dve, "tab_t", par, q.n("tab_t", par, j))
                    if name == "T_setup":
                        spent(dve, "deg_sd", par, q.n("deg_sd", par, j))
                    v.scalar_tensor_tensor(tab_in[par][:], blk(first, i), carry[:], scan[:, bass.ds(i * W + 1, W)],
                                           ALU.mult, ALU.add).then_inc(sig["tab_sum"][par], 1)
                    if name == "T_setup":
                        ready(dve, "deg_sd", par, q.n("deg_sd", par, j))
                        stored(dve, "st_d", par, q.n("st_d", par, j))
                        v.reciprocal(w[1][par][:], w[0][par][:]).then_inc(sig["deg_r"][par], 1)
                sweep(dve, EB, body)

            def gru(q, u, i):
                ready(dve, "ghn", u, q.n("ghn", u, i))
                ready(dve, "r", u, q.n("r", u, i))
                v.scalar_tensor_tensor(w[3][u][:], pD[u], one_col("hn"), w[1][u][:], ALU.add, ALU.mult
                                       ).then_inc(sig["rh"][u], 1)
                ready(dve, "rh", u, q.n("rh", u, i))
                ready(dve, "gin", u, q.n("gin", u, i))
                v.tensor_tensor(w[4][u][:], w[3][u][:], pA[u], ALU.add).then_inc(sig["npre"][u], 1)

            def gru_blend(q, u, i, old, new, kind, sub=0):
                ready(dve, "n", u, q.n("n", u, i, sub))
                v.tensor_tensor(w[3][u][:], old, w[1][u][:], ALU.subtract).then_inc(sig["u1"][u], 1)
                ready(dve, "u1", u, q.n("u1", u, i, sub))
                ready(dve, "z", u, q.n("z", u, i, sub))
                v.tensor_tensor(w[4][u][:], w[3][u][:], w[2][u][:], ALU.mult).then_inc(sig["u2"][u], 1)
                ready(dve, "u2", u, q.n("u2", u, i, sub))
                v.tensor_tensor(new, w[4][u][:], w[1][u][:], ALU.add).then_inc(sig[kind][u], 1)

            def edge_messages(q, i):
                ready(dve, "hrm", S_, q.n("hrm", S_, i))
                for k in range(TILES + 1):
                    if k < TILES:
                        landed(dve, "ld_w", k % RING, q.n("ld_w", k % RING, i, k // RING))
                        tile = rank3(ring[k % RING], D)
                        state = h_rows[:, k * D:k * D + D].rearrange("p (a i) -> p a i", a=1).to_broadcast([P, D, D])
                        v.tensor_tensor(tile, tile, state, ALU.mult).then_inc(sig["pr"][S_], 1)
                    if k:
                        m = k - 1
                        ready(dve, "pr", S_, q.n("pr", S_, i, m))
                        v.tensor_reduce(msg_rows[:, m * D:m * D + D], rank3(ring[m % RING][:], D), AX_X, ALU.add
                                        ).then_inc(sig["rd"][S_], 1)
                ready(dve, "mf", S_, q.n("mf", S_, i))
                run_sums(q, i, pC[S_])

            def relation_messages(q, i):
                v.tensor_tensor(onehot[:], etype[:, bass.ds(i * TILES, TILES)].rearrange("p (k a) -> p k a", a=1)
                                .to_broadcast([P, TILES, R]),
                                rel_id[:].rearrange("p (a r) -> p a r", a=1).to_broadcast([P, TILES, R]),
                                ALU.is_equal).then_inc(sig["oh"][S_], 1)
                ready(dve, "oh", S_, q.n("oh", S_, i))
                ready(dve, "hrm", S_, q.n("hrm", S_, i))
                for k in range(TILES + 1):
                    if k < TILES:
                        spent(dve, "zt", S_, q.n("zt", S_, i, k), 2)
                        v.tensor_tensor(rank3(Z[k % 2][:], D),
                                        h_rows[:, k * D:k * D + D].rearrange("p (a i) -> p a i", a=1).to_broadcast([P, T, D]),
                                        tv[:, bass.ds(i * TILES + k, 1), :].rearrange("p a (q b) -> p (a q) b", b=1)
                                        .to_broadcast([P, T, D]), ALU.mult).then_inc(sig["zz"][S_], 1)
                    if k:
                        m, half = k - 1, ((k - 1) % 2) * D * R
                        picked = rank3(w[0][S_][:, half:half + D * R], R)
                        ready(dve, "rg", S_, q.n("rg", S_, i, m))
                        v.tensor_tensor(picked, rank3((pD, pA)[m % 2][S_][:, 0:D * R], R),
                                        onehot[:, m:m + 1, :].to_broadcast([P, D, R]), ALU.mult).then_inc(sig["rgm"][S_], 1)
                        ready(dve, "rgm", S_, q.n("rgm", S_, i, m))
                        v.tensor_reduce(msg_rows[:, m * D:m * D + D], picked, AX_X, ALU.add).then_inc(sig["rd"][S_], 1)
                ready(dve, "mf", S_, q.n("mf", S_, i))
                run_sums(q, i, pA[S_])

            v.memset(scan[:], 0.0).then_inc(s_set, 1)
            dve.wait_ge(s_bd, 16 * 2 * T)
            v.tensor_tensor(keep[:], h[0][:].bitcast(I32), h[1][:].bitcast(I32), ALU.is_equal).then_inc(s_set, 1)
            dve.wait_ge(s_set, 2)
            v.tensor_tensor_scan(first[:], keep[:], keep[:], 1.0, ALU.min, ALU.min).then_inc(s_set, 1)
            dve.wait_ge(s_start, 48)
            dve.wait_ge(s_set, 3)
            v.tensor_tensor_scan(scan[:, 1:EC + 1], keep[:], keep[:], 0.0, ALU.mult, ALU.add).then_inc(s_set, 1)
            dve.wait_ge(s_const, 16 * 11)
            dve.wait_ge(s_idx, 16 * 3)
            v.tensor_copy(first_end[:], first[:, EC - 1:EC]).then_inc(s_own, 1)
            dve.wait_ge(s_own, 1)
            v.tensor_scalar(w[0][0][:, 0:P], mat["next_quarter"], first_end[:], None, ALU.mult).then_inc(s_set, 1)
            dve.wait_ge(s_pset, 1)
            dve.wait_ge(s_set, 5)
            v.scalar_tensor_tensor(w[1][0][:, 0:P], pA[0][:, 0:P], first_end[:], w[0][0][:, 0:P], ALU.mult, ALU.add
                                   ).then_inc(s_set, 1)
            dve.wait_ge(s_pset, 2)
            v.tensor_tensor(carry_mat[:], pB[0][:, 0:P], mat["next_quarter"], ALU.add).then_inc(s_set, 1)
            v.tensor_tensor(one_col("r"), one_col("ir"), one_col("hr"), ALU.add).then_inc(s_set, 1)
            v.tensor_tensor(one_col("z"), one_col("iz"), one_col("hz"), ALU.add).then_inc(s_set, 1)
            v.tensor_scalar(w[2][0][:, 0:1], one_col("conv_b"), 0.0, None, ALU.max).then_inc(s_set, 1)
            dve.wait_ge(s_set, 10)
            dve.wait_ge(s_pset, 5)
            for k, (name, part) in enumerate((("nr", "r"), ("nz", "z"), ("nn", "in"))):
                v.tensor_tensor(one_col(name), pC[0][:, k:k + 1], one_col(part), ALU.add).then_inc(s_set, 1)
            v.tensor_tensor(run_a, idx["dst"][:], idx["row"][:], ALU.not_equal).then_inc(s_set, 1)
            dve.wait_ge(s_set, 14)
            v.tensor_scalar(run_b, run_a, -float(BIG), float(BIG), ALU.mult, ALU.add).then_inc(s_set, 1)
            dve.wait_ge(s_set, 15)
            v.tensor_tensor(idx["run_end"][:], run_b, idx["dst"][:], ALU.add).then_inc(s_set, 1)
            v.tensor_copy(ends[:, :, 0:1], slot_row.rearrange("p (k a) -> p k a", a=1)).then_inc(s_set, 1)
            for t in range(T):
                last = v.tensor_copy(spread_bf[:, t, :], mat[f"spread{t}"])
            last.then_inc(s_set, 1)
            tables("T_setup", None)
            q = p_["ENDS"]
            for par in (0, 1):
                stored(dve, "st_d", par, q.n("st_d", par, 0))

            def body(i, par, j, q=q):
                dve.wait_ge(s_tg[par], (j + 1) * (16 * TILES))
                settle(dve)
                v.tensor_copy(idx["row"][:, bass.ds(i * TILES, TILES)].rearrange("p (k a) -> p k a", a=1),
                              pair_slot[par][:, :, 0:1]).then_inc(sig["ends_row"][par], 1)
                ready(dve, "ends_sd", par, q.n("ends_sd", par, j))
                v.reciprocal(deg_small[par][:], deg_small[par][:]).then_inc(sig["ends_r"][par], 1)
                ready(dve, "ends_r", par, q.n("ends_r", par, j))
                spent(dve, "ends_t", par, q.n("ends_t", par, j))
                v.tensor_copy(rank3(w[0][par][:], D), deg_small[par][:].rearrange("p (k a) -> p k a", a=1)
                              .to_broadcast([P, TILES, D])).then_inc(sig["ends_bc"][par], 1)
            sweep(dve, EB, body)

            q = p_["P0"]

            def body(i, par, j, q=q):
                for u in SPACES:
                    layer_norm(q, u, i, blk(h[u], i))
                ready(dve, "ln", S_, q.n("ln", S_, i))
                run_sums(q, i, blk(h[S_], i))
            sweep(dve, EB, body)
            tables("T0", "P0")

            q = p_["P1"]

            def sage(q, u, i, sub, kind):
                ready(dve, "l0x_mm", u, q.n("l0x_mm", u, i))
                v.scalar_tensor_tensor(xb[u][:], pD[u], one_col("b_out"), xb[u][:], ALU.add, ALU.add
                                       ).then_inc(sig[kind][u], 1)

            def body(i, par, j, q=q):
                for u in SPACES:
                    landed(dve, "ld_x", u, q.n("ld_x", u, i))
                    sage(q, u, i, 0, "l0x")
                ready(dve, "l0y", S_, q.n("l0y", S_, i))
                run_sums(q, i, pA[S_])
            sweep(dve, EB, body)
            tables("T1", "P1")

            q = p_["P2"]

            def body(i, par, j, q=q):
                for u in SPACES:
                    ready(dve, "head", u, q.n("head", u, i))
                    landed(dve, "ld_x", u, q.n("ld_x", u, i))
                    v.tensor_tensor(xb[u][:], xb[u][:], pA[u], ALU.add).then_inc(sig["xb"][u], 1)
                for u in SPACES:
                    layer_norm(q, u, i, hb[u])
                for u in SPACES:
                    ready(dve, "ln", u, q.n("ln", u, i))
                    landed(dve, "ld_d", u, q.n("ld_d", u, i))
                    v.tensor_tensor(blk(h[u], i), hb[u], db[u][:], ALU.mult).then_inc(sig["g"][u], 1)
                ready(dve, "g", S_, q.n("g", S_, i))
                run_sums(q, i, blk(h[S_], i))
            sweep(dve, EB, body)
            tables("T2", "P2")

            q = p_["P3"]

            def body(i, par, j, q=q):
                for u in SPACES:
                    ready(dve, "head", u, q.n("head", u, i))
                    v.tensor_tensor(w[0][u][:], blk(h[u], i), pA[u], ALU.add).then_inc(sig["c1a"][u], 1)
                for u in SPACES:
                    ready(dve, "c1a", u, q.n("c1a", u, i))
                    landed(dve, "ld_d", u, q.n("ld_d", u, i))
                    v.tensor_tensor(blk(h[u], i), w[0][u][:], db[u][:], ALU.mult).then_inc(sig["g"][u], 1)
            sweep(dve, EB, body)

            v.memset(carry[:], 0.0).then_inc(s_end4, 1)
            q = p_["T3"]
            for t in range(T):
                def body(i, par, j, t=t, q=q):
                    off = t * halves(EB)[par]
                    ready(dve, "b1r", par, q.n("b1r", par, j, off))
                    ready(dve, "bd", par, q.n("bd", par, j, off))
                    v.tensor_tensor(w[2][par][:], w[1][par][:], pB[par], ALU.mult).then_inc(sig["bm"][par], 1)
                    ready(dve, "bm", par, q.n("bm", par, j, off))
                    ready(dve, "bk", par, q.n("bk", par, j, off))
                    dve.wait_ge(s_end4, i + (t * EB + 1))
                    v.tensor_tensor_scan(w[3][par][:], pC[par], w[2][par][:], carry[:], ALU.mult, ALU.add
                                         ).then_inc(sig["b3"][par], 1)
                    ready(dve, "b3", par, q.n("b3", par, j, off))
                    v.tensor_copy(carry[:], w[3][par][:, W - 1:W]).then_inc(s_end4, 1)
                sweep(dve, EB, body)

            q = p_["P4"]

            def body(i, par, j, q=q):
                for t in range(T):
                    for u in SPACES:
                        ready(dve, "q1r", u, q.n("q1r", u, i, t))
                        ready(dve, "qd", u, q.n("qd", u, i, t))
                        v.tensor_tensor(w[2][u][:], w[1][u][:], pC[u], ALU.mult).then_inc(sig["q2"][u], 1)
                    for u in SPACES:
                        ready(dve, "q2", u, q.n("q2", u, i, t))
                        ready(dve, "q_head", u, q.n("q_head", u, i, t))
                        v.tensor_tensor(w[4][u][:], w[2][u][:], pA[u], ALU.add).then_inc(sig["q3"][u], 1)
                    for u in SPACES:
                        ready(dve, "q3", u, q.n("q3", u, i, t))
                        v.tensor_tensor(w[2][u][:], w[4][u][:], pC[u], ALU.mult).then_inc(sig["q4"][u], 1)
                for u in SPACES:
                    ready(dve, "q7", u, q.n("q7", u, i, T - 1))
                    v.tensor_tensor(blk(h[u], i), pD[u], db[u][:], ALU.mult).then_inc(sig["g"][u], 1)
                ready(dve, "g", S_, q.n("g", S_, i))
                run_sums(q, i, blk(h[S_], i))
            sweep(dve, EB, body)
            tables("T4", "P4")

            q = p_["WE"]

            def body(i, par, j, q=q):
                for t in (1, 3):
                    for k in range(Q):
                        ready(dve, "wep", 1, q.n("wep", 1, i, (t // 2) * Q + k))
                        stored(dve, "st_we", 2 + k % 2, i * (TILES // RING) + ((t // 2) * 2 + k // 2))
                        v.tensor_copy(ring[2 + k % 2][:], ps[:, 5:7, :].rearrange("p a f -> p (a f)")
                                      ).then_inc(sig["weo"][1], 1)
            sweep(dve, EB, body)

            q = p_["P5"]

            def body(i, par, j, q=q):
                for u in SPACES:
                    ready(dve, "head", u, q.n("head", u, i))
                    v.tensor_tensor(w[0][u][:], blk(h[u], i), pA[u], ALU.add).then_inc(sig["c1a"][u], 1)
                for u in SPACES:
                    ready(dve, "c1a", u, q.n("c1a", u, i))
                    landed(dve, "ld_d", u, q.n("ld_d", u, i))
                    v.tensor_tensor(w[1][u][:], w[0][u][:], db[u][:], ALU.mult).then_inc(sig["c1b"][u], 1)
                for u in SPACES:
                    ready(dve, "c5r", u, q.n("c5r", u, i))
                    landed(dve, "ld_x", u, q.n("ld_x", u, i))
                    v.tensor_tensor(xb[u][:], xb[u][:], w[2][u][:], ALU.add).then_inc(sig["xb"][u], 1)
                for u in SPACES:
                    layer_norm(q, u, i, hb[u])
                for u in SPACES:
                    ready(dve, "hn", u, q.n("hn", u, i))
                    settle(dve)
                    v.tensor_copy(blk(h[u], i), hn[u]).then_inc(sig["hs"][u], 1)
                edge_messages(q, i)
            sweep(dve, EB, body)
            tables("T5", "P5")

            for k, name in enumerate(GRU_PASSES):
                def body(i, par, j, q=p_[name]):
                    for u in SPACES:
                        gru(q, u, i)
                    gru_blend(q, S_, i, blk(h[S_], i), hn[S_], "hn")
                    gru_blend(q, D_, i, blk(h[D_], i), blk(h[D_], i), "hs")
                    ready(dve, "hn", S_, q.n("hn", S_, i))
                    settle(dve)
                    v.tensor_copy(blk(h[S_], i), hn[S_]).then_inc(sig["hs"][S_], 1)
                    edge_messages(q, i)
                sweep(dve, EB, body)
                tables(f"T{6 + k}", name)

            q = p_["P11"]

            def body(i, par, j, q=q):
                for u in SPACES:
                    gru(q, u, i)
                for u in SPACES:
                    gru_blend(q, u, i, blk(h[u], i), hn[u], "hn")
                for u in SPACES:
                    ready(dve, "hn", u, q.n("hn", u, i))
                    landed(dve, "ld_x", u, q.n("ld_x", u, i))
                    v.tensor_tensor(xb[u][:], xb[u][:], hn[u], ALU.add).then_inc(sig["xb"][u], 1)
                layer_norm(q, S_, i, hb[S_])
                relation_messages(q, i)
            sweep(dve, EB, body)
            tables("T11", "P11")
            q = p_["P12"]

            def body(i, par, j, q=q):
                relation_messages(q, i)
            sweep(dve, EB, body)
            tables("T12", "P12")

            q = p_["N"]
            with dve.Fori(0, NP) as i:
                for u in (0, 1):
                    layer_norm(q, u, i, hb[u], 0)
                for u in (0, 1):
                    sage(q, u, i, 1, "xb")
                for u in (0, 1):
                    layer_norm(q, u, i, hb[u], 1)
                for u in (0, 1):
                    ready(dve, "c5r", u, q.n("c5r", u, i))
                    v.tensor_tensor(xb[u][:], xb[u][:], w[1][u][:], ALU.add).then_inc(sig["xb"][u], 1)
                for u in (0, 1):
                    layer_norm(q, u, i, hb[u], 2)
                for k in range(STEPS):
                    for u in (0, 1):
                        ready(dve, "ghn", u, q.n("ghn", u, i, k))
                        ready(dve, "r", u, q.n("r", u, i, k))
                        v.scalar_tensor_tensor(w[3][u][:], pD[u], one_col("hn"), w[1][u][:], ALU.add, ALU.mult
                                               ).then_inc(sig["rh"][u], 1)
                    for u in (0, 1):
                        gru_blend(q, u, i, hn[u], hn[u], "hn", k)
                for u in (0, 1):
                    ready(dve, "hn", u, q.n("hn", u, i, STEPS))
                    v.tensor_tensor(w[0][u][:], xb[u][:], hn[u], ALU.add).then_inc(sig["of"][u], 1)

            q = p_["P13"]

            def body(i, par, j, q=q):
                ready(dve, "head", D_, q.n("head", D_, i))
                landed(dve, "ld_x", D_, q.n("ld_x", D_, i))
                v.tensor_tensor(w[0][D_][:], xb[D_][:], pA[D_], ALU.add).then_inc(sig["of"][D_], 1)
            sweep(dve, EB, body)


def kernel(**inputs):
    import numpy as _np
    import concourse.bacc as _bacc
    from concourse import mybir as _mybir
    from concourse.bass_utils import run_bass_kernel_spmd as _run

    a = {k: _np.asarray(v) for k, v in inputs.items()}
    f32, i32 = _np.float32, _np.int32
    nodes, edges = a["x"].shape[0], a["src"].shape[0]
    NP = -(-(nodes + 2) // (2 * W * T))
    EB = -(-edges // (W * T))
    NR, EC = NP * 2 * W, EB * W
    NODES, GE = NR * T, EC * T

    def rows_of(flat):
        v = flat.reshape((T, EC // P, P) + flat.shape[1:])
        v = v.transpose((2, 1, 0) + tuple(range(3, v.ndim)))
        return _np.ascontiguousarray(v.reshape((P, GE // P) + flat.shape[1:]))

    def pad(v, n, fill=0):
        return _np.concatenate([v, _np.full((n - v.shape[0],) + v.shape[1:], fill, v.dtype)])

    src = pad(a["src"], GE, nodes + 1)
    dst = pad(a["dst"], GE, nodes)
    before = _np.concatenate([_np.full((1,), -1, dst.dtype), dst[:-1]])
    after = _np.concatenate([dst[1:], _np.full((1,), -1, dst.dtype)])

    def quarters(v):
        return _np.ascontiguousarray(v.reshape(T, EC))

    def four(m, rows, cols, r_step=None, c_step=None, ts=range(T)):
        z = _np.zeros((P, P), m.dtype)
        for j, t in enumerate(ts):
            r, c = rows(j, t), cols(j, t)
            z[r:r + m.shape[0], c:c + m.shape[1]] = m
        return z

    own, pair, zero = (lambda j, t: t * D), (lambda j, t: j * H0), (lambda j, t: 0)
    g = {k: a["L2_gnn_" + k] for k in ("gru_wih", "gru_whh", "gru_bih", "gru_bhh")}
    wts = {}
    for k in (0, 1):
        ts = (2 * k, 2 * k + 1)
        wts[f"l0_l{k}"] = four(a["L0_gnn_W_l_in"].T, own, pair, ts=ts)
        wts[f"l0_r{k}"] = four(a["L0_gnn_W_r_in"].T, own, pair, ts=ts)
        wts[f"l0_ol{k}"] = four(a["L0_gnn_W_l_out"].T, pair, own, ts=ts)
        wts[f"l0_or{k}"] = four(a["L0_gnn_W_r_out"].T, pair, own, ts=ts)
    for t in range(T):
        wts[f"w1_{t}"] = four(a["L1_gnn_W1"], own, zero, ts=(t,))
        wts[f"w3_{t}"] = four(a["L1_gnn_W3"], zero, own, ts=(t,))
    wts["w2"] = a["L1_gnn_W2"]
    wts["lin0"] = four(a["L2_gnn_lin0_w"].T, own, own)
    for k, name in enumerate("rzn"):
        wts["i" + name] = four(g["gru_wih"][k * D:k * D + D].T, own, own)
        wts["h" + name] = four(g["gru_whh"][k * D:k * D + D].T, own, own)
    wts["en2b"] = four(a["L2_gnn_en2_b"].reshape(D, D), own, own)
    tile = lambda v: _np.concatenate([v] * (P // v.shape[0]))
    cols = {"b_in": a["L0_gnn_b_l_in"], "b_out": a["L0_gnn_b_l_out"], "b1": a["L1_gnn_b1"], "b2": a["L1_gnn_b2"],
            "b3": a["L1_gnn_b3"], "lin0_b": a["L2_gnn_lin0_b"], "en1_b": a["L2_gnn_en1_b"], "conv_b": a["L2_gnn_conv_bias"],
            "zero": _np.zeros(1, f32), "eps": _np.full(1, 1e-5, f32), "one": _np.ones(1, f32), "two": _np.full(1, 2, f32)}
    for k, name in enumerate("rzn"):
        cols["i" + name] = g["gru_bih"][k * D:k * D + D]
        cols["h" + name] = g["gru_bhh"][k * D:k * D + D]
    slot = _np.arange(GE)
    data = {
        "x": pad(a["x"], NODES).reshape(NR, P),
        "src": rows_of(src), "dst": rows_of(dst), "dst_after": rows_of(after),
        "dst_fm": quarters(dst), "dst_before_fm": quarters(before),
        "edge_attr_T": _np.ascontiguousarray(pad(a["edge_attr_32"], GE).T),
        "tv_T": _np.ascontiguousarray(pad(a["edge_attr_4"], GE).T.reshape(T, T, EC)),
        "tv": rows_of(pad(a["edge_attr_4"], GE)), "etype": rows_of(pad(a["edge_type_8"], GE)),
        "mats": shape_matrices(), "weights": _np.stack([wts[k] for k in WEIGHTS], 1),
        "biases": _np.stack([tile(cols[k]) for k in BIASES[:NB_LOADED]], 1),
        "en1": _np.ascontiguousarray(a["L2_gnn_en1_w"].T),
        "en2": _np.ascontiguousarray(a["L2_gnn_en2_w"].reshape(D, D, P).transpose(2, 1, 0).reshape(P, D * D)),
        "rel_w": _np.ascontiguousarray(_np.stack([a[f"L3_gnn_W{k}"].transpose(1, 2, 3, 0).reshape(P, D * R) for k in (1, 2)], 1)),
        "rel_b": _np.ascontiguousarray(_np.stack([a[f"L3_gnn_b{k}"].transpose(1, 2, 0).reshape(T, D * R) for k in (1, 2)], 1)),
        "rel_id": _np.ascontiguousarray(_np.broadcast_to(_np.arange(R, dtype=f32), (P, R))),
        "slot_row": rows_of(((slot % EC + 1) * T + slot // EC).astype(f32)),
    }
    nc = _bacc.Bacc("TRN2", target_bir_lowering=False, num_devices=1)
    arrays, ins = {}, {}
    for name, v in data.items():
        v = _np.ascontiguousarray(v)
        arrays[f"in_{name}_dram"] = v
        ins[name] = nc.dram_tensor(f"in_{name}_dram", v.shape, _mybir.dt.from_np(v.dtype), kind="ExternalInput").ap()
    out = nc.dram_tensor("out_0_dram", (NR, P), _mybir.dt.float32, kind="ExternalOutput").ap()
    gnn_kernel(nc, ins, out)
    r = _run(nc, [arrays], core_ids=[0])
    return _np.asarray(r.results[0]["out_0_dram"]).reshape(NODES, D)[:nodes]
```

```python
from contextlib import ExitStack

import numpy as np

import concourse.bass as bass
from concourse import mybir

P = 128
W = 512
Q = W // P
T = 4
D = 32
H0 = 64
H1 = 128
R = 8
STEPS = 6
TILES = Q * T
BIG = 1 << 22
CREDIT = 4

ALU = mybir.AluOpType
ACT = mybir.ActivationFunctionType
BF16 = mybir.dt.bfloat16
F32 = mybir.dt.float32
I32 = mybir.dt.int32
AX_X = mybir.AxisListType.X
SPACES = (0, 1)
S_, D_ = SPACES

MATS = ["ident", "center", "next_quarter", "prev_quarter"] + [f"spread{t}" for t in range(T)] + ["member_mean"]
WEIGHTS = (["l0_l0", "l0_l1", "l0_r0", "l0_r1", "l0_ol0", "l0_ol1", "l0_or0", "l0_or1"]
           + [f"w1_{t}" for t in range(T)] + ["w2"] + [f"w3_{t}" for t in range(T)]
           + ["lin0", "ir", "iz", "in", "hr", "hz", "hn", "en2b", "rel_b0", "rel_b1"])
BIASES = ["b_in", "b_out", "b1", "b2", "b3", "lin0_b", "en1_b", "conv_b", "ir", "iz", "in", "hr", "hz", "hn",
          "zero", "eps", "one", "two", "r", "z", "nr", "nz", "nn"]

NB_LOADED = BIASES.index("r")

SIGNALS = ("head xb ln_c ln_relu ln_sq ln_v ln_s ln_sd ln_r0 ln_a ln_b ln_y ln_r ln_t ln agg l0a l0b l0ra l0rb l0x l0y g c1a c1b c5r lin hn hs m gr gz ghn "
           "gin r z rh npre n u1 u2 mt hrm pr rd mf scan q_head q1 q1r qd q2 q3 q4 q5 q6 q7 "
           "b1 b1r bd bk bm b3 b3t b4 tab_end carry tab_sum tab_t tab_rm zz zt ztc rg rgm oh ob obt obc th "
           "of ot oc l0x_mm deg_sd deg_r ends_row ends_sd ends_r ends_bc ends_t ends_d scattered ehp eh wep weo").split()
SHARED = dict(
    b1="q1", b1r="q1r", bd="qd", bk="q2", bm="q3", b3="q4", b3t="q5", b4="q6",
    ends_row="q1", ends_sd="q1r", ends_r="qd", ends_bc="q2", ends_t="q3", ends_d="q4", deg_sd="q5", deg_r="q6",
    ehp="q1", eh="q1r", wep="q5", weo="q6",
    m="q_head", gin="qd", npre="q2", u1="q3", u2="q4",
    agg="q1", l0a="q2", l0b="qd", l0ra="q_head", l0rb="g", l0x="hs", l0x_mm="c1a", l0y="q3",
    c1b="q5", scattered="q1", zz="q5", zt="q6", ztc="q7", rg="q1", rgm="q1r", pr="q6", oh="c5r", ob="c1a", obt="hs", obc="g", th="lin",
    tab_sum="q1", tab_t="q1r", tab_rm="q7", tab_end="c1a", carry="lin")
LOADS = "ld_gs ld_gd ld_g4 ld_x ld_d ld_w ld_ea ld_n".split()
STORES = "st_x st_tab st_tab4 st_we st_out st_d".split()
CHAINS = 4
RING = 4


def shape_matrices():
    m = {"ident": np.eye(P), "center": np.eye(P) - np.kron(np.eye(T), np.full((D, D), 1.0 / D))}
    m["member_mean"] = np.zeros((P, P))
    m["member_mean"][:, 0:T] = np.kron(np.eye(T), np.full((D, 1), 1.0 / D))
    m["next_quarter"] = np.eye(P, k=D)
    m["prev_quarter"] = np.eye(P, k=-D)
    for t in range(T):
        s = np.zeros((P, P))
        s[t * D, :] = 1.0
        m[f"spread{t}"] = s
    return np.stack([m[k] for k in MATS], 1).astype(np.float32)


class Pass:

    def __init__(self, before, uses):
        self.base, self.uses = dict(before), {}
        for (kind, u), use in uses.items():
            self.use(before, kind, u, *use)

    def use(self, before, kind, u, per, blocks):
        key = (SHARED.get(kind, kind), u)
        assert key not in self.uses, (kind, u)
        self.base[key], self.uses[key] = before.get(key, 0), (per, blocks)
        before[key] = self.base[key] + per * blocks

    def n(self, kind, u, i, sub=0):
        key = (SHARED.get(kind, kind), u)
        return i * self.uses[key][0] + (self.base[key] + sub)

    def last(self, kind, u):
        key = (SHARED.get(kind, kind), u)
        per, blocks = self.uses[key]
        return self.base[key] + per * blocks - 1


def halves(n):
    return ((n + 1) // 2, n // 2)


LN = " ln_c ln_relu ln_sq ln_v ln_s ln_sd ln_r0 ln_a ln_b ln_y ln_r ln_t ln"
GRU = " gr gz ghn r z rh n u1 u2"
MSG = " mt hrm pr rd mf scan"
RG = " oh ob obt obc mt hrm zz zt ztc rg rgm rd mf scan"


def plan(EB, NP):
    before = {}
    out = {}

    def add(name, both="", s="", d="", times={}, blocks=(EB, EB), wide=False, gather=True, alternate=""):
        uses = {}
        for u, more in ((S_, s), (D_, d)):
            for k in (both + " " + more).split():
                uses[k, u] = (times.get(k, 1), blocks[u])
        for k in alternate.split():
            for par in (0, 1):
                uses[k, par] = (2, EB) if wide else (1, halves(EB)[par])
        out[name] = Pass(before, uses)

    K16 = {"pr": TILES, "rd": TILES}
    KR = {"zz": Q, "zt": Q, "ztc": Q, "rg": 2 * Q, "rgm": 2 * Q, "rd": 2 * Q}
    Q4 = {k: T for k in "q_head q1 q1r qd q2 q3 q4 q5 q6 q7".split()}
    tab = "tab_sum tab_t tab_rm st_tab"

    def alternate_only(name, kinds, per=1):
        for k in kinds.split():
            for par in (0, 1):
                out[name].use(before, k, par, per, halves(EB)[par])

    def add_tab(name):
        add(name, s="tab_end carry", blocks=(1, 1))
        alternate_only(name, tab)

    def ring(p):
        for slot in range(RING):
            p.use(before, "ld_w", slot, TILES // RING, EB)

    add_tab("T_setup")
    before["st_tab", 0] = before["st_tab", 1] = 0
    alternate_only("T_setup", "deg_sd deg_r st_d")
    add("ENDS")
    alternate_only("ENDS", "ends_row ends_sd ends_r ends_bc ends_t ends_d st_d")
    add("P0", "head xb st_x" + LN, s="scan")
    add("WE", "ehp eh wep weo", s="ld_ea", times={"ehp": 2, "eh": 2, "wep": 2 * Q, "weo": 2 * Q})
    add_tab("T0")
    add("P1", "head st_x ld_x agg l0a l0b l0ra l0rb l0x l0x_mm", s="l0y scan", alternate="ld_gs ld_gd")
    add_tab("T1")
    add("P2", "head xb st_x ld_x ld_d g" + LN, s="scan", alternate="ld_gs ld_gd")
    add_tab("T2")
    add("P3", "head ld_d c1a g", alternate="ld_gs ld_gd")
    n4 = tuple(T * h for h in halves(EB))
    add("T3", "ld_d b1 b1r bd bk bm b3 b3t b4 st_tab4", blocks=n4)
    add("P4", "ld_d g q_head q1 q1r qd q2 q3 q4 q5 q6 q7", s="scan", times=Q4, alternate="ld_gd", wide=True)
    add_tab("T4")
    add("P5", "head ld_d ld_x c1a c1b c5r xb st_x lin hn hs" + LN, s=MSG, times=K16, alternate="ld_gs ld_gd")
    ring(out["P5"])
    add_tab("T5")
    for k in range(6, 5 + STEPS):
        add(f"P{k}", "head hs m gin npre" + GRU, s=MSG + " hn", times=K16, alternate="ld_gs ld_gd")
        ring(out[f"P{k}"])
        add_tab(f"T{k}")
    add("P11", "head ld_x xb hn st_x m gin npre" + GRU, s=LN + RG, times=KR, alternate="ld_gs ld_gd")
    add_tab("T11")
    add("P12", s="head th" + RG, times=KR, alternate="ld_gs")
    add_tab("T12")
    many = {k: 3 for k in LN.split()}
    many.update({k: STEPS for k in GRU.split()}, xb=3, hn=STEPS + 1)
    many.update({k: T for k in "q1 q1r q5 q6 q7".split()})
    many = {k: 2 * many.get(k, 1) for k in ("head l0a l0b l0ra l0rb l0x_mm c5r lin of ot oc q1 q1r q5 q6 q7 xb hn"
                                            + LN + GRU).split()}
    add("N", "head l0a l0b l0ra l0rb l0x_mm c5r lin of ot oc q1 q1r q5 q6 q7 xb hn" + LN + GRU,
        times=many, blocks=(NP, NP))
    add("P13", d="head ld_x of ot oc scattered", alternate="ld_gd")
    used = {key for q in out.values() for key in q.uses}
    return out, used




def gnn_kernel(nc, ins, out):
    GE = ins["edge_attr_T"].shape[1]
    EC = GE // T
    EB = EC // W
    NR = ins["x"].shape[0]
    NP = NR // (CHAINS * W)
    NODES = NR * T
    SLOT_TILES = GE // P
    p_, used = plan(EB, NP)
    TAB = ["T_setup", "T0", "T1", "T2", "T4"] + [f"T{k}" for k in range(5, 13)]
    GRU_PASSES = [f"P{k}" for k in range(6, 5 + STEPS)]

    def dram(name, shape, dt=F32):
        return nc.dram_tensor(name, shape, dt, kind="Internal").ap()

    table = dram("table", (1 + EC, P))
    table4 = dram("table4", (1 + EC, T, P))
    last_of = dram("last_of", (NODES, 2))
    x_sp = dram("x_sp", (2, P, EC))
    d_sp = dram("d_sp", (2, P, EC))
    net = dram("net", (SLOT_TILES, P, D * D))
    prime = dram("prime", (16, P))

    with ExitStack() as ctx:
        def sb(name, shape, dt=F32):
            return ctx.enter_context(nc.sbuf_tensor(name, shape, dt))

        one = lambda name: ctx.enter_context(nc.semaphore(name))

        def sems(names, n=2):
            return {k: [ctx.enter_context(nc.semaphore(f"{k}{u}")) for u in range(n)] for k in names}

        sig = {k: [None, None] for k in SIGNALS}
        for k in SIGNALS:
            for u in (0, 1):
                if k not in SHARED and (k, u) in used:
                    sig[k][u] = one(f"{k}{u}")
        for k, other in SHARED.items():
            sig[k] = sig[other]
        dma = sems([k for k in LOADS + STORES if k not in ("ld_w", "st_we", "ld_n", "st_out")])
        dma["ld_g0"] = sems(["ld_g0"], 4)["ld_g0"]
        dma.update(sems(["ld_w", "st_we"], RING))
        dma.update(sems(["ld_n", "st_out"], CHAINS))
        s_const, s_idx, s_bd, s_start, s_slot, s_settled = one("s_const"), one("s_idx"), one("s_blockdiag"), one("s_start"), one("s_slot"), one("s_settled")
        s_set, s_pset, s_aset = one("s_set_dve"), one("s_set_pe"), one("s_set_act")
        s_table, s_nodes, s_scat, s_own, s_end4 = one("s_table"), one("s_nodes"), one("s_scat"), one("s_own"), one("s_end4")
        s_tg = [one("s_tg0"), one("s_tg1")]
        s_sc = [one("s_sc0"), one("s_sc1")]

        keep = sb("keep", [P, EC], BF16)
        first = sb("first", [P, EC], BF16)
        scan = sb("scan", [P, EC + 1])
        h = [sb(f"h{u}", [P, EC]) for u in SPACES]
        G = [[sb(f"gathered{k}{u}", [P, W])[:] for u in SPACES] for k in (0, 1)]
        w = [[sb(f"w{k}{u}", [P, W]) for u in SPACES] for k in range(5)]
        xb = [sb(f"x_block{u}", [P, W]) for u in SPACES]
        db = [sb(f"d_block{u}", [P, W]) for u in SPACES]
        blocks4 = sb("blocks4", [P, T, W])
        hb = [blocks4[:, u, :] for u in SPACES]
        hn = [blocks4[:, 2 + u, :] for u in SPACES]
        attr_in = blocks4[0:D, :, :]
        h_rows, msg_rows = w[3][0], w[4][0]
        state_rows, sum_rows = xb, db
        tab_in, tab_out = w[3], w[4]
        ring_all = sb("ring", [P, RING * D * D])
        ring = [ring_all[:, k * D * D:(k + 1) * D * D] for k in range(RING)]
        picked = [ring[k][:, 0:W] for k in (0, 1)]
        Z = [ring[2][:, k * W:k * W + W] for k in (0, 1)]
        ZT = [ring[3][:, k * W:k * W + W] for k in (0, 1)]
        mats = sb("mats", [P, len(MATS), P])
        wts = sb("wts", [P, len(WEIGHTS), P])
        bias = sb("bias", [P, len(BIASES)])
        spread_bf = sb("spread_bf", [P, T, P], BF16)
        en1 = sb("en1", [D, P])
        en2 = sb("en2", [P, D * D])
        rel_w = sb("rel_w", [P, 2, D * R])
        tv = sb("tv", [P, SLOT_TILES, T])
        etype = sb("etype", [P, SLOT_TILES], I32)
        rel_id = sb("rel_id", [P, R])
        onehot = sb("onehot", [P, TILES, R])
        idx = {k: sb(f"idx_{k}", [P, SLOT_TILES], I32) for k in ("src", "dst", "run_end", "row")}
        slot_row = w[2][1][:, 0:SLOT_TILES]
        run_a, run_b = w[3][0][:, 0:SLOT_TILES], w[4][0][:, 0:SLOT_TILES]
        ends = sb("ends", [P, SLOT_TILES, 2])
        slot = [sb(f"idx_slot{k}", [P, TILES], I32) for k in (0, 1)]
        pair_slot = [sb(f"pair_slot{k}", [P, TILES, 2]) for k in (0, 1)]
        carry = sb("carry", [P, 1])
        first_end = sb("first_end", [P, 1])
        slot_d = [sb(f"idx_slot_d{k}", [P, TILES], I32) for k in (0, 1)]
        carry_mat = sb("carry_mat", [P, P])
        var, root, newton = ([sb(f"{name}{u}", [P, TILES]) for u in range(CHAINS)] for name in ("var", "root", "newton"))
        deg_small = [sb(f"deg_small{k}", [P, TILES]) for k in (0, 1)]
        ps = ctx.enter_context(nc.psum_tensor("ps", [P, 8, W], F32))
        pA, pB, pC, pD = ([ps[:, 4 * u + k, :] for u in SPACES] for k in range(4))
        member_mean = mats[:, len(MATS) - 1, 0:T]

        class Chain:

            def __init__(self, c):
                self.u, self.turn = c % 2, c // 2
                at = lambda k: h[c - 2][:, k * W:k * W + W]
                if c < 2:
                    self.g, self.x, self.h, self.new, self.out = G[0][c], xb[c][:], hb[c], hn[c], db[c][:]
                    self.w = [w[k][c][:] for k in range(4)]
                else:
                    self.g, self.x, self.h, self.new, self.out = (at(k) for k in range(5))
                    self.w = [at(5 + k) for k in range(4)]
                self.a, self.b = ps[:, 2 * c, :], ps[:, 2 * c + 1, :]
                self.var, self.root, self.newton = var[c][:], root[c][:], newton[c][:]
                self.centred, self.small, self.spread = self.a, self.b, self.b
                self.depth = 2

            def n(self, q, kind, i, sub=0):
                return q.n(kind, self.u, i, 2 * sub + self.turn)

        class Space(Chain):

            def __init__(self, u):
                self.u, self.x, self.w = u, xb[u][:], [w[k][u][:] for k in range(4)]
                self.var, self.root, self.newton = var[u][:], root[u][:], newton[u][:]
                self.centred, self.small, self.spread = pB[u], pC[u], pD[u]
                self.depth = 1

            def n(self, q, kind, i, sub=0):
                return q.n(kind, self.u, i, sub)

        chains = [Chain(c) for c in range(CHAINS)]
        space = [Space(u) for u in SPACES]
        one_col = lambda name: bias[:, BIASES.index(name):BIASES.index(name) + 1]
        mat = {k: mats[:, i, :] for i, k in enumerate(MATS)}
        wt = {k: wts[:, i, :] for i, k in enumerate(WEIGHTS)}

        def settle(eng):
            eng.sem_inc(s_settled, 1)

        def ready(eng, kind, u, n):
            eng.wait_ge(sig[kind][u], n + 1 + CREDIT)
            if eng is nc.sync or eng is nc.gpsimd:
                settle(eng)

        def spent(eng, kind, u, n, depth=1):
            eng.wait_ge(sig[kind][u], n + 1 - depth + CREDIT)
            if eng is nc.sync or eng is nc.gpsimd:
                settle(eng)

        def landed(eng, kind, u, n):
            eng.wait_ge(dma[kind][u], 16 * (n + 1) if isinstance(n, int) else (n + 1) * 16)
            if eng is nc.sync or eng is nc.gpsimd:
                settle(eng)

        def stored(eng, kind, u, n):
            eng.wait_ge(dma[kind][u], 16 * (n + 1) if isinstance(n, int) else (n + 1) * 16)
            if eng is nc.sync or eng is nc.gpsimd:
                settle(eng)

        def sweep(eng, blocks, body):
            if blocks >= 2:
                with eng.Fori(0, blocks // 2) as j:
                    for par in (0, 1):
                        body(j * 2 + par, par, j)
            if blocks % 2:
                body(blocks - 1, 0, blocks // 2)

        def ahead(par, j):
            return 1 - par, j + par

        def sweep_ahead(eng, start, body, last):
            start()
            sweep(eng, EB - 1, lambda i, par, j: body(i, par, j, *ahead(par, j)))
            last(EB - 1, (EB - 1) % 2, (EB - 1) // 2)

        def col(i):
            return bass.ts(i, W)

        def blk(t, i):
            return t[:, bass.ts(i, W)]

        end_of = {"P0": ("scan", "ln"), "P1": ("scan", "l0x"), "P2": ("scan", "g"), "P3": ("g", "g"), "P4": ("scan", "g"),
                  "P5": ("scan", "hs"), "P11": ("scan", "xb"), "P12": ("scan", None), "P13": (None, "oc")}
        end_of.update({k: ("scan", "hs") for k in GRU_PASSES})

        def pass_over(eng, name):
            for u in SPACES:
                if end_of[name][u]:
                    ready(eng, end_of[name][u], u, p_[name].last(end_of[name][u], u))

        block = ctx.enter_context(nc.Block())

        @block.sync
        def _(sp):
            for kind in SIGNALS:
                for u in (0, 1):
                    if kind not in SHARED and sig[kind][u]:
                        sp.sem_inc(sig[kind][u], CREDIT)
            at = 0
            for kind in STORES:
                for x in dma[kind]:
                    sp.dma_start(prime[at:at + 1, :], ins["mats"][at:at + 1, 0, :]).then_inc(x, 16)
                    at += 1
            for t in range(T):
                part = slice(t * D, t * D + D)
                sp.dma_start(h[0][part, :].bitcast(I32), ins["dst_fm"][t:t + 1, :].to_broadcast([D, EC])).then_inc(s_bd, 16)
                sp.dma_start(h[1][part, :].bitcast(I32), ins["dst_before_fm"][t:t + 1, :].to_broadcast([D, EC])).then_inc(s_bd, 16)
            for dst, name in ((mats, "mats"), (bias[:, 0:NB_LOADED], "biases"), (wts, "weights"), (en1, "en1"), (en2, "en2"),
                              (rel_w, "rel_w"), (tv, "tv"), (etype, "etype"), (rel_id, "rel_id"),
                              (slot_row, "slot_row")):
                sp.dma_start(dst if dst is slot_row else dst[:], ins[name]).then_inc(s_const, 16)
            for k, name in (("src", "src"), ("dst", "dst"), ("row", "dst_after")):
                sp.dma_start(idx[k][:], ins[name]).then_inc(s_idx, 16)
            sp.wait_ge(s_set, 1)
            sp.dma_start(last_of.rearrange("(p n) two -> p (n two)", p=P), scan[:, 0:NODES * 2 // P]).then_inc(s_start, 16)
            sp.dma_start(table[0:1, :], scan[0:1, 0:P]).then_inc(s_start, 16)
            sp.dma_start(table4[0:1].rearrange("a t f -> a (t f)"), scan[0:1, 0:T * P]).then_inc(s_start, 16)

            def tables(name):
                q = p_[name]

                def body(i, par, j):
                    ready(sp, "tab_rm", par, q.n("tab_rm", par, j))
                    sp.dma_start(table[bass.ds(i * W + 1, W), :].rearrange("(q p) f -> p q f", p=P),
                                 tab_out[par][:].rearrange("p (q f) -> p q f", q=Q)).then_inc(dma["st_tab"][par], 16)
                sweep(sp, EB, body)
                for par in (0, 1):
                    stored(sp, "st_tab", par, q.last("st_tab", par) + 1)
                sp.sem_inc(s_table, 1)

            def d_rows(name, i, par, j):
                q = p_[name]
                spent(sp, "head", D_, q.n("head", D_, i), 2)
                sp.dma_start(G[par][D_].rearrange("p (q f) -> p q f", q=Q),
                             table[bass.ds(i * W + 1, W), :].rearrange("(q p) f -> p q f", p=P)
                             ).then_inc(dma["ld_gd"][par], 16)

            def gru_io(name):
                def tiles(i, par, j):
                    edge_matrices(p_[name], i)

                def body(i, par, j, par1, j1):
                    d_rows(name, i + 1, par1, j1)
                    tiles(i, par, j)
                sweep_ahead(sp, lambda: d_rows(name, 0, 0, 0), body, tiles)

            def edge_matrices(q, i):
                for k in range(TILES):
                    spent(sp, "rd", S_, q.n("rd", S_, i, k), RING)
                    sp.dma_start(ring[k % RING][:], net[bass.ds(i * TILES + k, 1), :, :].rearrange("a p f -> p (a f)")
                                 ).then_inc(dma["ld_w"][k % RING], 16)

            def pass_io(name, x_load=(), x_store=(), x_kind="xb", d_load=(), rows=True, tiles=False):
                q = p_[name]

                def body(i, par, j):
                    if rows:
                        d_rows(name, i, par, j)
                    for u in x_load:
                        spent(sp, end_of[name][u], u, q.n(end_of[name][u], u, i))
                        if u in x_store:
                            stored(sp, "st_x", u, q.n("st_x", u, i))
                        sp.dma_start(xb[u][:], x_sp[u, :, col(i)]).then_inc(dma["ld_x"][u], 16)
                    for u in d_load:
                        spent(sp, end_of[name][u], u, q.n(end_of[name][u], u, i))
                        sp.dma_start(db[u][:], d_sp[u, :, col(i)]).then_inc(dma["ld_d"][u], 16)
                    for u in x_store:
                        ready(sp, x_kind, u, q.n(x_kind, u, i))
                        sp.dma_start(x_sp[u, :, col(i)], xb[u][:]).then_inc(dma["st_x"][u], 16)
                    if tiles:
                        edge_matrices(q, i)
                sweep(sp, EB, body)
                for u in x_store:
                    stored(sp, "st_x", u, q.last("st_x", u) + 1)

            q = p_["T_setup"]

            def body(i, par, j):
                ready(sp, "deg_r", par, q.n("deg_r", par, j))
                sp.dma_start(d_sp[D_, :, col(i)], w[1][par][:]).then_inc(dma["st_d"][par], 16)
            sweep(sp, EB, body)
            q2 = p_["ENDS"]

            def body(i, par, j):
                ready(sp, "ends_d", par, q2.n("ends_d", par, j))
                sp.dma_start(d_sp[S_, :, col(i)], w[1][par][:]).then_inc(dma["st_d"][par], 16)
            sweep(sp, EB, body)
            for par in (0, 1):
                stored(sp, "st_d", par, q2.last("st_d", par) + 1)

            q, q2 = p_["P0"], p_["WE"]

            def body(i, par, j, q=q, q2=q2):
                for u in (0, 1):
                    spent(sp, "ehp", u, q2.n("ehp", u, i, 0))
                sp.dma_start(attr_in, ins["edge_attr_T"].rearrange("d (t e) -> d t e", t=T)[:, :, col(i)]
                             ).then_inc(dma["ld_ea"][0], 16)
                for u in SPACES:
                    ready(sp, "xb", u, q.n("xb", u, i))
                    sp.dma_start(x_sp[u, :, col(i)], xb[u][:]).then_inc(dma["st_x"][u], 16)
                for t in range(T):
                    for k in range(Q):
                        b, k2 = k % 2, k // 2
                        ready(sp, "weo", b, q2.n("weo", b, i, 2 * t + k2))
                        sp.dma_start(net[bass.ds(i * TILES + (k * T + t), 1), :, :].rearrange("a p f -> p (a f)"),
                                     ring[2 * b + k2]).then_inc(dma["st_we"][2 * b + k2], 16)
            sweep(sp, EB, body)
            for u in SPACES:
                stored(sp, "st_x", u, q.last("st_x", u) + 1)
            for k in range(RING):
                stored(sp, "st_we", k, EB * TILES // RING)
            tables("T0")
            pass_io("P1", x_load=SPACES, x_store=SPACES, x_kind="l0x")
            tables("T1")
            pass_io("P2", x_load=SPACES, x_store=SPACES, d_load=SPACES)
            tables("T2")
            pass_io("P3", d_load=SPACES)

            pass_over(sp, "P3")
            q = p_["T3"]
            for t in range(T):
                def body(i, par, j, t=t):
                    spent(sp, "bd", par, q.n("bd", par, j, t * halves(EB)[par]))
                    sp.dma_start(db[par][:], d_sp[S_, :, col(i)]).then_inc(dma["ld_d"][par], 16)
                    ready(sp, "b4", par, q.n("b4", par, j, t * halves(EB)[par]))
                    sp.dma_start(table4[bass.ds(i * W + 1, W), t, :].rearrange("(q p) f -> p q f", p=P),
                                 w[4][par][:].rearrange("p (q f) -> p q f", q=Q)).then_inc(dma["st_tab4"][par], 16)
                sweep(sp, EB, body)
            for par in (0, 1):
                stored(sp, "st_tab4", par, q.last("st_tab4", par) + 1)
            sp.sem_inc(s_table, 1)

            q = p_["P4"]

            def body(i, par, j):
                for u in SPACES:
                    spent(sp, "g", u, q.n("g", u, i))
                    sp.dma_start(db[u][:], d_sp[u, :, col(i)]).then_inc(dma["ld_d"][u], 16)
                for t in range(T):
                    spent(sp, "q_head", D_, q.n("q_head", D_, i, t), 2)
                    sp.dma_start(G[t % 2][D_].rearrange("p (q f) -> p q f", q=Q),
                                 table4[bass.ds(i * W + 1, W), t, :].rearrange("(q p) f -> p q f", p=P)
                                 ).then_inc(dma["ld_gd"][t % 2], 16)
            sweep(sp, EB, body)
            tables("T4")

            pass_io("P5", x_load=SPACES, x_store=SPACES, d_load=SPACES, tiles=True)
            tables("T5")
            for k, name in enumerate(GRU_PASSES):
                gru_io(name)
                tables(f"T{6 + k}")
            pass_io("P11", x_load=SPACES, x_store=SPACES)
            tables("T11")
            pass_io("P12", rows=False)
            tables("T12")

            q = p_["N"]
            pass_over(sp, "P12")
            with sp.Fori(0, NP) as i:
                for c, b in enumerate(chains):
                    spent(sp, "head", b.u, b.n(q, "head", i), 2)
                    sp.dma_start(b.g.rearrange("p (q f) -> p q f", q=Q),
                                 ins["x"][bass.ds((i * CHAINS + c) * W, W), :].rearrange("(p q) f -> p q f", q=Q)
                                 ).then_inc(dma["ld_n"][c], 16)
                for c, b in enumerate(chains):
                    ready(sp, "oc", b.u, b.n(q, "oc", i))
                    sp.dma_start(out[bass.ds((i * CHAINS + c) * W, W), :].rearrange("(p q) f -> p q f", q=Q),
                                 b.out.rearrange("p (q f) -> p q f", q=Q)).then_inc(dma["st_out"][c], 16)
            for c in range(CHAINS):
                stored(sp, "st_out", c, NP)
            sp.sem_inc(s_nodes, 1)

            pass_io("P13", x_load=(D_,))

        @block.gpsimd
        def _(pool):
            slots = [0]

            def fetch(i, index, dst, rows, dests, done, base, per, sub):
                nc.gpsimd.tensor_copy(dst[:], index[:, bass.ds(i * TILES, TILES)]).then_inc(s_slot, 1)
                pool.wait_ge(s_slot, i * per + (base + sub + 1))
                settle(pool)
                for k in range(TILES):
                    pool.indirect_dma_start(dests(k), None, rows, bass.IndirectOffsetOnAxis(ap=dst[:, k:k + 1], axis=0)
                                            ).then_inc(done, 16)

            q = p_["T_setup"]
            pool.wait_ge(s_set, 18)
            pool.wait_ge(s_start, 48)

            def body(i, par, j):
                ready(pool, "tab_rm", par, q.n("tab_rm", par, j))
                nc.gpsimd.tensor_copy(slot[par][:], idx["run_end"][:, bass.ds(i * TILES, TILES)]).then_inc(s_slot, 1)
                nc.gpsimd.tensor_copy(pair_slot[par][:], ends[:, bass.ds(i * TILES, TILES), :]).then_inc(s_slot, 1)
                pool.wait_ge(s_slot, i * 2 + 2)
                settle(pool)
                for k in range(TILES):
                    pool.indirect_dma_start(last_of, bass.IndirectOffsetOnAxis(ap=slot[par][:, k:k + 1], axis=0),
                                            pair_slot[par][:, k, :], None, bounds_check=NODES - 1, oob_is_err=False
                                            ).then_inc(s_sc[par], 16)
                pool.wait_ge(s_sc[par], (j + 1) * (16 * TILES))
                settle(pool)
            sweep(pool, EB, body)
            slots[0] = 2 * EB
            q2 = p_["ENDS"]

            def body(i, par, j):
                spent(pool, "ends_row", par, q2.n("ends_row", par, j))
                spent(pool, "ends_sd", par, q2.n("ends_sd", par, j))
                fetch(i, idx["src"], slot[par], last_of, lambda k: pair_slot[par][:, k, :], s_tg[par], slots[0], 1, 0)
            sweep(pool, EB, body)
            slots[0] += EB

            for par in (0, 1):
                pool.wait_ge(s_tg[par], halves(EB)[par] * (16 * TILES))
            q3 = p_["P0"]
            x_rows = ins["x"].rearrange("r (t f) -> (r t) f", t=T)

            def body(i, par, j):
                for u, name in ((S_, "src"), (D_, "dst")):
                    spent(pool, "head", u, q3.n("head", u, i), 2)
                    fetch(i, idx[name], (slot if u == S_ else slot_d)[par], x_rows,
                          lambda k: G[par][u][:, k * D:k * D + D], dma["ld_g0"][2 * u + par], slots[0], 2, u)
            sweep(pool, EB, body)
            slots[0] += 2 * EB

            def gather(name, tables_before):
                q = p_[name]
                pool.wait_ge(s_table, tables_before)

                def body(i, par, j):
                    spent(pool, "head", S_, q.n("head", S_, i), 2)
                    fetch(i, idx["row"], slot[par], table.rearrange("r (t f) -> (r t) f", t=T),
                          lambda k: G[par][S_][:, k * D:k * D + D], dma["ld_gs"][par], slots[0], 1, 0)
                sweep(pool, EB, body)
                slots[0] += EB

            for k in (1, 2, 3):
                gather(f"P{k}", k)
            q4 = p_["P4"]
            pool.wait_ge(s_table, 4)

            def body(i, par, j):
                spent(pool, "q_head", S_, q4.n("q_head", S_, i), 2)
                nc.gpsimd.tensor_copy(slot[par][:], idx["row"][:, bass.ds(i * TILES, TILES)]).then_inc(s_slot, 1)
                pool.wait_ge(s_slot, i + (slots[0] + 1))
                settle(pool)
                for t in range(T):
                    spent(pool, "q_head", S_, q4.n("q_head", S_, i, t), 2)
                    for k in range(Q):
                        pool.indirect_dma_start(
                            G[t % 2][S_][:, k * P:k * P + P], None, table4.rearrange("r t f -> (r t) f"),
                            bass.IndirectOffsetOnAxis(ap=slot[par][:, k * T + t:k * T + t + 1], axis=0)
                        ).then_inc(dma["ld_g4"][t % 2], 16)
            sweep(pool, EB, body)
            slots[0] += EB
            for k in range(5, 13):
                gather(f"P{k}", k)

            q5 = p_["P13"]
            pool.wait_ge(s_nodes, 1)

            def body(i, par, j):
                nc.gpsimd.tensor_copy(slot[par][:], idx["run_end"][:, bass.ds(i * TILES, TILES)]).then_inc(s_slot, 1)
                pool.wait_ge(s_slot, i + (slots[0] + 1))
                settle(pool)
                ready(pool, "oc", D_, q5.n("oc", D_, i))
                for k in range(TILES):
                    pool.indirect_dma_start(out.rearrange("r (t f) -> (r t) f", t=T),
                                            bass.IndirectOffsetOnAxis(ap=slot[par][:, k:k + 1], axis=0),
                                            db[D_][:, k * D:k * D + D], None, bounds_check=NODES - 1, oob_is_err=False
                                            ).then_inc(s_scat, 16)
                pool.wait_ge(s_scat, (i + 1) * (16 * TILES))
                settle(pool)
                pool.sem_inc(sig["scattered"][D_], 1)
            sweep(pool, EB, body)

        @block.tensor
        def _(pe):
            mm = nc.tensor.matmul

            def turn(dst, src):
                for k in range(Q):
                    last = nc.tensor.transpose(dst[:, k * P:k * P + P], src[:, k * P:k * P + P], mat["ident"])
                return last

            def centre(q, b, i, sub=0):
                ready(pe, "xb", b.u, b.n(q, "xb", i, sub))
                mm(b.centred, mat["center"], b.x, start=True, stop=True).then_inc(sig["ln_c"][b.u], 1)

            def variances(q, b, i, sub=0):
                ready(pe, "ln_sq", b.u, b.n(q, "ln_sq", i, sub))
                for k in range(Q):
                    last = mm(b.small[:, k * T:k * T + T], b.w[0][:, k * P:k * P + P], member_mean, start=True, stop=True)
                last.then_inc(sig["ln_v"][b.u], 1)

            def scales(q, b, i, sub=0):
                ready(pe, "ln_r", b.u, b.n(q, "ln_r", i, sub))
                turn(b.spread, b.w[2]).then_inc(sig["ln_t"][b.u], 1)

            def layer_norm(q, bs, i, sub=0):
                for stage in (centre, variances, scales):
                    for b in bs:
                        stage(q, b, i, sub)

            def head(q, u, i, par, j, load, ends):
                landed_n(pe, load, par, q, i, j)
                spent(pe, ends, u, q.n(ends, u, i))
                turn(pA[u], G[par][u]).then_inc(sig["head"][u], 1)

            def landed_n(eng, load, par, q, i, j):
                if load == "ld_gs":
                    eng.wait_ge(dma[load][par], (q.n(load, par, j) + 1) * (16 * TILES))
                else:
                    landed(eng, load, par, q.n(load, par, j))

            def gru(q, u, i, state):
                mm(pD[u], wt["hn"], state, start=True, stop=True).then_inc(sig["ghn"][u], 1)
                mm(pB[u], wt["hr"], state, start=True, stop=False)
                ready(pe, "m", u, q.n("m", u, i))
                mm(pB[u], wt["ir"], w[0][u][:], start=False, stop=True).then_inc(sig["gr"][u], 1)
                mm(pC[u], wt["hz"], state, start=True, stop=False)
                mm(pC[u], wt["iz"], w[0][u][:], start=False, stop=True).then_inc(sig["gz"][u], 1)
                mm(pA[u], wt["in"], w[0][u][:], start=True, stop=True).then_inc(sig["gin"][u], 1)

            def to_rows(q, i, kind, src):
                ready(pe, kind, S_, q.n(kind, S_, i))
                turn(pB[S_], src).then_inc(sig["mt"][S_], 1)

            def edge_messages(q, i):
                to_rows(q, i, "hn", hn[S_])
                mm(pC[S_], wt["en2b"], hn[S_], start=True, stop=False)
                ready(pe, "rd", S_, q.n("rd", S_, i, TILES - 1))
                for k in range(Q):
                    last = mm(pC[S_][:, k * P:k * P + P], msg_rows[:, k * P:k * P + P], mat["ident"],
                              start=False, stop=(k == Q - 1))
                last.then_inc(sig["mf"][S_], 1)

            def relation_messages(q, i, kind, layer):
                to_rows(q, i, kind, hb[S_])
                ready(pe, "ob", S_, q.n("ob", S_, i))
                turn(pC[S_], w[2][S_]).then_inc(sig["obt"][S_], 1)
                for g in range(Q + 1):
                    if g < Q:
                        ready(pe, "zz", S_, q.n("zz", S_, i, g))
                        if g == 1:
                            ready(pe, "obc", S_, q.n("obc", S_, i))
                        spent(pe, "ztc", S_, q.n("ztc", S_, i, g), 2)
                        turn((pB, pC)[g % 2][S_], Z[g % 2]).then_inc(sig["zt"][S_], 1)
                    if g:
                        ready(pe, "ztc", S_, q.n("ztc", S_, i, g - 1))
                        for half, bank in enumerate((pD, pA)):
                            spent(pe, "rgm", S_, q.n("rgm", S_, i, 2 * (g - 1) + half), 2)
                            for t in (0, 1):
                                at = (2 * half + t) * P
                                last = mm(bank[S_][:, t * D * R:(t + 1) * D * R], ZT[(g - 1) % 2][:, at:at + P],
                                          rel_w[:, layer, :], start=True, stop=True)
                            last.then_inc(sig["rg"][S_], 1)
                ready(pe, "rgm", S_, q.n("rgm", S_, i, 2 * Q - 1))
                mm(pA[S_], wt[f"rel_b{layer}"], w[1][S_][:], start=True, stop=False)
                ready(pe, "rd", S_, q.n("rd", S_, i, 2 * Q - 1))
                for k in range(Q):
                    last = mm(pA[S_][:, k * P:k * P + P], msg_rows[:, k * P:k * P + P], mat["ident"],
                              start=False, stop=(k == Q - 1))
                last.then_inc(sig["mf"][S_], 1)

            def tables(name, after):
                q = p_[name]
                if after:
                    pass_over(pe, after)
                mm(pA[0][:, 0:1], carry_mat[:], scan[:, EC:EC + 1], start=True, stop=True).then_inc(sig["tab_end"][0], 1)

                def body(i, par, j):
                    ready(pe, "tab_sum", par, q.n("tab_sum", par, j))
                    spent(pe, "tab_rm", par, q.n("tab_rm", par, j))
                    turn(pD[par], tab_in[par]).then_inc(sig["tab_t"][par], 1)
                sweep(pe, EB, body)

            pe.wait_ge(s_const, 16 * 10)
            pe.wait_ge(s_set, 5)
            mm(pA[0][:, 0:P], mat["prev_quarter"], w[0][0][:, 0:P], start=True, stop=True).then_inc(s_pset, 1)
            pe.wait_ge(s_set, 6)
            mm(pB[0][:, 0:P], mat["prev_quarter"], w[1][0][:, 0:P], start=True, stop=True).then_inc(s_pset, 1)
            pe.wait_ge(s_set, 10)
            for k, name in enumerate(("ir", "iz", "in")):
                mm(pC[0][:, k:k + 1], wt[name], w[2][0][:, 0:1], start=True, stop=True).then_inc(s_pset, 1)
            pe.wait_ge(s_set, 18)
            tables("T_setup", None)
            q = p_["ENDS"]

            def body(i, par, j):
                ready(pe, "ends_bc", par, q.n("ends_bc", par, j))
                spent(pe, "ends_d", par, q.n("ends_d", par, j))
                turn(pA[par], w[0][par]).then_inc(sig["ends_t"][par], 1)
            sweep(pe, EB, body)

            for par in (0, 1):
                ready(pe, "ends_d", par, q.last("ends_d", par))
            q = p_["P0"]

            def body(i, par, j, q=q, q2=p_["WE"]):
                for u in SPACES:
                    spent(pe, "weo", u, q2.n("weo", u, i))
                for u in SPACES:
                    pe.wait_ge(dma["ld_g0"][2 * u + par], (j + 1) * (16 * TILES))
                    spent(pe, end_of["P0"][u], u, q.n(end_of["P0"][u], u, i))
                    turn(pA[u], G[par][u]).then_inc(sig["head"][u], 1)
                layer_norm(q, space, i)
                ready(pe, "scan", S_, q.n("scan", S_, i))
                ready(pe, "ln", D_, q.n("ln", D_, i))
                landed(pe, "ld_ea", 0, q2.n("ld_ea", 0, i))

                def hidden(t):
                    mm(pA[t % 2], en1[:], attr_in[:, t, :], start=True, stop=True).then_inc(sig["ehp"][t % 2], 1)
                hidden(0)
                for t in range(T):
                    if t + 1 < T:
                        hidden(t + 1)
                    ready(pe, "eh", t % 2, q2.n("eh", t % 2, i, t // 2))
                    for k in range(Q):
                        b = k % 2
                        spent(pe, "weo", b, q2.n("weo", b, i, 2 * t + k // 2))
                        lhs = w[0][t % 2][:, k * P:k * P + P]
                        mm(pB[b], lhs, en2[:, 0:W], start=True, stop=True)
                        mm(pC[b], lhs, en2[:, W:2 * W], start=True, stop=True).then_inc(sig["wep"][b], 1)
            sweep(pe, EB, body)
            tables("T0", "P0")

            q = p_["P1"]

            def sage(q, u, i, state, messages):
                for k, (dst, kind) in enumerate(((pB, "l0a"), (pC, "l0b"))):
                    mm(dst[u], wt[f"l0_l{k}"], w[0][u][:], start=True, stop=False)
                    mm(dst[u], wt[f"l0_r{k}"], state, start=False, stop=True).then_inc(sig[kind][u], 1)
                ready(pe, "l0ra", u, q.n("l0ra", u, i))
                ready(pe, "l0rb", u, q.n("l0rb", u, i))
                if messages:
                    mm(pA[u], wt["l0_ol0"], w[1][u][:], start=True, stop=False)
                    mm(pA[u], wt["l0_ol1"], w[2][u][:], start=False, stop=True).then_inc(sig["l0y"][u], 1)
                mm(pD[u], wt["l0_or0"], w[1][u][:], start=True, stop=False)
                mm(pD[u], wt["l0_or1"], w[2][u][:], start=False, stop=True).then_inc(sig["l0x_mm"][u], 1)

            def body(i, par, j, q=q):
                for u in SPACES:
                    head(q, u, i, par, j, ("ld_gs", "ld_gd")[u], end_of["P1"][u])
                for u in SPACES:
                    ready(pe, "agg", u, q.n("agg", u, i))
                    sage(q, u, i, blk(h[u], i), u == S_)
            sweep(pe, EB, body)
            tables("T1", "P1")

            q = p_["P2"]

            def body(i, par, j, q=q):
                for u in SPACES:
                    head(q, u, i, par, j, ("ld_gs", "ld_gd")[u], end_of["P2"][u])
                layer_norm(q, space, i)
            sweep(pe, EB, body)
            tables("T2", "P2")

            q = p_["P3"]

            def body(i, par, j, q=q):
                for u in SPACES:
                    head(q, u, i, par, j, ("ld_gs", "ld_gd")[u], end_of["P3"][u])
            sweep(pe, EB, body)
            pass_over(pe, "P3")

            q = p_["T3"]
            for t in range(T):
                def body(i, par, j, t=t, q=q):
                    spent(pe, "b4", par, q.n("b4", par, j, t * halves(EB)[par]))
                    mm(pA[par], wt[f"w1_{t}"], blk(h[S_], i), start=True, stop=True).then_inc(sig["b1"][par], 1)
                    landed(pe, "ld_d", par, q.n("ld_d", par, j, t * halves(EB)[par]))
                    mm(pB[par], mat[f"spread{t}"], db[par][:], start=True, stop=True
                       ).then_inc(sig["bd"][par], 1)
                    mm(pC[par], spread_bf[:, t, :], blk(keep, i), start=True, stop=True
                       ).then_inc(sig["bk"][par], 1)
                    ready(pe, "b3", par, q.n("b3", par, j, t * halves(EB)[par]))
                    turn(pD[par], w[3][par]).then_inc(sig["b3t"][par], 1)
                sweep(pe, EB, body)
            for par in (0, 1):
                ready(pe, "b4", par, q.last("b4", par))

            q = p_["P4"]

            def body(i, par, j, q=q):
                for t in range(T):
                    for u in SPACES:
                        if u == S_:
                            pe.wait_ge(dma["ld_g4"][t % 2], (i * 2 + (t // 2 + 1)) * (16 * Q))
                        else:
                            landed(pe, "ld_gd", t % 2, q.n("ld_gd", t % 2, i, t // 2))
                        spent(pe, "q3", u, q.n("q3", u, i, t))
                        turn(pA[u], G[t % 2][u]).then_inc(sig["q_head"][u], 1)
                        spent(pe, "q6", u, q.n("q6", u, i, t))
                        mm(pB[u], wt[f"w1_{t}"], blk(h[u], i), start=True, stop=True).then_inc(sig["q1"][u], 1)
                        spent(pe, "q4", u, q.n("q4", u, i, t))
                        landed(pe, "ld_d", u, q.n("ld_d", u, i))
                        mm(pC[u], mat[f"spread{t}"], db[u][:], start=True, stop=True).then_inc(sig["qd"][u], 1)
                    for u in SPACES:
                        ready(pe, "q4", u, q.n("q4", u, i, t))
                        mm(pB[u], wt["w2"], w[2][u][:], start=True, stop=True).then_inc(sig["q5"][u], 1)
                    for u in SPACES:
                        ready(pe, "q6", u, q.n("q6", u, i, t))
                        if t == 0:
                            spent(pe, "g", u, q.n("g", u, i))
                        mm(pD[u], wt[f"w3_{t}"], w[3][u][:], start=(t == 0), stop=(t == T - 1)
                           ).then_inc(sig["q7"][u], 1)
            sweep(pe, EB, body)
            tables("T4", "P4")

            q = p_["P5"]

            def body(i, par, j, q=q):
                for u in SPACES:
                    head(q, u, i, par, j, ("ld_gs", "ld_gd")[u], end_of["P5"][u])
                layer_norm(q, space, i)
                for u in SPACES:
                    ready(pe, "ln", u, q.n("ln", u, i))
                    mm(pD[u], wt["lin0"], hb[u], start=True, stop=True).then_inc(sig["lin"][u], 1)
                edge_messages(q, i)
            sweep(pe, EB, body)
            tables("T5", "P5")

            for k, name in enumerate(GRU_PASSES):
                q = p_[name]

                def step(i, par, j, q=q):
                    for u in SPACES:
                        head(q, u, i, par, j, ("ld_gs", "ld_gd")[u], "hs")
                        if u == S_:
                            spent(pe, "scan", u, q.n("scan", u, i), 2)
                            spent(pe, "hrm", u, q.n("hrm", u, i))
                        gru(q, u, i, blk(h[u], i))
                    to_rows(q, i, "hn", hn[S_])

                def messages(i, par, j, q=q):
                    ready(pe, "hs", S_, q.n("hs", S_, i))
                    ready(pe, "rd", S_, q.n("rd", S_, i, TILES - 1))
                    mm(pC[S_], wt["en2b"], blk(h[S_], i), start=True, stop=False)
                    for k in range(Q):
                        last = mm(pC[S_][:, k * P:k * P + P], sum_rows[par][:, k * P:k * P + P], mat["ident"],
                                  start=False, stop=(k == Q - 1))
                    last.then_inc(sig["mf"][S_], 1)

                def body(i, par, j, par1, j1):
                    step(i + 1, par1, j1)
                    messages(i, par, j)
                sweep_ahead(pe, lambda: step(0, 0, 0), body, messages)
                tables(f"T{6 + k}", name)

            q = p_["P11"]

            def body(i, par, j, q=q):
                for u in SPACES:
                    head(q, u, i, par, j, ("ld_gs", "ld_gd")[u], end_of["P11"][u])
                    gru(q, u, i, blk(h[u], i))
                layer_norm(q, space[:1], i)
                relation_messages(q, i, "ln", 0)
            sweep(pe, EB, body)
            tables("T11", "P11")
            q = p_["P12"]

            def body(i, par, j, q=q):
                head(q, S_, i, par, j, "ld_gs", "scan")
                relation_messages(q, i, "th", 1)
            sweep(pe, EB, body)
            tables("T12", "P12")

            q = p_["N"]
            for par in (0, 1):
                ready(pe, "tab_rm", par, p_["T12"].last("tab_rm", par))
            with pe.Fori(0, NP) as i:
                for c, b in enumerate(chains):
                    landed(pe, "ld_n", c, i)
                    spent(pe, "oc", b.u, b.n(q, "oc", i), 2)
                    turn(b.a, b.g).then_inc(sig["head"][b.u], 1)
                layer_norm(q, chains, i, 0)
                for b in chains:
                    ready(pe, "ln", b.u, b.n(q, "ln", i, 0))
                    mm(b.a, wt["l0_r0"], b.h, start=True, stop=True).then_inc(sig["l0a"][b.u], 1)
                    mm(b.b, wt["l0_r1"], b.h, start=True, stop=True).then_inc(sig["l0b"][b.u], 1)
                for b in chains:
                    ready(pe, "l0ra", b.u, b.n(q, "l0ra", i))
                    ready(pe, "l0rb", b.u, b.n(q, "l0rb", i))
                    mm(b.a, wt["l0_or0"], b.w[1], start=True, stop=False)
                    mm(b.a, wt["l0_or1"], b.w[2], start=False, stop=True).then_inc(sig["l0x_mm"][b.u], 1)
                layer_norm(q, chains, i, 1)
                for t in range(T):
                    for b in chains:
                        if t == 0:
                            ready(pe, "ln", b.u, b.n(q, "ln", i, 1))
                        mm(b.a, wt[f"w1_{t}"], b.h, start=True, stop=True).then_inc(sig["q1"][b.u], 1)
                    for b in chains:
                        ready(pe, "q1r", b.u, b.n(q, "q1r", i, t))
                        mm(b.a, wt["w2"], b.w[1], start=True, stop=True).then_inc(sig["q5"][b.u], 1)
                    for b in chains:
                        ready(pe, "q6", b.u, b.n(q, "q6", i, t))
                        mm(b.b, wt[f"w3_{t}"], b.w[2], start=(t == 0), stop=(t == T - 1)).then_inc(sig["q7"][b.u], 1)
                layer_norm(q, chains, i, 2)
                for b in chains:
                    ready(pe, "ln", b.u, b.n(q, "ln", i, 2))
                    mm(b.a, wt["lin0"], b.h, start=True, stop=True).then_inc(sig["lin"][b.u], 1)
                for k in range(STEPS):
                    for b in chains:
                        ready(pe, "hn", b.u, b.n(q, "hn", i, k))
                        mm(b.a, wt["hr"], b.new, start=True, stop=True).then_inc(sig["gr"][b.u], 1)
                        mm(b.b, wt["hz"], b.new, start=True, stop=True).then_inc(sig["gz"][b.u], 1)
                    for b in chains:
                        ready(pe, "r", b.u, b.n(q, "r", i, k))
                        mm(b.a, wt["hn"], b.new, start=True, stop=True).then_inc(sig["ghn"][b.u], 1)
                for b in chains:
                    ready(pe, "of", b.u, b.n(q, "of", i))
                    turn(b.a, b.w[0]).then_inc(sig["ot"][b.u], 1)

            q = p_["P13"]

            def body(i, par, j, q=q):
                head(q, D_, i, par, j, "ld_gd", "oc")
                ready(pe, "of", D_, q.n("of", D_, i))
                turn(pB[D_], w[0][D_]).then_inc(sig["ot"][D_], 1)
            sweep(pe, EB, body)

        @block.scalar
        def _(act):
            f = nc.scalar.activation

            def layer_norm(q, bs, i, sub=0):
                for b in bs:
                    ready(act, "ln_c", b.u, b.n(q, "ln_c", i, sub))
                    f(b.w[0], b.centred, ACT.Square).then_inc(sig["ln_sq"][b.u], 1)
                    f(b.w[1], b.centred, ACT.Relu).then_inc(sig["ln_relu"][b.u], 1)
                for b in bs:
                    ready(act, "ln_s", b.u, b.n(q, "ln_s", i, sub))
                    f(b.root, b.var, ACT.Sqrt).then_inc(sig["ln_sd"][b.u], 1)

            def tables(name):
                q = p_[name]

                def body(i, par, j):
                    ready(act, "tab_t", par, q.n("tab_t", par, j))
                    stored(act, "st_tab", par, q.n("st_tab", par, j))
                    f(tab_out[par][:], pD[par], ACT.Copy).then_inc(sig["tab_rm"][par], 1)
                sweep(act, EB, body)

            def sage(q, u, i):
                for k, (src, dst, kind, out_kind) in enumerate(((pB, w[1], "l0a", "l0ra"), (pC, w[2], "l0b", "l0rb"))):
                    ready(act, kind, u, q.n(kind, u, i))
                    f(dst[u][:], src[u], ACT.Relu, bias=one_col("b_in")).then_inc(sig[out_kind][u], 1)

            def gru(q, u, i):
                ready(act, "gr", u, q.n("gr", u, i))
                f(w[1][u][:], pB[u], ACT.Sigmoid, bias=one_col("r")).then_inc(sig["r"][u], 1)
                ready(act, "gz", u, q.n("gz", u, i))
                f(w[2][u][:], pC[u], ACT.Sigmoid, bias=one_col("z")).then_inc(sig["z"][u], 1)

            def gru_new(q, u, i):
                ready(act, "npre", u, q.n("npre", u, i))
                f(w[1][u][:], w[4][u][:], ACT.Tanh, bias=one_col("in")).then_inc(sig["n"][u], 1)

            def rows(q, i):
                ready(act, "mt", S_, q.n("mt", S_, i))
                f(h_rows[:], pB[S_], ACT.Copy).then_inc(sig["hrm"][S_], 1)

            def relation(q, i):
                rows(q, i)
                ready(act, "obt", S_, q.n("obt", S_, i))
                f(w[1][S_][:], pC[S_], ACT.Copy).then_inc(sig["obc"][S_], 1)
                for g in range(Q):
                    ready(act, "zt", S_, q.n("zt", S_, i, g))
                    spent(act, "rg", S_, q.n("rg", S_, i, 2 * g), 3)
                    f(ZT[g % 2], (pB, pC)[g % 2][S_], ACT.Copy).then_inc(sig["ztc"][S_], 1)

            act.wait_ge(s_const, 16 * 10)
            q = p_["T_setup"]

            def body(i, par, j, q=q):
                ready(act, "tab_sum", par, q.n("tab_sum", par, j))
                spent(act, "deg_r", par, q.n("deg_r", par, j))
                f(w[0][par][:], tab_in[par][:], ACT.Sqrt, bias=one_col("two")).then_inc(sig["deg_sd"][par], 1)
                ready(act, "tab_t", par, q.n("tab_t", par, j))
                f(ends[:, bass.ds(i * TILES, TILES), 1:2],
                  pD[par].rearrange("p (k f) -> p k f", f=D)[:, :, 0:1], ACT.Identity, bias=one_col("one")
                  ).then_inc(sig["tab_rm"][par], 1)
            sweep(act, EB, body)
            q = p_["ENDS"]

            def body(i, par, j, q=q):
                act.wait_ge(s_tg[par], (j + 1) * (16 * TILES))
                spent(act, "ends_bc", par, q.n("ends_bc", par, j))
                f(deg_small[par][:].rearrange("p (k a) -> p k a", a=1), pair_slot[par][:, :, 1:2], ACT.Sqrt, bias=one_col("one")
                  ).then_inc(sig["ends_sd"][par], 1)
                ready(act, "ends_t", par, q.n("ends_t", par, j))
                stored(act, "st_d", par, q.n("st_d", par, j))
                f(w[1][par][:], pA[par], ACT.Copy).then_inc(sig["ends_d"][par], 1)
            sweep(act, EB, body)

            q = p_["P0"]
            for par in (0, 1):
                stored(act, "st_d", par, p_["ENDS"].last("st_d", par) + 1)

            def body(i, par, j, q=q, q2=p_["WE"]):
                for u in SPACES:
                    ready(act, "head", u, q.n("head", u, i))
                    stored(act, "st_x", u, q.n("st_x", u, i))
                    f(xb[u][:], pA[u], ACT.Copy).then_inc(sig["xb"][u], 1)
                layer_norm(q, space, i)
                def hidden(t):
                    ready(act, "ehp", t % 2, q2.n("ehp", t % 2, i, t // 2))
                    f(w[0][t % 2][:], pA[t % 2], ACT.Relu, bias=one_col("en1_b")).then_inc(sig["eh"][t % 2], 1)
                hidden(0)
                for t in range(T):
                    if t + 1 < T:
                        hidden(t + 1)
                    for k in (0, 2):
                        ready(act, "wep", 0, q2.n("wep", 0, i, 2 * t + k // 2))
                        stored(act, "st_we", k // 2, i * T + t)
                        f(ring[k // 2], ps[:, 1:3, :].rearrange("p a f -> p (a f)"), ACT.Copy).then_inc(sig["weo"][0], 1)
            sweep(act, EB, body)
            tables("T0")

            q = p_["P1"]

            def body(i, par, j, q=q):
                for u in SPACES:
                    ready(act, "head", u, q.n("head", u, i))
                    f(w[0][u][:], pA[u], ACT.Copy).then_inc(sig["agg"][u], 1)
                for u in SPACES:
                    sage(q, u, i)
            sweep(act, EB, body)
            tables("T1")

            q = p_["P2"]

            def body(i, par, j, q=q):
                layer_norm(q, space, i)
            sweep(act, EB, body)
            tables("T2")

            q = p_["T3"]
            for t in range(T):
                def body(i, par, j, t=t, q=q):
                    off = t * halves(EB)[par]
                    ready(act, "b1", par, q.n("b1", par, j, off))
                    f(w[1][par][:], pA[par], ACT.Relu, bias=one_col("b1")).then_inc(sig["b1r"][par], 1)
                    ready(act, "b3t", par, q.n("b3t", par, j, off))
                    stored(act, "st_tab4", par, q.n("st_tab4", par, j, off))
                    f(w[4][par][:], pD[par], ACT.Copy).then_inc(sig["b4"][par], 1)
                sweep(act, EB, body)

            q = p_["P4"]

            def body(i, par, j, q=q):
                for t in range(T):
                    for u in SPACES:
                        ready(act, "q1", u, q.n("q1", u, i, t))
                        f(w[1][u][:], pB[u], ACT.Relu, bias=one_col("b1")).then_inc(sig["q1r"][u], 1)
                    for u in SPACES:
                        ready(act, "q5", u, q.n("q5", u, i, t))
                        spent(act, "q7", u, q.n("q7", u, i, t))
                        f(w[3][u][:], pB[u], ACT.Relu, bias=one_col("b2")).then_inc(sig["q6"][u], 1)
            sweep(act, EB, body)
            tables("T4")

            q = p_["P5"]

            def body(i, par, j, q=q):
                for u in SPACES:
                    ready(act, "c1b", u, q.n("c1b", u, i))
                    f(w[2][u][:], w[1][u][:], ACT.Relu, bias=one_col("b3")).then_inc(sig["c5r"][u], 1)
                layer_norm(q, space, i)
                for u in SPACES:
                    ready(act, "lin", u, q.n("lin", u, i))
                    f(hn[u], pD[u], ACT.Relu, bias=one_col("lin0_b")).then_inc(sig["hn"][u], 1)
                rows(q, i)
            sweep(act, EB, body)
            tables("T5")

            def gru_pass(q, more):
                def body(i, par, j):
                    for u in SPACES:
                        ready(act, "head", u, q.n("head", u, i))
                        f(w[0][u][:], pA[u], ACT.Relu, bias=one_col("conv_b")).then_inc(sig["m"][u], 1)
                        gru(q, u, i)
                    for u in SPACES:
                        gru_new(q, u, i)
                    more(i, par, j)
                sweep(act, EB, body)

            for k, name in enumerate(GRU_PASSES):
                def new_rows(i, par, j, q=p_[name]):
                    ready(act, "mt", S_, q.n("mt", S_, i))
                    spent(act, "pr", S_, q.n("pr", S_, i), TILES + 1)
                    f(state_rows[par][:], pB[S_], ACT.Copy).then_inc(sig["hrm"][S_], 1)
                gru_pass(p_[name], new_rows)
                tables(f"T{6 + k}")

            def last_layer(i, par, j, q=p_["P11"]):
                layer_norm(q, space[:1], i)
                relation(q, i)
            gru_pass(p_["P11"], last_layer)
            tables("T11")
            q = p_["P12"]

            def body(i, par, j, q=q):
                ready(act, "head", S_, q.n("head", S_, i))
                f(hb[S_], pA[S_], ACT.Tanh).then_inc(sig["th"][S_], 1)
                relation(q, i)
            sweep(act, EB, body)
            tables("T12")

            q = p_["N"]
            with act.Fori(0, NP) as i:
                for b in chains:
                    ready(act, "head", b.u, b.n(q, "head", i))
                    f(b.x, b.a, ACT.Copy).then_inc(sig["xb"][b.u], 1)
                layer_norm(q, chains, i, 0)
                for b in chains:
                    ready(act, "l0a", b.u, b.n(q, "l0a", i))
                    f(b.w[1], b.a, ACT.Relu, bias=one_col("b_in")).then_inc(sig["l0ra"][b.u], 1)
                    ready(act, "l0b", b.u, b.n(q, "l0b", i))
                    f(b.w[2], b.b, ACT.Relu, bias=one_col("b_in")).then_inc(sig["l0rb"][b.u], 1)
                layer_norm(q, chains, i, 1)
                for t in range(T):
                    for b in chains:
                        ready(act, "q1", b.u, b.n(q, "q1", i, t))
                        f(b.w[1], b.a, ACT.Relu, bias=one_col("b1")).then_inc(sig["q1r"][b.u], 1)
                    for b in chains:
                        ready(act, "q5", b.u, b.n(q, "q5", i, t))
                        spent(act, "q7", b.u, b.n(q, "q7", i, t), 2)
                        f(b.w[2], b.a, ACT.Relu, bias=one_col("b2")).then_inc(sig["q6"][b.u], 1)
                for b in chains:
                    ready(act, "q7", b.u, b.n(q, "q7", i, T - 1))
                    f(b.w[1], b.b, ACT.Relu, bias=one_col("b3")).then_inc(sig["c5r"][b.u], 1)
                layer_norm(q, chains, i, 2)
                for b in chains:
                    ready(act, "lin", b.u, b.n(q, "lin", i))
                    f(b.new, b.a, ACT.Relu, bias=one_col("lin0_b")).then_inc(sig["hn"][b.u], 1)
                for k in range(STEPS):
                    for b in chains:
                        ready(act, "gr", b.u, b.n(q, "gr", i, k))
                        f(b.w[1], b.a, ACT.Sigmoid, bias=one_col("nr")).then_inc(sig["r"][b.u], 1)
                        ready(act, "gz", b.u, b.n(q, "gz", i, k))
                        f(b.w[2], b.b, ACT.Sigmoid, bias=one_col("nz")).then_inc(sig["z"][b.u], 1)
                    for b in chains:
                        ready(act, "rh", b.u, b.n(q, "rh", i, k))
                        f(b.w[1], b.w[3], ACT.Tanh, bias=one_col("nn")).then_inc(sig["n"][b.u], 1)
                for c, b in enumerate(chains):
                    ready(act, "ot", b.u, b.n(q, "ot", i))
                    stored(act, "st_out", c, i)
                    f(b.out, b.a, ACT.Copy).then_inc(sig["oc"][b.u], 1)

            q = p_["P13"]
            stored(act, "st_out", D_, NP)

            def body(i, par, j, q=q):
                ready(act, "ot", D_, q.n("ot", D_, i))
                spent(act, "scattered", D_, q.n("scattered", D_, i))
                f(db[D_][:], pB[D_], ACT.Copy).then_inc(sig["oc"][D_], 1)
            sweep(act, EB, body)

        @block.vector
        def _(dve):
            v = nc.vector

            def rank3(ap, n):
                return ap.rearrange("p (a b) -> p a b", b=n)

            def layer_norm(q, bs, i, dsts, sub=0):
                for b in bs:
                    ready(dve, "ln_v", b.u, b.n(q, "ln_v", i, sub))
                    v.tensor_scalar(b.var, b.small[:, 0:TILES], 1e-5, None, ALU.add).then_inc(sig["ln_s"][b.u], 1)
                for b in bs:
                    ready(dve, "ln_sd", b.u, b.n(q, "ln_sd", i, sub))
                    v.reciprocal(b.root, b.root).then_inc(sig["ln_r0"][b.u], 1)
                for b in bs:
                    ready(dve, "ln_r0", b.u, b.n(q, "ln_r0", i, sub))
                    v.tensor_tensor(b.newton, b.root, b.root, ALU.mult).then_inc(sig["ln_a"][b.u], 1)
                for b in bs:
                    ready(dve, "ln_a", b.u, b.n(q, "ln_a", i, sub))
                    v.scalar_tensor_tensor(b.newton, b.newton, -0.5, b.var, ALU.mult, ALU.mult).then_inc(sig["ln_b"][b.u], 1)
                for b in bs:
                    ready(dve, "ln_b", b.u, b.n(q, "ln_b", i, sub))
                    v.scalar_tensor_tensor(b.root, b.newton, 1.5, b.root, ALU.add, ALU.mult).then_inc(sig["ln_y"][b.u], 1)
                for b in bs:
                    ready(dve, "ln_y", b.u, b.n(q, "ln_y", i, sub))
                    v.tensor_copy(rank3(b.w[2], D), b.root.rearrange("p (k a) -> p k a", a=1)
                                  .to_broadcast([P, TILES, D])).then_inc(sig["ln_r"][b.u], 1)
                for b, dst in zip(bs, dsts):
                    ready(dve, "ln_relu", b.u, b.n(q, "ln_relu", i, sub))
                    ready(dve, "ln_t", b.u, b.n(q, "ln_t", i, sub))
                    v.tensor_tensor(dst, b.w[1], b.spread, ALU.mult).then_inc(sig["ln"][b.u], 1)

            def run_sums(q, i, messages):
                spent(dve, "scan", S_, q.n("scan", S_, i))
                v.tensor_tensor_scan(scan[:, bass.ds(i * W + 1, W)], blk(keep, i), messages, scan[:, bass.ds(i * W, 1)],
                                     ALU.mult, ALU.add).then_inc(sig["scan"][S_], 1)

            def tables(name, after):
                q = p_[name]
                if after:
                    pass_over(dve, after)
                ready(dve, "tab_end", 0, q.n("tab_end", 0, 0))
                v.tensor_copy(carry[:], pA[0][:, 0:1]).then_inc(sig["carry"][0], 1)
                ready(dve, "carry", 0, q.n("carry", 0, 0))

                def body(i, par, j):
                    spent(dve, "tab_t", par, q.n("tab_t", par, j))
                    if name == "T_setup":
                        spent(dve, "deg_sd", par, q.n("deg_sd", par, j))
                    v.scalar_tensor_tensor(tab_in[par][:], blk(first, i), carry[:], scan[:, bass.ds(i * W + 1, W)],
                                           ALU.mult, ALU.add).then_inc(sig["tab_sum"][par], 1)
                    if name == "T_setup":
                        ready(dve, "deg_sd", par, q.n("deg_sd", par, j))
                        stored(dve, "st_d", par, q.n("st_d", par, j))
                        v.reciprocal(w[1][par][:], w[0][par][:]).then_inc(sig["deg_r"][par], 1)
                sweep(dve, EB, body)

            def gate(q, u, i):
                ready(dve, "ghn", u, q.n("ghn", u, i))
                ready(dve, "r", u, q.n("r", u, i))
                v.scalar_tensor_tensor(w[3][u][:], pD[u], one_col("hn"), w[1][u][:], ALU.add, ALU.mult
                                       ).then_inc(sig["rh"][u], 1)

            def sum_new(q, u, i):
                ready(dve, "rh", u, q.n("rh", u, i))
                ready(dve, "gin", u, q.n("gin", u, i))
                v.tensor_tensor(w[4][u][:], w[3][u][:], pA[u], ALU.add).then_inc(sig["npre"][u], 1)

            def gru(q, u, i):
                gate(q, u, i)
                sum_new(q, u, i)

            def blend_a(q, u, i, old):
                ready(dve, "n", u, q.n("n", u, i))
                v.tensor_tensor(w[3][u][:], old, w[1][u][:], ALU.subtract).then_inc(sig["u1"][u], 1)

            def blend_b(q, u, i):
                ready(dve, "u1", u, q.n("u1", u, i))
                ready(dve, "z", u, q.n("z", u, i))
                v.tensor_tensor(w[4][u][:], w[3][u][:], w[2][u][:], ALU.mult).then_inc(sig["u2"][u], 1)

            def blend_c(q, u, i, new, kind):
                ready(dve, "u2", u, q.n("u2", u, i))
                v.tensor_tensor(new, w[4][u][:], w[1][u][:], ALU.add).then_inc(sig[kind][u], 1)

            def gru_blend(q, u, i, old, new, kind):
                blend_a(q, u, i, old)
                blend_b(q, u, i)
                blend_c(q, u, i, new, kind)

            def edge_messages(q, i):
                edge_tiles(q, i, h_rows, msg_rows, {})

            def edge_tiles(q, i, h_rows, msg_rows, between):
                ready(dve, "hrm", S_, q.n("hrm", S_, i))
                for k in range(TILES + 1):
                    if k < TILES:
                        landed(dve, "ld_w", k % RING, q.n("ld_w", k % RING, i, k // RING))
                        tile = rank3(ring[k % RING], D)
                        state = h_rows[:, k * D:k * D + D].rearrange("p (a i) -> p a i", a=1).to_broadcast([P, D, D])
                        v.tensor_tensor(tile, tile, state, ALU.mult).then_inc(sig["pr"][S_], 1)
                    if k:
                        m = k - 1
                        ready(dve, "pr", S_, q.n("pr", S_, i, m))
                        v.tensor_reduce(msg_rows[:, m * D:m * D + D], rank3(ring[m % RING][:], D), AX_X, ALU.add
                                        ).then_inc(sig["rd"][S_], 1)
                    if k in between:
                        between[k]()
                ready(dve, "mf", S_, q.n("mf", S_, i))
                run_sums(q, i, pC[S_])

            def relation_messages(q, i):
                v.tensor_tensor(onehot[:], etype[:, bass.ds(i * TILES, TILES)].rearrange("p (k a) -> p k a", a=1)
                                .to_broadcast([P, TILES, R]),
                                rel_id[:].rearrange("p (a r) -> p a r", a=1).to_broadcast([P, TILES, R]),
                                ALU.is_equal).then_inc(sig["oh"][S_], 1)
                ready(dve, "oh", S_, q.n("oh", S_, i))
                ready(dve, "hrm", S_, q.n("hrm", S_, i))
                hot, truth = onehot[:], tv[:, bass.ds(i * TILES, TILES), :]
                v.tensor_tensor(w[2][S_][:].rearrange("p (k r q) -> p k r q", r=R, q=T),
                                hot.rearrange("p k (r a) -> p k r a", a=1).to_broadcast([P, TILES, R, T]),
                                truth.rearrange("p k (a q) -> p k a q", a=1).to_broadcast([P, TILES, R, T]),
                                ALU.mult).then_inc(sig["ob"][S_], 1)
                for g in range(Q + 1):
                    if g < Q:
                        spent(dve, "zt", S_, q.n("zt", S_, i, g), 2)
                        v.tensor_tensor(Z[g % 2].rearrange("p (t q i) -> p t q i", t=T, q=T),
                                        h_rows[:, g * P:g * P + P].rearrange("p (t a i) -> p t a i", t=T, a=1)
                                        .to_broadcast([P, T, T, D]),
                                        tv[:, bass.ds(i * TILES + g * T, T), :].rearrange("p t (q b) -> p t q b", b=1)
                                        .to_broadcast([P, T, T, D]), ALU.mult).then_inc(sig["zz"][S_], 1)
                    if g:
                        for half, bank in enumerate((pD, pA)):
                            m = 2 * (g - 1) + half
                            ready(dve, "rg", S_, q.n("rg", S_, i, m))
                            v.tensor_tensor(picked[half].rearrange("p (t o r) -> p t o r", t=2, r=R),
                                            bank[S_].rearrange("p (t o r) -> p t o r", t=2, r=R),
                                            onehot[:, 2 * m:2 * m + 2, :].rearrange("p t (a r) -> p t a r", a=1)
                                            .to_broadcast([P, 2, D, R]), ALU.mult).then_inc(sig["rgm"][S_], 1)
                            ready(dve, "rgm", S_, q.n("rgm", S_, i, m))
                            v.tensor_reduce(msg_rows[:, 2 * m * D:2 * (m + 1) * D], rank3(picked[half], R), AX_X, ALU.add
                                            ).then_inc(sig["rd"][S_], 1)
                ready(dve, "mf", S_, q.n("mf", S_, i))
                run_sums(q, i, pA[S_])

            v.memset(scan[:], 0.0).then_inc(s_set, 1)
            dve.wait_ge(s_bd, 16 * 2 * T)
            v.tensor_tensor(keep[:], h[0][:].bitcast(I32), h[1][:].bitcast(I32), ALU.is_equal).then_inc(s_set, 1)
            dve.wait_ge(s_set, 2)
            v.tensor_tensor_scan(first[:], keep[:], keep[:], 1.0, ALU.min, ALU.min).then_inc(s_set, 1)
            dve.wait_ge(s_start, 48)
            dve.wait_ge(s_set, 3)
            v.tensor_tensor_scan(scan[:, 1:EC + 1], keep[:], keep[:], 0.0, ALU.mult, ALU.add).then_inc(s_set, 1)
            dve.wait_ge(s_const, 16 * 10)
            dve.wait_ge(s_idx, 16 * 3)
            v.tensor_copy(first_end[:], first[:, EC - 1:EC]).then_inc(s_own, 1)
            dve.wait_ge(s_own, 1)
            v.tensor_scalar(w[0][0][:, 0:P], mat["next_quarter"], first_end[:], None, ALU.mult).then_inc(s_set, 1)
            dve.wait_ge(s_pset, 1)
            dve.wait_ge(s_set, 5)
            v.scalar_tensor_tensor(w[1][0][:, 0:P], pA[0][:, 0:P], first_end[:], w[0][0][:, 0:P], ALU.mult, ALU.add
                                   ).then_inc(s_set, 1)
            dve.wait_ge(s_pset, 2)
            v.tensor_tensor(carry_mat[:], pB[0][:, 0:P], mat["next_quarter"], ALU.add).then_inc(s_set, 1)
            v.tensor_tensor(one_col("r"), one_col("ir"), one_col("hr"), ALU.add).then_inc(s_set, 1)
            v.tensor_tensor(one_col("z"), one_col("iz"), one_col("hz"), ALU.add).then_inc(s_set, 1)
            v.tensor_scalar(w[2][0][:, 0:1], one_col("conv_b"), 0.0, None, ALU.max).then_inc(s_set, 1)
            dve.wait_ge(s_set, 10)
            dve.wait_ge(s_pset, 5)
            for k, (name, part) in enumerate((("nr", "r"), ("nz", "z"), ("nn", "in"))):
                v.tensor_tensor(one_col(name), pC[0][:, k:k + 1], one_col(part), ALU.add).then_inc(s_set, 1)
            v.tensor_tensor(run_a, idx["dst"][:], idx["row"][:], ALU.not_equal).then_inc(s_set, 1)
            dve.wait_ge(s_set, 14)
            v.tensor_scalar(run_b, run_a, -float(BIG), float(BIG), ALU.mult, ALU.add).then_inc(s_set, 1)
            dve.wait_ge(s_set, 15)
            v.tensor_tensor(idx["run_end"][:], run_b, idx["dst"][:], ALU.add).then_inc(s_set, 1)
            v.tensor_copy(ends[:, :, 0:1], slot_row.rearrange("p (k a) -> p k a", a=1)).then_inc(s_set, 1)
            for t in range(T):
                last = v.tensor_copy(spread_bf[:, t, :], mat[f"spread{t}"])
            last.then_inc(s_set, 1)
            tables("T_setup", None)
            q = p_["ENDS"]
            for par in (0, 1):
                stored(dve, "st_d", par, q.n("st_d", par, 0))

            def body(i, par, j, q=q):
                dve.wait_ge(s_tg[par], (j + 1) * (16 * TILES))
                settle(dve)
                v.tensor_copy(idx["row"][:, bass.ds(i * TILES, TILES)].rearrange("p (k a) -> p k a", a=1),
                              pair_slot[par][:, :, 0:1]).then_inc(sig["ends_row"][par], 1)
                ready(dve, "ends_sd", par, q.n("ends_sd", par, j))
                v.reciprocal(deg_small[par][:], deg_small[par][:]).then_inc(sig["ends_r"][par], 1)
                ready(dve, "ends_r", par, q.n("ends_r", par, j))
                spent(dve, "ends_t", par, q.n("ends_t", par, j))
                v.tensor_copy(rank3(w[0][par][:], D), deg_small[par][:].rearrange("p (k a) -> p k a", a=1)
                              .to_broadcast([P, TILES, D])).then_inc(sig["ends_bc"][par], 1)
            sweep(dve, EB, body)

            q = p_["P0"]

            def body(i, par, j, q=q, q2=p_["WE"]):
                layer_norm(q, space, i, [blk(h[u], i) for u in SPACES])
                ready(dve, "ln", S_, q.n("ln", S_, i))
                run_sums(q, i, blk(h[S_], i))
                for t in range(T):
                    for k in (1, 3):
                        ready(dve, "wep", 1, q2.n("wep", 1, i, 2 * t + k // 2))
                        stored(dve, "st_we", 2 + k // 2, i * T + t)
                        v.tensor_copy(ring[2 + k // 2], ps[:, 5:7, :].rearrange("p a f -> p (a f)")
                                      ).then_inc(sig["weo"][1], 1)
            sweep(dve, EB, body)
            tables("T0", "P0")

            q = p_["P1"]

            def sage(q, u, i, sub, kind):
                ready(dve, "l0x_mm", u, q.n("l0x_mm", u, i))
                v.scalar_tensor_tensor(xb[u][:], pD[u], one_col("b_out"), xb[u][:], ALU.add, ALU.add
                                       ).then_inc(sig[kind][u], 1)

            def body(i, par, j, q=q):
                for u in SPACES:
                    landed(dve, "ld_x", u, q.n("ld_x", u, i))
                    sage(q, u, i, 0, "l0x")
                ready(dve, "l0y", S_, q.n("l0y", S_, i))
                run_sums(q, i, pA[S_])
            sweep(dve, EB, body)
            tables("T1", "P1")

            q = p_["P2"]

            def body(i, par, j, q=q):
                for u in SPACES:
                    ready(dve, "head", u, q.n("head", u, i))
                    landed(dve, "ld_x", u, q.n("ld_x", u, i))
                    v.tensor_tensor(xb[u][:], xb[u][:], pA[u], ALU.add).then_inc(sig["xb"][u], 1)
                layer_norm(q, space, i, hb)
                for u in SPACES:
                    ready(dve, "ln", u, q.n("ln", u, i))
                    landed(dve, "ld_d", u, q.n("ld_d", u, i))
                    v.tensor_tensor(blk(h[u], i), hb[u], db[u][:], ALU.mult).then_inc(sig["g"][u], 1)
                ready(dve, "g", S_, q.n("g", S_, i))
                run_sums(q, i, blk(h[S_], i))
            sweep(dve, EB, body)
            tables("T2", "P2")

            q = p_["P3"]

            def body(i, par, j, q=q):
                for u in SPACES:
                    ready(dve, "head", u, q.n("head", u, i))
                    v.tensor_tensor(w[0][u][:], blk(h[u], i), pA[u], ALU.add).then_inc(sig["c1a"][u], 1)
                for u in SPACES:
                    ready(dve, "c1a", u, q.n("c1a", u, i))
                    landed(dve, "ld_d", u, q.n("ld_d", u, i))
                    v.tensor_tensor(blk(h[u], i), w[0][u][:], db[u][:], ALU.mult).then_inc(sig["g"][u], 1)
            sweep(dve, EB, body)

            v.memset(carry[:], 0.0).then_inc(s_end4, 1)
            q = p_["T3"]
            for t in range(T):
                def body(i, par, j, t=t, q=q):
                    off = t * halves(EB)[par]
                    ready(dve, "b1r", par, q.n("b1r", par, j, off))
                    ready(dve, "bd", par, q.n("bd", par, j, off))
                    v.tensor_tensor(w[2][par][:], w[1][par][:], pB[par], ALU.mult).then_inc(sig["bm"][par], 1)
                    ready(dve, "bm", par, q.n("bm", par, j, off))
                    ready(dve, "bk", par, q.n("bk", par, j, off))
                    dve.wait_ge(s_end4, i + (t * EB + 1))
                    v.tensor_tensor_scan(w[3][par][:], pC[par], w[2][par][:], carry[:], ALU.mult, ALU.add
                                         ).then_inc(sig["b3"][par], 1)
                    ready(dve, "b3", par, q.n("b3", par, j, off))
                    v.tensor_copy(carry[:], w[3][par][:, W - 1:W]).then_inc(s_end4, 1)
                sweep(dve, EB, body)

            q = p_["P4"]

            def body(i, par, j, q=q):
                for t in range(T):
                    for u in SPACES:
                        ready(dve, "q1r", u, q.n("q1r", u, i, t))
                        ready(dve, "qd", u, q.n("qd", u, i, t))
                        v.tensor_tensor(w[2][u][:], w[1][u][:], pC[u], ALU.mult).then_inc(sig["q2"][u], 1)
                    for u in SPACES:
                        ready(dve, "q2", u, q.n("q2", u, i, t))
                        ready(dve, "q_head", u, q.n("q_head", u, i, t))
                        v.tensor_tensor(w[4][u][:], w[2][u][:], pA[u], ALU.add).then_inc(sig["q3"][u], 1)
                    for u in SPACES:
                        ready(dve, "q3", u, q.n("q3", u, i, t))
                        v.tensor_tensor(w[2][u][:], w[4][u][:], pC[u], ALU.mult).then_inc(sig["q4"][u], 1)
                for u in SPACES:
                    ready(dve, "q7", u, q.n("q7", u, i, T - 1))
                    v.tensor_tensor(blk(h[u], i), pD[u], db[u][:], ALU.mult).then_inc(sig["g"][u], 1)
                ready(dve, "g", S_, q.n("g", S_, i))
                run_sums(q, i, blk(h[S_], i))
            sweep(dve, EB, body)
            tables("T4", "P4")

            q = p_["P5"]

            def body(i, par, j, q=q):
                for u in SPACES:
                    ready(dve, "head", u, q.n("head", u, i))
                    v.tensor_tensor(w[0][u][:], blk(h[u], i), pA[u], ALU.add).then_inc(sig["c1a"][u], 1)
                for u in SPACES:
                    ready(dve, "c1a", u, q.n("c1a", u, i))
                    landed(dve, "ld_d", u, q.n("ld_d", u, i))
                    v.tensor_tensor(w[1][u][:], w[0][u][:], db[u][:], ALU.mult).then_inc(sig["c1b"][u], 1)
                for u in SPACES:
                    ready(dve, "c5r", u, q.n("c5r", u, i))
                    landed(dve, "ld_x", u, q.n("ld_x", u, i))
                    v.tensor_tensor(xb[u][:], xb[u][:], w[2][u][:], ALU.add).then_inc(sig["xb"][u], 1)
                layer_norm(q, space, i, hb)
                for u in SPACES:
                    ready(dve, "hn", u, q.n("hn", u, i))
                    settle(dve)
                    v.tensor_copy(blk(h[u], i), hn[u]).then_inc(sig["hs"][u], 1)
                edge_messages(q, i)
            sweep(dve, EB, body)
            tables("T5", "P5")

            for k, name in enumerate(GRU_PASSES):
                q = p_[name]

                def own_state(q, i):
                    ready(dve, "hn", S_, q.n("hn", S_, i))
                    settle(dve)
                    v.tensor_copy(blk(h[S_], i), hn[S_]).then_inc(sig["hs"][S_], 1)

                def stages(q, i):
                    return {2: lambda: gate(q, S_, i), 3: lambda: sum_new(q, S_, i),
                            4: lambda: gate(q, D_, i), 5: lambda: sum_new(q, D_, i),
                            6: lambda: blend_a(q, S_, i, blk(h[S_], i)), 7: lambda: blend_b(q, S_, i),
                            8: lambda: blend_c(q, S_, i, hn[S_], "hn"), 9: lambda: own_state(q, i),
                            TILES: lambda: gru_blend(q, D_, i, blk(h[D_], i), blk(h[D_], i), "hs")}

                def start(q=q):
                    for run in stages(q, 0).values():
                        run()

                def body(i, par, j, par1, j1, q=q):
                    edge_tiles(q, i, state_rows[par], sum_rows[par], stages(q, i + 1))

                def last(i, par, j, q=q):
                    edge_tiles(q, i, state_rows[par], sum_rows[par], {})
                sweep_ahead(dve, start, body, last)
                tables(f"T{6 + k}", name)

            q = p_["P11"]

            def body(i, par, j, q=q):
                for u in SPACES:
                    gru(q, u, i)
                for u in SPACES:
                    gru_blend(q, u, i, blk(h[u], i), hn[u], "hn")
                for u in SPACES:
                    ready(dve, "hn", u, q.n("hn", u, i))
                    landed(dve, "ld_x", u, q.n("ld_x", u, i))
                    v.tensor_tensor(xb[u][:], xb[u][:], hn[u], ALU.add).then_inc(sig["xb"][u], 1)
                layer_norm(q, space[:1], i, hb)
                relation_messages(q, i)
            sweep(dve, EB, body)
            tables("T11", "P11")
            q = p_["P12"]

            def body(i, par, j, q=q):
                relation_messages(q, i)
            sweep(dve, EB, body)
            tables("T12", "P12")

            q = p_["N"]
            with dve.Fori(0, NP) as i:
                layer_norm(q, chains, i, [b.h for b in chains], 0)
                for b in chains:
                    ready(dve, "l0x_mm", b.u, b.n(q, "l0x_mm", i))
                    v.scalar_tensor_tensor(b.x, b.a, one_col("b_out"), b.x, ALU.add, ALU.add).then_inc(sig["xb"][b.u], 1)
                layer_norm(q, chains, i, [b.h for b in chains], 1)
                for b in chains:
                    ready(dve, "c5r", b.u, b.n(q, "c5r", i))
                    v.tensor_tensor(b.x, b.x, b.w[1], ALU.add).then_inc(sig["xb"][b.u], 1)
                layer_norm(q, chains, i, [b.h for b in chains], 2)
                for k in range(STEPS):
                    for b in chains:
                        ready(dve, "ghn", b.u, b.n(q, "ghn", i, k))
                        ready(dve, "r", b.u, b.n(q, "r", i, k))
                        v.scalar_tensor_tensor(b.w[3], b.a, one_col("hn"), b.w[1], ALU.add, ALU.mult
                                               ).then_inc(sig["rh"][b.u], 1)
                    for b in chains:
                        ready(dve, "n", b.u, b.n(q, "n", i, k))
                        v.tensor_tensor(b.w[3], b.new, b.w[1], ALU.subtract).then_inc(sig["u1"][b.u], 1)
                        ready(dve, "u1", b.u, b.n(q, "u1", i, k))
                        ready(dve, "z", b.u, b.n(q, "z", i, k))
                        v.tensor_tensor(b.w[3], b.w[3], b.w[2], ALU.mult).then_inc(sig["u2"][b.u], 1)
                        ready(dve, "u2", b.u, b.n(q, "u2", i, k))
                        v.tensor_tensor(b.new, b.w[3], b.w[1], ALU.add).then_inc(sig["hn"][b.u], 1)
                for b in chains:
                    ready(dve, "hn", b.u, b.n(q, "hn", i, STEPS))
                    v.tensor_tensor(b.w[0], b.x, b.new, ALU.add).then_inc(sig["of"][b.u], 1)

            q = p_["P13"]

            def body(i, par, j, q=q):
                ready(dve, "head", D_, q.n("head", D_, i))
                landed(dve, "ld_x", D_, q.n("ld_x", D_, i))
                v.tensor_tensor(w[0][D_][:], xb[D_][:], pA[D_], ALU.add).then_inc(sig["of"][D_], 1)
            sweep(dve, EB, body)


def kernel(**inputs):
    import numpy as _np
    import concourse.bacc as _bacc
    from concourse import mybir as _mybir
    from concourse.bass_utils import run_bass_kernel_spmd as _run

    a = {k: _np.asarray(v) for k, v in inputs.items()}
    f32, i32 = _np.float32, _np.int32
    nodes, edges = a["x"].shape[0], a["src"].shape[0]
    NP = -(-(nodes + 2) // (CHAINS * W * T))
    EB = -(-edges // (W * T))
    NR, EC = NP * CHAINS * W, EB * W
    NODES, GE = NR * T, EC * T

    def rows_of(flat):
        v = flat.reshape((T, EC // P, P) + flat.shape[1:])
        v = v.transpose((2, 1, 0) + tuple(range(3, v.ndim)))
        return _np.ascontiguousarray(v.reshape((P, GE // P) + flat.shape[1:]))

    def pad(v, n, fill=0):
        return _np.concatenate([v, _np.full((n - v.shape[0],) + v.shape[1:], fill, v.dtype)])

    src = pad(a["src"], GE, nodes + 1)
    dst = pad(a["dst"], GE, nodes)
    before = _np.concatenate([_np.full((1,), -1, dst.dtype), dst[:-1]])
    after = _np.concatenate([dst[1:], _np.full((1,), -1, dst.dtype)])

    def quarters(v):
        return _np.ascontiguousarray(v.reshape(T, EC))

    def four(m, rows, cols, r_step=None, c_step=None, ts=range(T)):
        z = _np.zeros((P, P), m.dtype)
        for j, t in enumerate(ts):
            r, c = rows(j, t), cols(j, t)
            z[r:r + m.shape[0], c:c + m.shape[1]] = m
        return z

    own, pair, zero = (lambda j, t: t * D), (lambda j, t: j * H0), (lambda j, t: 0)
    g = {k: a["L2_gnn_" + k] for k in ("gru_wih", "gru_whh", "gru_bih", "gru_bhh")}
    wts = {}
    for k in (0, 1):
        ts = (2 * k, 2 * k + 1)
        wts[f"l0_l{k}"] = four(a["L0_gnn_W_l_in"].T, own, pair, ts=ts)
        wts[f"l0_r{k}"] = four(a["L0_gnn_W_r_in"].T, own, pair, ts=ts)
        wts[f"l0_ol{k}"] = four(a["L0_gnn_W_l_out"].T, pair, own, ts=ts)
        wts[f"l0_or{k}"] = four(a["L0_gnn_W_r_out"].T, pair, own, ts=ts)
    for t in range(T):
        wts[f"w1_{t}"] = four(a["L1_gnn_W1"], own, zero, ts=(t,))
        wts[f"w3_{t}"] = four(a["L1_gnn_W3"], zero, own, ts=(t,))
    wts["w2"] = a["L1_gnn_W2"]
    wts["lin0"] = four(a["L2_gnn_lin0_w"].T, own, own)
    for k, name in enumerate("rzn"):
        wts["i" + name] = four(g["gru_wih"][k * D:k * D + D].T, own, own)
        wts["h" + name] = four(g["gru_whh"][k * D:k * D + D].T, own, own)
    wts["en2b"] = four(a["L2_gnn_en2_b"].reshape(D, D), own, own)
    for k in (0, 1):
        wts[f"rel_b{k}"] = four(a[f"L3_gnn_b{k + 1}"].reshape(R * T, D), own, own)
    tile = lambda v: _np.concatenate([v] * (P // v.shape[0]))
    cols = {"b_in": a["L0_gnn_b_l_in"], "b_out": a["L0_gnn_b_l_out"], "b1": a["L1_gnn_b1"], "b2": a["L1_gnn_b2"],
            "b3": a["L1_gnn_b3"], "lin0_b": a["L2_gnn_lin0_b"], "en1_b": a["L2_gnn_en1_b"], "conv_b": a["L2_gnn_conv_bias"],
            "zero": _np.zeros(1, f32), "eps": _np.full(1, 1e-5, f32), "one": _np.ones(1, f32), "two": _np.full(1, 2, f32)}
    for k, name in enumerate("rzn"):
        cols["i" + name] = g["gru_bih"][k * D:k * D + D]
        cols["h" + name] = g["gru_bhh"][k * D:k * D + D]
    slot = _np.arange(GE)
    data = {
        "x": pad(a["x"], NODES).reshape(NR, P),
        "src": rows_of(src), "dst": rows_of(dst), "dst_after": rows_of(after),
        "dst_fm": quarters(dst), "dst_before_fm": quarters(before),
        "edge_attr_T": _np.ascontiguousarray(pad(a["edge_attr_32"], GE).T),
        "tv": rows_of(pad(a["edge_attr_4"], GE)), "etype": rows_of(pad(a["edge_type_8"], GE)),
        "mats": shape_matrices(), "weights": _np.stack([wts[k] for k in WEIGHTS], 1),
        "biases": _np.stack([tile(cols[k]) for k in BIASES[:NB_LOADED]], 1),
        "en1": _np.ascontiguousarray(a["L2_gnn_en1_w"].T),
        "en2": _np.ascontiguousarray(a["L2_gnn_en2_w"].reshape(D, D, P).transpose(2, 1, 0).reshape(P, D * D)),
        "rel_w": _np.ascontiguousarray(_np.stack([a[f"L3_gnn_W{k}"].transpose(1, 2, 3, 0).reshape(P, D * R) for k in (1, 2)], 1)),
        "rel_id": _np.ascontiguousarray(_np.broadcast_to(_np.arange(R, dtype=f32), (P, R))),
        "slot_row": rows_of(((slot % EC + 1) * T + slot // EC).astype(f32)),
    }
    nc = _bacc.Bacc("TRN2", target_bir_lowering=False, num_devices=1)
    arrays, ins = {}, {}
    for name, v in data.items():
        v = _np.ascontiguousarray(v)
        arrays[f"in_{name}_dram"] = v
        ins[name] = nc.dram_tensor(f"in_{name}_dram", v.shape, _mybir.dt.from_np(v.dtype), kind="ExternalInput").ap()
    out = nc.dram_tensor("out_0_dram", (NR, P), _mybir.dt.float32, kind="ExternalOutput").ap()
    gnn_kernel(nc, ins, out)
    r = _run(nc, [arrays], core_ids=[0])
    return _np.asarray(r.results[0]["out_0_dram"]).reshape(NODES, D)[:nodes]
```

```python
from contextlib import ExitStack

import numpy as np

import concourse.bass as bass
from concourse import mybir

P = 128
W = 512
Q = W // P
T = 4
D = 32
H0 = 64
H1 = 128
R = 8
STEPS = 6
TILES = Q * T
BIG = 1 << 22
CREDIT = 4

ALU = mybir.AluOpType
ACT = mybir.ActivationFunctionType
BF16 = mybir.dt.bfloat16
F32 = mybir.dt.float32
I32 = mybir.dt.int32
AX_X = mybir.AxisListType.X
SPACES = (0, 1)
S_, D_ = SPACES

MATS = ["ident", "center", "next_quarter", "prev_quarter"] + [f"spread{t}" for t in range(T)] + ["member_mean"]
WEIGHTS = (["l0_l0", "l0_l1", "l0_r0", "l0_r1", "l0_ol0", "l0_ol1", "l0_or0", "l0_or1"]
           + [f"w1_{t}" for t in range(T)] + ["w2"] + [f"w3_{t}" for t in range(T)]
           + ["lin0", "ir", "iz", "in", "hr", "hz", "hn", "en2b", "rel_b0", "rel_b1"])
BIASES = ["b_in", "b_out", "b1", "b2", "b3", "lin0_b", "en1_b", "conv_b", "ir", "iz", "in", "hr", "hz", "hn",
          "zero", "eps", "one", "two", "r", "z", "nr", "nz", "nn"]

NB_LOADED = BIASES.index("r")

SIGNALS = ("head xb ln_c ln_relu ln_sq ln_v ln_s ln_sd ln_r0 ln_a ln_b ln_y ln_r ln_t ln agg l0a l0b l0ra l0rb l0x l0y g c1a c1b c5r lin hn hs m gr gz ghn "
           "gin r z rh npre n u1 u2 mt hrm pr rd mf scan q_head q1 q1r qd q2 q3 q4 q5 q6 q7 "
           "b1 b1r bd bk bm b3 b3t b4 tab_end carry tab_sum tab_t tab_rm zz zt ztc rg rgm oh ob obt obc th "
           "of ot oc l0x_mm deg_sd deg_r ends_row ends_sd ends_r ends_bc ends_t ends_d scattered ehp eh wep weo").split()
SHARED = dict(
    b1="q1", b1r="q1r", bd="qd", bk="q2", bm="q3", b3="q4", b3t="q5", b4="q6",
    ends_row="q1", ends_sd="q1r", ends_r="qd", ends_bc="q2", ends_t="q3", ends_d="q4", deg_sd="q5", deg_r="q6",
    ehp="q1", eh="q1r", wep="q5", weo="q6",
    m="q_head", gin="qd", npre="q2", u1="q3", u2="q4",
    agg="q1", l0a="q2", l0b="qd", l0ra="q_head", l0rb="g", l0x="hs", l0x_mm="c1a", l0y="q3",
    c1b="q5", scattered="q1", zz="q5", zt="q6", ztc="q7", rg="q1", rgm="q1r", pr="q6", oh="c5r", ob="c1a", obt="hs", obc="g", th="lin",
    tab_sum="q1", tab_t="q1r", tab_rm="q7", tab_end="c1a", carry="lin")
LOADS = "ld_d4 ld_gs ld_gd ld_g4 ld_x ld_d ld_w ld_ea ld_n".split()
STORES = "st_x st_tab st_tab4 st_we st_out st_d".split()
EARLY = 2
ROWS = 4
CHAINS = 4
RING = 4


def shape_matrices():
    m = {"ident": np.eye(P), "center": np.eye(P) - np.kron(np.eye(T), np.full((D, D), 1.0 / D))}
    m["member_mean"] = np.zeros((P, P))
    m["member_mean"][:, 0:T] = np.kron(np.eye(T), np.full((D, 1), 1.0 / D))
    m["next_quarter"] = np.eye(P, k=D)
    m["prev_quarter"] = np.eye(P, k=-D)
    for t in range(T):
        s = np.zeros((P, P))
        s[t * D, :] = 1.0
        m[f"spread{t}"] = s
    return np.stack([m[k] for k in MATS], 1).astype(np.float32)


class Pass:

    def __init__(self, before, uses):
        self.base, self.uses = dict(before), {}
        for (kind, u), use in uses.items():
            self.use(before, kind, u, *use)

    def use(self, before, kind, u, per, blocks):
        key = (SHARED.get(kind, kind), u)
        assert key not in self.uses, (kind, u)
        self.base[key], self.uses[key] = before.get(key, 0), (per, blocks)
        before[key] = self.base[key] + per * blocks

    def n(self, kind, u, i, sub=0):
        key = (SHARED.get(kind, kind), u)
        return i * self.uses[key][0] + (self.base[key] + sub)

    def last(self, kind, u):
        key = (SHARED.get(kind, kind), u)
        per, blocks = self.uses[key]
        return self.base[key] + per * blocks - 1


def halves(n):
    return ((n + 1) // 2, n // 2)


LN = " ln_c ln_relu ln_sq ln_v ln_s ln_sd ln_r0 ln_a ln_b ln_y ln_r ln_t ln"
GRU = " gr gz ghn r z rh n u1 u2"
MSG = " mt hrm pr rd mf scan"
RG = "th oh ob obt obc mt hrm zz zt ztc rg rgm rd mf"


def plan(EB, NP):
    before = {}
    out = {}

    def add(name, both="", s="", d="", times={}, blocks=(EB, EB), wide=False, gather=True, alternate=""):
        uses = {}
        for u, more in ((S_, s), (D_, d)):
            for k in (both + " " + more).split():
                uses[k, u] = (times.get(k, 1), blocks[u])
        for k in alternate.split():
            for par in (0, 1):
                uses[k, par] = (2, EB) if wide else (1, halves(EB)[par])
        out[name] = Pass(before, uses)

    K16 = {"pr": TILES, "rd": TILES}
    KR = {"zz": Q, "zt": Q, "ztc": Q, "rg": 2 * Q, "rgm": 2 * Q, "rd": 2 * Q}
    Q4 = {k: T for k in "q_head q1 q1r qd q2 q3 q4 q5 q6 q7".split()}
    tab = "tab_sum tab_t tab_rm"

    def alternate_only(name, kinds, per=1):
        for k in kinds.split():
            for par in (0, 1):
                out[name].use(before, k, par, per, halves(EB)[par])

    def add_tab(name):
        add(name, s="tab_end carry", blocks=(1, 1))
        alternate_only(name, tab)
        for b in range(ROWS):
            out[name].use(before, "st_tab", b, 1, len(range(b, EB, ROWS)))

    def ring(p):
        for slot in range(RING):
            p.use(before, "ld_w", slot, TILES // RING, EB)

    many = {k: 3 for k in LN.split()}
    many.update({k: STEPS for k in GRU.split()}, xb=3, hn=STEPS + 1)
    many.update({k: T for k in "q1 q1r q5 q6 q7".split()})
    kinds = "head l0a l0b l0ra l0rb l0x_mm c5r lin of ot oc q1 q1r q5 q6 q7 xb hn" + LN + GRU

    def add_nodes(name, groups):
        add(name, kinds, times={k: 2 * many.get(k, 1) for k in kinds.split()}, blocks=(groups, groups))

    add_tab("T_setup")
    for b in range(ROWS):
        before["st_tab", b] = 0
    alternate_only("T_setup", "deg_sd deg_r st_d")
    add_nodes("N_early", EARLY)
    add("ENDS")
    alternate_only("ENDS", "ends_row ends_sd ends_r ends_bc ends_t ends_d st_d")
    add("P0", "head xb st_x" + LN, s="scan")
    add("WE", "ehp eh wep weo", s="ld_ea", times={"ehp": 2, "eh": 2, "wep": 2 * Q, "weo": 2 * Q})
    add_tab("T0")
    add("P1", "head st_x ld_x agg l0a l0b l0ra l0rb l0x l0x_mm", s="l0y scan", alternate="ld_gs ld_gd")
    add_tab("T1")
    add("P2", "head xb st_x ld_x ld_d g" + LN, s="scan", alternate="ld_gs ld_gd")
    add_tab("T2")
    add("P3", "head ld_d c1a g", alternate="ld_gs ld_gd")
    n4 = tuple(T * h for h in halves(EB))
    add("T3", "ld_d4 b1 b1r bd bk bm b3 b3t b4 st_tab4", blocks=n4)
    add("P4", "ld_d g q_head q1 q1r qd q2 q3 q4 q5 q6 q7", s="scan", times=Q4, alternate="ld_gd", wide=True)
    add_tab("T4")
    add("P5", "head ld_d ld_x c1a c1b c5r xb st_x lin hn hs" + LN, s=MSG, times=K16, alternate="ld_gs ld_gd")
    ring(out["P5"])
    add_tab("T5")
    for k in range(6, 5 + STEPS):
        add(f"P{k}", "head hs m gin npre" + GRU, s=MSG + " hn", times=K16, alternate="ld_gs ld_gd")
        ring(out[f"P{k}"])
        add_tab(f"T{k}")
    add("P11", "head ld_x xb hn m gin npre" + GRU, s=LN, d="st_x", alternate="ld_gs ld_gd")
    for name, more, table in (("R11", "", "T11"), ("P12", "head ld_gs", "T12")):
        add(name, s="scan", alternate=more)
        for k in RG.split():
            alternate_only(name, k, KR.get(k, 1))
        add_tab(table)
    add_nodes("N", NP - EARLY)
    add("P13", d="head ld_x of ot oc scattered", alternate="ld_gd")
    used = {key for q in out.values() for key in q.uses}
    return out, used




def gnn_kernel(nc, ins, out):
    GE = ins["edge_attr_T"].shape[1]
    EC = GE // T
    EB = EC // W
    NR = ins["x"].shape[0]
    NP = NR // (CHAINS * W)
    NODES = NR * T
    SLOT_TILES = GE // P
    p_, used = plan(EB, NP)
    TAB = ["T_setup", "T0", "T1", "T2", "T4"] + [f"T{k}" for k in range(5, 13)]
    GRU_PASSES = [f"P{k}" for k in range(6, 5 + STEPS)]

    def dram(name, shape, dt=F32):
        return nc.dram_tensor(name, shape, dt, kind="Internal").ap()

    table = dram("table", (1 + EC, P))
    table4 = dram("table4", (1 + EC, T, P))
    last_of = dram("last_of", (NODES, 2))
    x_sp = dram("x_sp", (2, P, EC))
    d_sp = dram("d_sp", (2, P, EC))
    net = dram("net", (SLOT_TILES, P, D * D))
    prime = dram("prime", (32, P))

    with ExitStack() as ctx:
        def sb(name, shape, dt=F32):
            return ctx.enter_context(nc.sbuf_tensor(name, shape, dt))

        one = lambda name: ctx.enter_context(nc.semaphore(name))

        def sems(names, n=2):
            return {k: [ctx.enter_context(nc.semaphore(f"{k}{u}")) for u in range(n)] for k in names}

        sig = {k: [None, None] for k in SIGNALS}
        for k in SIGNALS:
            for u in (0, 1):
                if k not in SHARED and (k, u) in used:
                    sig[k][u] = one(f"{k}{u}")
        for k, other in SHARED.items():
            sig[k] = sig[other]
        dma = sems([k for k in LOADS + STORES if k not in ("ld_w", "st_we", "ld_n", "st_out", "st_tab")])
        dma.update(sems(["st_tab"], ROWS))
        dma["ld_g0"] = sems(["ld_g0"], 4)["ld_g0"]
        dma.update(sems(["ld_w", "st_we"], RING))
        dma.update(sems(["ld_n", "st_out"], CHAINS))
        s_const, s_idx, s_bd, s_start, s_slot, s_settled = one("s_const"), one("s_idx"), one("s_blockdiag"), one("s_start"), one("s_slot"), one("s_settled")
        s_pairs = one("s_pairs")
        s_set, s_pset, s_aset = one("s_set_dve"), one("s_set_pe"), one("s_set_act")
        s_table, s_nodes, s_scat, s_own, s_end4 = one("s_table"), one("s_nodes"), one("s_scat"), one("s_own"), one("s_end4")
        s_tg = [one("s_tg0"), one("s_tg1")]
        s_sc = [one("s_sc0"), one("s_sc1")]

        keep = sb("keep", [P, EC], BF16)
        first = sb("first", [P, EC], BF16)
        scan = sb("scan", [P, EC + 1])
        h = [sb(f"h{u}", [P, EC]) for u in SPACES]
        G = [[sb(f"gathered{k}{u}", [P, W])[:] for u in SPACES] for k in (0, 1)]
        w = [[sb(f"w{k}{u}", [P, W]) for u in SPACES] for k in range(5)]
        xb = [sb(f"x_block{u}", [P, W]) for u in SPACES]
        db = [sb(f"d_block{u}", [P, W]) for u in SPACES]
        blocks4 = sb("blocks4", [P, T, W])
        hb = [blocks4[:, u, :] for u in SPACES]
        hn = [blocks4[:, 2 + u, :] for u in SPACES]
        attr_in = blocks4[0:D, :, :]
        h_rows, msg_rows = w[3][0], w[4][0]
        state_rows, sum_rows = xb, db
        tab_in, tab_out = w[3], [w[4][0], w[4][1], w[2][0], w[2][1]]
        ring_all = sb("ring", [P, RING * D * D])
        ring = [ring_all[:, k * D * D:(k + 1) * D * D] for k in range(RING)]
        picked = [[ring[k][:, c * W:c * W + W] for k in (0, 1)] for c in (0, 1)]
        Z = [[ring[2][:, k * W:k * W + W] for k in (0, 1)], [xb[k][:] for k in (0, 1)]]
        ZT = [[ring[3][:, k * W:k * W + W] for k in (0, 1)], [db[k][:] for k in (0, 1)]]
        mats = sb("mats", [P, len(MATS), P])
        wts = sb("wts", [P, len(WEIGHTS), P])
        bias = sb("bias", [P, len(BIASES)])
        spread_bf = sb("spread_bf", [P, T, P], BF16)
        en1 = sb("en1", [D, P])
        en2 = sb("en2", [P, D * D])
        rel_w = sb("rel_w", [P, 2, D * R])
        tv = sb("tv", [P, SLOT_TILES, T])
        etype = sb("etype", [P, SLOT_TILES], I32)
        rel_id = sb("rel_id", [P, R])
        onehot = [sb(f"onehot{c}", [P, TILES, R]) for c in (0, 1)]
        idx = {k: sb(f"idx_{k}", [P, SLOT_TILES], I32) for k in ("src", "dst", "run_end", "row")}
        slot_row = w[2][1][:, 0:SLOT_TILES]
        run_a, run_b = w[3][0][:, 0:SLOT_TILES], w[4][0][:, 0:SLOT_TILES]
        ends = sb("ends", [P, SLOT_TILES, 2])
        slot = [sb(f"idx_slot{k}", [P, TILES], I32) for k in (0, 1)]
        pair_slot = [sb(f"pair_slot{k}", [P, TILES, 2]) for k in (0, 1)]
        src_ends = sb("src_ends", [P, SLOT_TILES, 2])
        carry = sb("carry", [P, 1])
        first_end = sb("first_end", [P, 1])
        slot_d = [sb(f"idx_slot_d{k}", [P, TILES], I32) for k in (0, 1)]
        carry_mat = sb("carry_mat", [P, P])
        var, root, newton = ([sb(f"{name}{u}", [P, TILES]) for u in range(CHAINS)] for name in ("var", "root", "newton"))
        deg_small = [sb(f"deg_small{k}", [P, TILES]) for k in (0, 1)]
        ps = ctx.enter_context(nc.psum_tensor("ps", [P, 8, W], F32))
        pA, pB, pC, pD = ([ps[:, 4 * u + k, :] for u in SPACES] for k in range(4))
        member_mean = mats[:, len(MATS) - 1, 0:T]

        class Chain:

            def __init__(self, c):
                self.u, self.turn = c % 2, c // 2
                at = lambda k: h[c - 2][:, k * W:k * W + W]
                if c < 2:
                    self.g, self.x, self.h, self.new, self.out = G[0][c], xb[c][:], hb[c], hn[c], db[c][:]
                    self.w = [w[k][c][:] for k in range(4)]
                else:
                    self.g, self.x, self.h, self.new, self.out = (at(k) for k in range(5))
                    self.w = [at(5 + k) for k in range(4)]
                self.a, self.b = ps[:, 2 * c, :], ps[:, 2 * c + 1, :]
                self.var, self.root, self.newton = var[c][:], root[c][:], newton[c][:]
                self.centred, self.small, self.spread = self.a, self.b, self.b
                self.depth = 2

            def n(self, q, kind, i, sub=0):
                return q.n(kind, self.u, i, 2 * sub + self.turn)

        class Space(Chain):

            def __init__(self, u):
                self.u, self.x, self.w = u, xb[u][:], [w[k][u][:] for k in range(4)]
                self.var, self.root, self.newton = var[u][:], root[u][:], newton[u][:]
                self.centred, self.small, self.spread = pB[u], pC[u], pD[u]
                self.depth = 1

            def n(self, q, kind, i, sub=0):
                return q.n(kind, self.u, i, sub)

        chains = [Chain(c) for c in range(CHAINS)]
        space = [Space(u) for u in SPACES]
        one_col = lambda name: bias[:, BIASES.index(name):BIASES.index(name) + 1]
        mat = {k: mats[:, i, :] for i, k in enumerate(MATS)}
        wt = {k: wts[:, i, :] for i, k in enumerate(WEIGHTS)}

        def settle(eng):
            eng.sem_inc(s_settled, 1)

        def ready(eng, kind, u, n):
            eng.wait_ge(sig[kind][u], n + 1 + CREDIT)
            if eng is nc.sync or eng is nc.gpsimd:
                settle(eng)

        def spent(eng, kind, u, n, depth=1):
            eng.wait_ge(sig[kind][u], n + 1 - depth + CREDIT)
            if eng is nc.sync or eng is nc.gpsimd:
                settle(eng)

        def landed(eng, kind, u, n):
            eng.wait_ge(dma[kind][u], 16 * (n + 1) if isinstance(n, int) else (n + 1) * 16)
            if eng is nc.sync or eng is nc.gpsimd:
                settle(eng)

        def stored(eng, kind, u, n):
            eng.wait_ge(dma[kind][u], 16 * (n + 1) if isinstance(n, int) else (n + 1) * 16)
            if eng is nc.sync or eng is nc.gpsimd:
                settle(eng)

        def sweep(eng, blocks, body):
            if blocks >= 2:
                with eng.Fori(0, blocks // 2) as j:
                    for par in (0, 1):
                        body(j * 2 + par, par, j)
            if blocks % 2:
                body(blocks - 1, 0, blocks // 2)

        def sweep_pairs(eng, body):
            if EB >= 2:
                with eng.Fori(0, EB // 2) as j:
                    body([(c, j * 2 + c, j) for c in (0, 1)])
            if EB % 2:
                body([(0, EB - 1, EB // 2)])

        def sweep_rows(eng, body):
            n = ROWS
            if EB >= n:
                with eng.Fori(0, EB // n) as trip:
                    for k in range(n):
                        body(trip * n + k, k % 2, trip * (n // 2) + k // 2, k, trip)
            for i in range(EB // n * n, EB):
                body(i, i % 2, i // 2, i % n, i // n)

        def ahead(par, j):
            return 1 - par, j + par

        def sweep_ahead(eng, start, body, last):
            start()
            sweep(eng, EB - 1, lambda i, par, j: body(i, par, j, *ahead(par, j)))
            last(EB - 1, (EB - 1) % 2, (EB - 1) // 2)

        def col(i):
            return bass.ts(i, W)

        def blk(t, i):
            return t[:, bass.ts(i, W)]

        end_of = {"P0": ("scan", "ln"), "P1": ("scan", "l0x"), "P2": ("scan", "g"), "P3": ("g", "g"), "P4": ("scan", "g"),
                  "P5": ("scan", "hs"), "P11": ("ln", "xb"), "R11": ("scan", None), "P12": ("scan", None), "P13": (None, "oc")}
        end_of.update({k: ("scan", "hs") for k in GRU_PASSES})
        end_of["N_early"] = ("oc", "oc")

        def pass_over(eng, name):
            for u in SPACES:
                if end_of[name][u]:
                    ready(eng, end_of[name][u], u, p_[name].last(end_of[name][u], u))

        block = ctx.enter_context(nc.Block())

        @block.sync
        def _(sp):
            for kind in SIGNALS:
                for u in (0, 1):
                    if kind not in SHARED and sig[kind][u]:
                        sp.sem_inc(sig[kind][u], CREDIT)
            at = 0
            for kind in STORES:
                for x in dma[kind]:
                    sp.dma_start(prime[at:at + 1, :], ins["mats"][at:at + 1, 0, :]).then_inc(x, 16)
                    at += 1
            for t in range(T):
                part = slice(t * D, t * D + D)
                sp.dma_start(h[0][part, :].bitcast(I32), ins["dst_fm"][t:t + 1, :].to_broadcast([D, EC])).then_inc(s_bd, 16)
                sp.dma_start(h[1][part, :].bitcast(I32), ins["dst_before_fm"][t:t + 1, :].to_broadcast([D, EC])).then_inc(s_bd, 16)
            for dst, name in ((mats, "mats"), (bias[:, 0:NB_LOADED], "biases"), (wts, "weights"), (en1, "en1"), (en2, "en2"),
                              (rel_w, "rel_w"), (tv, "tv"), (etype, "etype"), (rel_id, "rel_id"),
                              (slot_row, "slot_row")):
                sp.dma_start(dst if dst is slot_row else dst[:], ins[name]).then_inc(s_const, 16)
            for k, name in (("src", "src"), ("dst", "dst"), ("row", "dst_after")):
                sp.dma_start(idx[k][:], ins[name]).then_inc(s_idx, 16)
            sp.wait_ge(s_set, 1)
            sp.dma_start(last_of.rearrange("(p n) two -> p (n two)", p=P), scan[:, 0:NODES * 2 // P]).then_inc(s_start, 16)
            sp.dma_start(table[0:1, :], scan[0:1, 0:P]).then_inc(s_start, 16)
            sp.dma_start(table4[0:1].rearrange("a t f -> a (t f)"), scan[0:1, 0:T * P]).then_inc(s_start, 16)

            def tables(name):
                q = p_[name]

                def body(i, par, j, buffer, trip):
                    ready(sp, "tab_rm", par, q.n("tab_rm", par, j))
                    sp.dma_start(table[bass.ds(i * W + 1, W), :].rearrange("(q p) f -> p q f", p=P),
                                 tab_out[buffer][:].rearrange("p (q f) -> p q f", q=Q)).then_inc(dma["st_tab"][buffer], 16)
                sweep_rows(sp, body)
                for b in range(ROWS):
                    stored(sp, "st_tab", b, q.last("st_tab", b) + 1)
                sp.sem_inc(s_table, 1)

            def d_rows(name, i, par, j):
                q = p_[name]
                spent(sp, "head", D_, q.n("head", D_, i), 2)
                sp.dma_start(G[par][D_].rearrange("p (q f) -> p q f", q=Q),
                             table[bass.ds(i * W + 1, W), :].rearrange("(q p) f -> p q f", p=P)
                             ).then_inc(dma["ld_gd"][par], 16)

            def gru_io(name):
                def tiles(i, par, j):
                    edge_matrices(p_[name], i)

                def body(i, par, j, par1, j1):
                    d_rows(name, i + 1, par1, j1)
                    tiles(i, par, j)
                sweep_ahead(sp, lambda: d_rows(name, 0, 0, 0), body, tiles)

            def edge_matrices(q, i):
                for k in range(TILES):
                    spent(sp, "rd", S_, q.n("rd", S_, i, k), RING)
                    sp.dma_start(ring[k % RING][:], net[bass.ds(i * TILES + k, 1), :, :].rearrange("a p f -> p (a f)")
                                 ).then_inc(dma["ld_w"][k % RING], 16)

            def pass_io(name, x_load=(), x_store=(), x_kind="xb", d_load=(), tiles=False):
                q = p_[name]

                def body(i, par, j):
                    d_rows(name, i, par, j)
                    for u in x_load:
                        spent(sp, end_of[name][u], u, q.n(end_of[name][u], u, i))
                        if u in x_store:
                            stored(sp, "st_x", u, q.n("st_x", u, i))
                        sp.dma_start(xb[u][:], x_sp[u, :, col(i)]).then_inc(dma["ld_x"][u], 16)
                    for u in d_load:
                        spent(sp, end_of[name][u], u, q.n(end_of[name][u], u, i))
                        sp.dma_start(db[u][:], d_sp[u, :, col(i)]).then_inc(dma["ld_d"][u], 16)
                    for u in x_store:
                        ready(sp, x_kind, u, q.n(x_kind, u, i))
                        sp.dma_start(x_sp[u, :, col(i)], xb[u][:]).then_inc(dma["st_x"][u], 16)
                    if tiles:
                        edge_matrices(q, i)
                sweep(sp, EB, body)
                for u in x_store:
                    stored(sp, "st_x", u, q.last("st_x", u) + 1)

            def nodes(name, first, groups):
                q = p_[name]
                with sp.Fori(0, groups) as i:
                    for c, b in enumerate(chains):
                        spent(sp, "head", b.u, b.n(q, "head", i), 2)
                        sp.dma_start(b.g.rearrange("p (q f) -> p q f", q=Q),
                                     ins["x"][bass.ds(i * (CHAINS * W) + (first * CHAINS + c) * W, W), :]
                                     .rearrange("(p q) f -> p q f", q=Q)).then_inc(dma["ld_n"][c], 16)
                    for c, b in enumerate(chains):
                        ready(sp, "oc", b.u, b.n(q, "oc", i))
                        sp.dma_start(out[bass.ds(i * (CHAINS * W) + (first * CHAINS + c) * W, W), :]
                                     .rearrange("(p q) f -> p q f", q=Q),
                                     b.out.rearrange("p (q f) -> p q f", q=Q)).then_inc(dma["st_out"][c], 16)

            q = p_["T_setup"]

            def body(i, par, j):
                ready(sp, "deg_r", par, q.n("deg_r", par, j))
                sp.dma_start(d_sp[D_, :, col(i)], w[1][par][:]).then_inc(dma["st_d"][par], 16)
            sweep(sp, EB, body)
            sp.wait_ge(s_set, 3)
            nodes("N_early", 0, EARLY)
            q2 = p_["ENDS"]

            def body(i, par, j):
                ready(sp, "ends_d", par, q2.n("ends_d", par, j))
                sp.dma_start(d_sp[S_, :, col(i)], w[1][par][:]).then_inc(dma["st_d"][par], 16)
            sweep(sp, EB, body)
            for par in (0, 1):
                stored(sp, "st_d", par, q2.last("st_d", par) + 1)

            q, q2 = p_["P0"], p_["WE"]

            def body(i, par, j, q=q, q2=q2):
                for u in (0, 1):
                    spent(sp, "ehp", u, q2.n("ehp", u, i, 0))
                sp.dma_start(attr_in, ins["edge_attr_T"].rearrange("d (t e) -> d t e", t=T)[:, :, col(i)]
                             ).then_inc(dma["ld_ea"][0], 16)
                for u in SPACES:
                    ready(sp, "xb", u, q.n("xb", u, i))
                    sp.dma_start(x_sp[u, :, col(i)], xb[u][:]).then_inc(dma["st_x"][u], 16)
                for t in range(T):
                    for k in range(Q):
                        b, k2 = k % 2, k // 2
                        ready(sp, "weo", b, q2.n("weo", b, i, 2 * t + k2))
                        sp.dma_start(net[bass.ds(i * TILES + (k * T + t), 1), :, :].rearrange("a p f -> p (a f)"),
                                     ring[2 * b + k2]).then_inc(dma["st_we"][2 * b + k2], 16)
            sweep(sp, EB, body)
            for u in SPACES:
                stored(sp, "st_x", u, q.last("st_x", u) + 1)
            for k in range(RING):
                stored(sp, "st_we", k, EB * TILES // RING)
            tables("T0")
            pass_io("P1", x_load=SPACES, x_store=SPACES, x_kind="l0x")
            tables("T1")
            pass_io("P2", x_load=SPACES, x_store=SPACES, d_load=SPACES)
            tables("T2")
            pass_io("P3", d_load=SPACES)

            pass_over(sp, "P3")
            q = p_["T3"]
            for t in range(T):
                def body(i, par, j, t=t):
                    ready(sp, "b4", par, q.n("b4", par, j, t * halves(EB)[par]))
                    sp.dma_start(table4[bass.ds(i * W + 1, W), t, :].rearrange("(q p) f -> p q f", p=P),
                                 w[4][par][:].rearrange("p (q f) -> p q f", q=Q)).then_inc(dma["st_tab4"][par], 16)
                sweep(sp, EB, body)
            for par in (0, 1):
                stored(sp, "st_tab4", par, q.last("st_tab4", par) + 1)
            sp.sem_inc(s_table, 1)

            q = p_["P4"]

            def body(i, par, j):
                for u in SPACES:
                    spent(sp, "g", u, q.n("g", u, i))
                    sp.dma_start(db[u][:], d_sp[u, :, col(i)]).then_inc(dma["ld_d"][u], 16)
                for t in range(T):
                    spent(sp, "q_head", D_, q.n("q_head", D_, i, t), 2)
                    sp.dma_start(G[t % 2][D_].rearrange("p (q f) -> p q f", q=Q),
                                 table4[bass.ds(i * W + 1, W), t, :].rearrange("(q p) f -> p q f", p=P)
                                 ).then_inc(dma["ld_gd"][t % 2], 16)
            sweep(sp, EB, body)
            tables("T4")

            pass_io("P5", x_load=SPACES, x_store=SPACES, d_load=SPACES, tiles=True)
            tables("T5")
            for k, name in enumerate(GRU_PASSES):
                gru_io(name)
                tables(f"T{6 + k}")
            pass_io("P11", x_load=SPACES, x_store=(D_,))
            tables("T11")
            tables("T12")

            pass_over(sp, "P12")
            nodes("N", EARLY, NP - EARLY)
            for c in range(CHAINS):
                stored(sp, "st_out", c, NP)
            sp.sem_inc(s_nodes, 1)

            pass_io("P13", x_load=(D_,))

        @block.gpsimd
        def _(pool):
            slots = [0]

            def fetch(i, index, dst, rows, dests, done, base, per, sub):
                nc.gpsimd.tensor_copy(dst[:], index[:, bass.ds(i * TILES, TILES)]).then_inc(s_slot, 1)
                pool.wait_ge(s_slot, i * per + (base + sub + 1))
                settle(pool)
                for k in range(TILES):
                    pool.indirect_dma_start(dests(k), None, rows, bass.IndirectOffsetOnAxis(ap=dst[:, k:k + 1], axis=0)
                                            ).then_inc(done, 16)

            q = p_["T_setup"]
            pool.wait_ge(s_set, 18)
            pool.wait_ge(s_start, 48)

            def body(i, par, j):
                ready(pool, "tab_rm", par, q.n("tab_rm", par, j))
                nc.gpsimd.tensor_copy(slot[par][:], idx["run_end"][:, bass.ds(i * TILES, TILES)]).then_inc(s_slot, 1)
                nc.gpsimd.tensor_copy(pair_slot[par][:], ends[:, bass.ds(i * TILES, TILES), :]).then_inc(s_slot, 1)
                pool.wait_ge(s_slot, i * 2 + 2)
                settle(pool)
                for k in range(TILES):
                    pool.indirect_dma_start(last_of, bass.IndirectOffsetOnAxis(ap=slot[par][:, k:k + 1], axis=0),
                                            pair_slot[par][:, k, :], None, bounds_check=NODES - 1, oob_is_err=False
                                            ).then_inc(s_sc[par], 16)
                pool.wait_ge(s_sc[par], (j + 1) * (16 * TILES))
                settle(pool)
            sweep(pool, EB, body)
            slots[0] = 2 * EB

            def keep_pairs(i, par, j):
                pool.wait_ge(s_tg[par], (j + 1) * (16 * TILES))
                settle(pool)
                nc.gpsimd.tensor_copy(src_ends[:, bass.ds(i * TILES, TILES), :], pair_slot[par][:]).then_inc(s_pairs, 1)

            def body(i, par, j, par1, j1):
                fetch_pairs(i + 1, par1, j1)
                keep_pairs(i, par, j)

            def fetch_pairs(i, par, j):
                pool.wait_ge(s_pairs, i + 1)
                settle(pool)
                fetch(i, idx["src"], slot[par], last_of, lambda k: pair_slot[par][:, k, :], s_tg[par], slots[0], 1, 0)
            pool.sem_inc(s_pairs, 2)
            sweep_ahead(pool, lambda: fetch_pairs(0, 0, 0), body, keep_pairs)
            slots[0] += EB

            for par in (0, 1):
                pool.wait_ge(s_tg[par], halves(EB)[par] * (16 * TILES))
            q3 = p_["P0"]
            x_rows = ins["x"].rearrange("r (t f) -> (r t) f", t=T)

            def body(i, par, j):
                for u, name in ((S_, "src"), (D_, "dst")):
                    spent(pool, "head", u, q3.n("head", u, i), 2)
                    fetch(i, idx[name], (slot if u == S_ else slot_d)[par], x_rows,
                          lambda k: G[par][u][:, k * D:k * D + D], dma["ld_g0"][2 * u + par], slots[0], 2, u)
            sweep(pool, EB, body)
            slots[0] += 2 * EB

            def gather(name, tables_before):
                q = p_[name]
                pool.wait_ge(s_table, tables_before)

                def body(i, par, j):
                    if name == "P12":
                        spent(pool, "head", par, q.n("head", par, j))
                    else:
                        spent(pool, "head", S_, q.n("head", S_, i), 2)
                    fetch(i, idx["row"], slot[par], table.rearrange("r (t f) -> (r t) f", t=T),
                          lambda k: G[par][S_][:, k * D:k * D + D], dma["ld_gs"][par], slots[0], 1, 0)
                sweep(pool, EB, body)
                slots[0] += EB

            for k in (1, 2, 3):
                gather(f"P{k}", k)

            pass_over(pool, "P3")
            q3 = p_["T3"]
            for t in range(T):
                def body(i, par, j, t=t):
                    spent(pool, "bd", par, q3.n("bd", par, j, t * halves(EB)[par]))
                    pool.dma_start(db[par][:], d_sp[S_, :, col(i)]).then_inc(dma["ld_d4"][par], 16)
                sweep(pool, EB, body)
            q4 = p_["P4"]
            pool.wait_ge(s_table, 4)

            def body(i, par, j):
                spent(pool, "q_head", S_, q4.n("q_head", S_, i), 2)
                nc.gpsimd.tensor_copy(slot[par][:], idx["row"][:, bass.ds(i * TILES, TILES)]).then_inc(s_slot, 1)
                pool.wait_ge(s_slot, i + (slots[0] + 1))
                settle(pool)
                for t in range(T):
                    spent(pool, "q_head", S_, q4.n("q_head", S_, i, t), 2)
                    for k in range(Q):
                        pool.indirect_dma_start(
                            G[t % 2][S_][:, k * P:k * P + P], None, table4.rearrange("r t f -> (r t) f"),
                            bass.IndirectOffsetOnAxis(ap=slot[par][:, k * T + t:k * T + t + 1], axis=0)
                        ).then_inc(dma["ld_g4"][t % 2], 16)
            sweep(pool, EB, body)
            slots[0] += EB
            for k in range(5, 13):
                gather(f"P{k}", k)

            q5 = p_["P13"]
            pool.wait_ge(s_nodes, 1)

            def body(i, par, j):
                nc.gpsimd.tensor_copy(slot[par][:], idx["run_end"][:, bass.ds(i * TILES, TILES)]).then_inc(s_slot, 1)
                pool.wait_ge(s_slot, i + (slots[0] + 1))
                settle(pool)
                ready(pool, "oc", D_, q5.n("oc", D_, i))
                for k in range(TILES):
                    pool.indirect_dma_start(out.rearrange("r (t f) -> (r t) f", t=T),
                                            bass.IndirectOffsetOnAxis(ap=slot[par][:, k:k + 1], axis=0),
                                            db[D_][:, k * D:k * D + D], None, bounds_check=NODES - 1, oob_is_err=False
                                            ).then_inc(s_scat, 16)
                pool.wait_ge(s_scat, (i + 1) * (16 * TILES))
                settle(pool)
                pool.sem_inc(sig["scattered"][D_], 1)
            sweep(pool, EB, body)

        @block.tensor
        def _(pe):
            mm = nc.tensor.matmul

            def turn(dst, src):
                for k in range(Q):
                    last = nc.tensor.transpose(dst[:, k * P:k * P + P], src[:, k * P:k * P + P], mat["ident"])
                return last

            def centre(q, b, i, sub=0):
                ready(pe, "xb", b.u, b.n(q, "xb", i, sub))
                mm(b.centred, mat["center"], b.x, start=True, stop=True).then_inc(sig["ln_c"][b.u], 1)

            def variances(q, b, i, sub=0):
                ready(pe, "ln_sq", b.u, b.n(q, "ln_sq", i, sub))
                for k in range(Q):
                    last = mm(b.small[:, k * T:k * T + T], b.w[0][:, k * P:k * P + P], member_mean, start=True, stop=True)
                last.then_inc(sig["ln_v"][b.u], 1)

            def scales(q, b, i, sub=0):
                ready(pe, "ln_r", b.u, b.n(q, "ln_r", i, sub))
                turn(b.spread, b.w[2]).then_inc(sig["ln_t"][b.u], 1)

            def layer_norm(q, bs, i, sub=0):
                for stage in (centre, variances, scales):
                    for b in bs:
                        stage(q, b, i, sub)

            def head(q, u, i, par, j, load, ends):
                landed_n(pe, load, par, q, i, j)
                spent(pe, ends, u, q.n(ends, u, i))
                turn(pA[u], G[par][u]).then_inc(sig["head"][u], 1)

            def landed_n(eng, load, par, q, i, j):
                if load == "ld_gs":
                    eng.wait_ge(dma[load][par], (q.n(load, par, j) + 1) * (16 * TILES))
                else:
                    landed(eng, load, par, q.n(load, par, j))

            def gru(q, u, i, state):
                mm(pD[u], wt["hn"], state, start=True, stop=True).then_inc(sig["ghn"][u], 1)
                mm(pB[u], wt["hr"], state, start=True, stop=False)
                ready(pe, "m", u, q.n("m", u, i))
                mm(pB[u], wt["ir"], w[0][u][:], start=False, stop=True).then_inc(sig["gr"][u], 1)
                mm(pC[u], wt["hz"], state, start=True, stop=False)
                mm(pC[u], wt["iz"], w[0][u][:], start=False, stop=True).then_inc(sig["gz"][u], 1)
                mm(pA[u], wt["in"], w[0][u][:], start=True, stop=True).then_inc(sig["gin"][u], 1)

            def to_rows(q, i, kind, src):
                ready(pe, kind, S_, q.n(kind, S_, i))
                turn(pB[S_], src).then_inc(sig["mt"][S_], 1)

            def edge_messages(q, i):
                to_rows(q, i, "hn", hn[S_])
                mm(pC[S_], wt["en2b"], hn[S_], start=True, stop=False)
                ready(pe, "rd", S_, q.n("rd", S_, i, TILES - 1))
                for k in range(Q):
                    last = mm(pC[S_][:, k * P:k * P + P], msg_rows[:, k * P:k * P + P], mat["ident"],
                              start=False, stop=(k == Q - 1))
                last.then_inc(sig["mf"][S_], 1)

            def relation_messages(q, blocks, layer):
                for c, i, j in blocks:
                    ready(pe, "th", c, q.n("th", c, j))
                    spent(pe, "scan", S_, q.n("scan", S_, i), 2)
                    turn(pB[c], hb[c]).then_inc(sig["mt"][c], 1)
                for c, i, j in blocks:
                    ready(pe, "ob", c, q.n("ob", c, j))
                    turn(pC[c], w[2][c]).then_inc(sig["obt"][c], 1)
                for g in range(Q + 1):
                    for c, i, j in blocks:
                        if g < Q:
                            ready(pe, "zz", c, q.n("zz", c, j, g))
                            if g == 1:
                                ready(pe, "obc", c, q.n("obc", c, j))
                            spent(pe, "ztc", c, q.n("ztc", c, j, g), 2)
                            turn((pB, pC)[g % 2][c], Z[c][g % 2]).then_inc(sig["zt"][c], 1)
                    for c, i, j in blocks:
                        if g:
                            ready(pe, "ztc", c, q.n("ztc", c, j, g - 1))
                            for half, bank in enumerate((pD, pA)):
                                spent(pe, "rgm", c, q.n("rgm", c, j, 2 * (g - 1) + half), 2)
                                for t in (0, 1):
                                    at = (2 * half + t) * P
                                    last = mm(bank[c][:, t * D * R:(t + 1) * D * R], ZT[c][(g - 1) % 2][:, at:at + P],
                                              rel_w[:, layer, :], start=True, stop=True)
                                last.then_inc(sig["rg"][c], 1)
                for c, i, j in blocks:
                    ready(pe, "rgm", c, q.n("rgm", c, j, 2 * Q - 1))
                    mm(pA[c], wt[f"rel_b{layer}"], w[1][c][:], start=True, stop=False)
                    ready(pe, "rd", c, q.n("rd", c, j, 2 * Q - 1))
                    for k in range(Q):
                        last = mm(pA[c][:, k * P:k * P + P], w[4][c][:, k * P:k * P + P], mat["ident"],
                                  start=False, stop=(k == Q - 1))
                    last.then_inc(sig["mf"][c], 1)

            def tables(name, after):
                q = p_[name]
                if after:
                    pass_over(pe, after)
                mm(pA[0][:, 0:1], carry_mat[:], scan[:, EC:EC + 1], start=True, stop=True).then_inc(sig["tab_end"][0], 1)

                def body(i, par, j):
                    ready(pe, "tab_sum", par, q.n("tab_sum", par, j))
                    spent(pe, "tab_rm", par, q.n("tab_rm", par, j))
                    turn(pD[par], tab_in[par]).then_inc(sig["tab_t"][par], 1)
                sweep(pe, EB, body)

            def nodes(name, first, groups):
                q = p_[name]
                with pe.Fori(0, groups) as i:
                    for c, b in enumerate(chains):
                        landed(pe, "ld_n", c, i + first)
                        spent(pe, "oc", b.u, b.n(q, "oc", i), 2)
                        turn(b.a, b.g).then_inc(sig["head"][b.u], 1)
                    layer_norm(q, chains, i, 0)
                    for b in chains:
                        ready(pe, "ln", b.u, b.n(q, "ln", i, 0))
                        mm(b.a, wt["l0_r0"], b.h, start=True, stop=True).then_inc(sig["l0a"][b.u], 1)
                        mm(b.b, wt["l0_r1"], b.h, start=True, stop=True).then_inc(sig["l0b"][b.u], 1)
                    for b in chains:
                        ready(pe, "l0ra", b.u, b.n(q, "l0ra", i))
                        ready(pe, "l0rb", b.u, b.n(q, "l0rb", i))
                        mm(b.a, wt["l0_or0"], b.w[1], start=True, stop=False)
                        mm(b.a, wt["l0_or1"], b.w[2], start=False, stop=True).then_inc(sig["l0x_mm"][b.u], 1)
                    layer_norm(q, chains, i, 1)
                    for t in range(T):
                        for b in chains:
                            if t == 0:
                                ready(pe, "ln", b.u, b.n(q, "ln", i, 1))
                            mm(b.a, wt[f"w1_{t}"], b.h, start=True, stop=True).then_inc(sig["q1"][b.u], 1)
                        for b in chains:
                            ready(pe, "q1r", b.u, b.n(q, "q1r", i, t))
                            mm(b.a, wt["w2"], b.w[1], start=True, stop=True).then_inc(sig["q5"][b.u], 1)
                        for b in chains:
                            ready(pe, "q6", b.u, b.n(q, "q6", i, t))
                            mm(b.b, wt[f"w3_{t}"], b.w[2], start=(t == 0), stop=(t == T - 1)).then_inc(sig["q7"][b.u], 1)
                    layer_norm(q, chains, i, 2)
                    for b in chains:
                        ready(pe, "ln", b.u, b.n(q, "ln", i, 2))
                        mm(b.a, wt["lin0"], b.h, start=True, stop=True).then_inc(sig["lin"][b.u], 1)
                    for k in range(STEPS):
                        for b in chains:
                            ready(pe, "hn", b.u, b.n(q, "hn", i, k))
                            mm(b.a, wt["hr"], b.new, start=True, stop=True).then_inc(sig["gr"][b.u], 1)
                            mm(b.b, wt["hz"], b.new, start=True, stop=True).then_inc(sig["gz"][b.u], 1)
                        for b in chains:
                            ready(pe, "r", b.u, b.n(q, "r", i, k))
                            mm(b.a, wt["hn"], b.new, start=True, stop=True).then_inc(sig["ghn"][b.u], 1)
                    for b in chains:
                        ready(pe, "of", b.u, b.n(q, "of", i))
                        turn(b.a, b.w[0]).then_inc(sig["ot"][b.u], 1)

            pe.wait_ge(s_const, 16 * 10)
            pe.wait_ge(s_set, 5)
            mm(pA[0][:, 0:P], mat["prev_quarter"], w[0][0][:, 0:P], start=True, stop=True).then_inc(s_pset, 1)
            pe.wait_ge(s_set, 6)
            mm(pB[0][:, 0:P], mat["prev_quarter"], w[1][0][:, 0:P], start=True, stop=True).then_inc(s_pset, 1)
            pe.wait_ge(s_set, 10)
            for k, name in enumerate(("ir", "iz", "in")):
                mm(pC[0][:, k:k + 1], wt[name], w[2][0][:, 0:1], start=True, stop=True).then_inc(s_pset, 1)
            pe.wait_ge(s_set, 18)
            tables("T_setup", None)
            for par in (0, 1):
                ready(pe, "tab_rm", par, p_["T_setup"].last("tab_rm", par))
            nodes("N_early", 0, EARLY)
            pass_over(pe, "N_early")
            q = p_["ENDS"]

            def body(i, par, j):
                ready(pe, "ends_bc", par, q.n("ends_bc", par, j))
                spent(pe, "ends_d", par, q.n("ends_d", par, j))
                turn(pA[par], w[0][par]).then_inc(sig["ends_t"][par], 1)
            sweep(pe, EB, body)

            for par in (0, 1):
                ready(pe, "ends_d", par, q.last("ends_d", par))
            q = p_["P0"]

            def body(i, par, j, q=q, q2=p_["WE"]):
                for u in SPACES:
                    spent(pe, "weo", u, q2.n("weo", u, i))
                for u in SPACES:
                    pe.wait_ge(dma["ld_g0"][2 * u + par], (j + 1) * (16 * TILES))
                    spent(pe, end_of["P0"][u], u, q.n(end_of["P0"][u], u, i))
                    turn(pA[u], G[par][u]).then_inc(sig["head"][u], 1)
                layer_norm(q, space, i)
                ready(pe, "scan", S_, q.n("scan", S_, i))
                ready(pe, "ln", D_, q.n("ln", D_, i))
                landed(pe, "ld_ea", 0, q2.n("ld_ea", 0, i))

                def hidden(t):
                    mm(pA[t % 2], en1[:], attr_in[:, t, :], start=True, stop=True).then_inc(sig["ehp"][t % 2], 1)
                hidden(0)
                for t in range(T):
                    if t + 1 < T:
                        hidden(t + 1)
                    ready(pe, "eh", t % 2, q2.n("eh", t % 2, i, t // 2))
                    for k in range(Q):
                        b = k % 2
                        spent(pe, "weo", b, q2.n("weo", b, i, 2 * t + k // 2))
                        lhs = w[0][t % 2][:, k * P:k * P + P]
                        mm(pB[b], lhs, en2[:, 0:W], start=True, stop=True)
                        mm(pC[b], lhs, en2[:, W:2 * W], start=True, stop=True).then_inc(sig["wep"][b], 1)
            sweep(pe, EB, body)
            tables("T0", "P0")

            q = p_["P1"]

            def sage(q, u, i, state, messages):
                for k, (dst, kind) in enumerate(((pB, "l0a"), (pC, "l0b"))):
                    mm(dst[u], wt[f"l0_l{k}"], w[0][u][:], start=True, stop=False)
                    mm(dst[u], wt[f"l0_r{k}"], state, start=False, stop=True).then_inc(sig[kind][u], 1)
                ready(pe, "l0ra", u, q.n("l0ra", u, i))
                ready(pe, "l0rb", u, q.n("l0rb", u, i))
                if messages:
                    mm(pA[u], wt["l0_ol0"], w[1][u][:], start=True, stop=False)
                    mm(pA[u], wt["l0_ol1"], w[2][u][:], start=False, stop=True).then_inc(sig["l0y"][u], 1)
                mm(pD[u], wt["l0_or0"], w[1][u][:], start=True, stop=False)
                mm(pD[u], wt["l0_or1"], w[2][u][:], start=False, stop=True).then_inc(sig["l0x_mm"][u], 1)

            def body(i, par, j, q=q):
                for u in SPACES:
                    head(q, u, i, par, j, ("ld_gs", "ld_gd")[u], end_of["P1"][u])
                for u in SPACES:
                    ready(pe, "agg", u, q.n("agg", u, i))
                    sage(q, u, i, blk(h[u], i), u == S_)
            sweep(pe, EB, body)
            tables("T1", "P1")

            q = p_["P2"]

            def body(i, par, j, q=q):
                for u in SPACES:
                    head(q, u, i, par, j, ("ld_gs", "ld_gd")[u], end_of["P2"][u])
                layer_norm(q, space, i)
            sweep(pe, EB, body)
            tables("T2", "P2")

            q = p_["P3"]

            def body(i, par, j, q=q):
                for u in SPACES:
                    head(q, u, i, par, j, ("ld_gs", "ld_gd")[u], end_of["P3"][u])
            sweep(pe, EB, body)
            pass_over(pe, "P3")

            q = p_["T3"]
            for t in range(T):
                def products(i, par, j, t=t, q=q):
                    spent(pe, "b4", par, q.n("b4", par, j, t * halves(EB)[par]))
                    mm(pA[par], wt[f"w1_{t}"], blk(h[S_], i), start=True, stop=True).then_inc(sig["b1"][par], 1)
                    landed(pe, "ld_d4", par, q.n("ld_d4", par, j, t * halves(EB)[par]))
                    mm(pB[par], mat[f"spread{t}"], db[par][:], start=True, stop=True
                       ).then_inc(sig["bd"][par], 1)
                    mm(pC[par], spread_bf[:, t, :], blk(keep, i), start=True, stop=True
                       ).then_inc(sig["bk"][par], 1)

                def sums(i, par, j, t=t, q=q):
                    ready(pe, "b3", par, q.n("b3", par, j, t * halves(EB)[par]))
                    turn(pD[par], w[3][par]).then_inc(sig["b3t"][par], 1)

                def body(i, par, j, par1, j1):
                    products(i + 1, par1, j1)
                    sums(i, par, j)
                sweep_ahead(pe, lambda: products(0, 0, 0), body, sums)
            for par in (0, 1):
                ready(pe, "b4", par, q.last("b4", par))

            q = p_["P4"]

            def body(i, par, j, q=q):
                def rows(u, t):
                    if u == S_:
                        pe.wait_ge(dma["ld_g4"][t % 2], (i * 2 + (t // 2 + 1)) * (16 * Q))
                    else:
                        landed(pe, "ld_gd", t % 2, q.n("ld_gd", t % 2, i, t // 2))
                    spent(pe, "q3", u, q.n("q3", u, i, t))
                    turn(pA[u], G[t % 2][u]).then_inc(sig["q_head"][u], 1)
                    spent(pe, "q6", u, q.n("q6", u, i, t))
                    mm(pB[u], wt[f"w1_{t}"], blk(h[u], i), start=True, stop=True).then_inc(sig["q1"][u], 1)

                def degrees(u, t):
                    spent(pe, "q4", u, q.n("q4", u, i, t))
                    landed(pe, "ld_d", u, q.n("ld_d", u, i))
                    mm(pC[u], mat[f"spread{t}"], db[u][:], start=True, stop=True).then_inc(sig["qd"][u], 1)

                def second(u, t):
                    ready(pe, "q4", u, q.n("q4", u, i, t))
                    mm(pB[u], wt["w2"], w[2][u][:], start=True, stop=True).then_inc(sig["q5"][u], 1)

                def third(u, t):
                    ready(pe, "q6", u, q.n("q6", u, i, t))
                    if t == 0:
                        spent(pe, "g", u, q.n("g", u, i))
                    mm(pD[u], wt[f"w3_{t}"], w[3][u][:], start=(t == 0), stop=(t == T - 1)
                       ).then_inc(sig["q7"][u], 1)

                for t in range(T + 1):
                    if t < T:
                        rows(S_, t)
                    if t:
                        second(D_, t - 1)
                    if t < T:
                        degrees(S_, t)
                    if t:
                        third(D_, t - 1)
                    if t < T:
                        rows(D_, t)
                        second(S_, t)
                        degrees(D_, t)
                        third(S_, t)
            sweep(pe, EB, body)
            tables("T4", "P4")

            q = p_["P5"]

            def body(i, par, j, q=q):
                for u in SPACES:
                    head(q, u, i, par, j, ("ld_gs", "ld_gd")[u], end_of["P5"][u])
                layer_norm(q, space, i)
                for u in SPACES:
                    ready(pe, "ln", u, q.n("ln", u, i))
                    mm(pD[u], wt["lin0"], hb[u], start=True, stop=True).then_inc(sig["lin"][u], 1)
                edge_messages(q, i)
            sweep(pe, EB, body)
            tables("T5", "P5")

            for k, name in enumerate(GRU_PASSES):
                q = p_[name]

                def step(i, par, j, q=q):
                    for u in SPACES:
                        head(q, u, i, par, j, ("ld_gs", "ld_gd")[u], "hs")
                        if u == S_:
                            spent(pe, "scan", u, q.n("scan", u, i), 2)
                            spent(pe, "hrm", u, q.n("hrm", u, i))
                        gru(q, u, i, blk(h[u], i))
                    to_rows(q, i, "hn", hn[S_])

                def messages(i, par, j, q=q):
                    ready(pe, "hs", S_, q.n("hs", S_, i))
                    ready(pe, "rd", S_, q.n("rd", S_, i, TILES - 1))
                    mm(pC[S_], wt["en2b"], blk(h[S_], i), start=True, stop=False)
                    for k in range(Q):
                        last = mm(pC[S_][:, k * P:k * P + P], sum_rows[par][:, k * P:k * P + P], mat["ident"],
                                  start=False, stop=(k == Q - 1))
                    last.then_inc(sig["mf"][S_], 1)

                def body(i, par, j, par1, j1):
                    step(i + 1, par1, j1)
                    messages(i, par, j)
                sweep_ahead(pe, lambda: step(0, 0, 0), body, messages)
                tables(f"T{6 + k}", name)

            q = p_["P11"]

            def body(i, par, j, q=q):
                for u in SPACES:
                    head(q, u, i, par, j, ("ld_gs", "ld_gd")[u], end_of["P11"][u])
                    gru(q, u, i, blk(h[u], i))
                layer_norm(q, space[:1], i)
            sweep(pe, EB, body)

            pass_over(pe, "P11")
            sweep_pairs(pe, lambda blocks: relation_messages(p_["R11"], blocks, 0))
            tables("T11", "R11")

            def body(blocks, q=p_["P12"]):
                for c, i, j in blocks:
                    landed_n(pe, "ld_gs", c, q, i, j)
                    spent(pe, "scan", S_, q.n("scan", S_, i), 2)
                    turn(pA[c], G[c][S_]).then_inc(sig["head"][c], 1)
                relation_messages(q, blocks, 1)
            sweep_pairs(pe, body)
            tables("T12", "P12")

            for par in (0, 1):
                ready(pe, "tab_rm", par, p_["T12"].last("tab_rm", par))
            nodes("N", EARLY, NP - EARLY)

            q = p_["P13"]

            def body(i, par, j, q=q):
                head(q, D_, i, par, j, "ld_gd", "oc")
                ready(pe, "of", D_, q.n("of", D_, i))
                turn(pB[D_], w[0][D_]).then_inc(sig["ot"][D_], 1)
            sweep(pe, EB, body)

        @block.scalar
        def _(act):
            f = nc.scalar.activation

            def layer_norm(q, bs, i, sub=0):
                for b in bs:
                    ready(act, "ln_c", b.u, b.n(q, "ln_c", i, sub))
                    f(b.w[0], b.centred, ACT.Square).then_inc(sig["ln_sq"][b.u], 1)
                    f(b.w[1], b.centred, ACT.Relu).then_inc(sig["ln_relu"][b.u], 1)
                for b in bs:
                    ready(act, "ln_s", b.u, b.n(q, "ln_s", i, sub))
                    f(b.root, b.var, ACT.Sqrt).then_inc(sig["ln_sd"][b.u], 1)

            def tables(name):
                q = p_[name]

                def body(i, par, j, buffer, trip):
                    ready(act, "tab_t", par, q.n("tab_t", par, j))
                    stored(act, "st_tab", buffer, q.n("st_tab", buffer, trip))
                    f(tab_out[buffer][:], pD[par], ACT.Copy).then_inc(sig["tab_rm"][par], 1)
                sweep_rows(act, body)

            def sage(q, u, i):
                for k, (src, dst, kind, out_kind) in enumerate(((pB, w[1], "l0a", "l0ra"), (pC, w[2], "l0b", "l0rb"))):
                    ready(act, kind, u, q.n(kind, u, i))
                    f(dst[u][:], src[u], ACT.Relu, bias=one_col("b_in")).then_inc(sig[out_kind][u], 1)

            def gru(q, u, i):
                ready(act, "gr", u, q.n("gr", u, i))
                f(w[1][u][:], pB[u], ACT.Sigmoid, bias=one_col("r")).then_inc(sig["r"][u], 1)
                ready(act, "gz", u, q.n("gz", u, i))
                f(w[2][u][:], pC[u], ACT.Sigmoid, bias=one_col("z")).then_inc(sig["z"][u], 1)

            def gru_new(q, u, i):
                ready(act, "npre", u, q.n("npre", u, i))
                f(w[1][u][:], w[4][u][:], ACT.Tanh, bias=one_col("in")).then_inc(sig["n"][u], 1)

            def rows(q, i):
                ready(act, "mt", S_, q.n("mt", S_, i))
                f(h_rows[:], pB[S_], ACT.Copy).then_inc(sig["hrm"][S_], 1)

            def relation(q, blocks):
                for c, i, j in blocks:
                    ready(act, "mt", c, q.n("mt", c, j))
                    f(w[3][c][:], pB[c], ACT.Copy).then_inc(sig["hrm"][c], 1)
                for c, i, j in blocks:
                    ready(act, "obt", c, q.n("obt", c, j))
                    f(w[1][c][:], pC[c], ACT.Copy).then_inc(sig["obc"][c], 1)
                for g in range(Q):
                    for c, i, j in blocks:
                        ready(act, "zt", c, q.n("zt", c, j, g))
                        spent(act, "rg", c, q.n("rg", c, j, 2 * g), 3)
                        f(ZT[c][g % 2], (pB, pC)[g % 2][c], ACT.Copy).then_inc(sig["ztc"][c], 1)

            def nodes(name, first, groups):
                q = p_[name]
                with act.Fori(0, groups) as i:
                    for b in chains:
                        ready(act, "head", b.u, b.n(q, "head", i))
                        f(b.x, b.a, ACT.Copy).then_inc(sig["xb"][b.u], 1)
                    layer_norm(q, chains, i, 0)
                    for b in chains:
                        ready(act, "l0a", b.u, b.n(q, "l0a", i))
                        f(b.w[1], b.a, ACT.Relu, bias=one_col("b_in")).then_inc(sig["l0ra"][b.u], 1)
                        ready(act, "l0b", b.u, b.n(q, "l0b", i))
                        f(b.w[2], b.b, ACT.Relu, bias=one_col("b_in")).then_inc(sig["l0rb"][b.u], 1)
                    layer_norm(q, chains, i, 1)
                    for t in range(T):
                        for b in chains:
                            ready(act, "q1", b.u, b.n(q, "q1", i, t))
                            f(b.w[1], b.a, ACT.Relu, bias=one_col("b1")).then_inc(sig["q1r"][b.u], 1)
                        for b in chains:
                            ready(act, "q5", b.u, b.n(q, "q5", i, t))
                            spent(act, "q7", b.u, b.n(q, "q7", i, t), 2)
                            f(b.w[2], b.a, ACT.Relu, bias=one_col("b2")).then_inc(sig["q6"][b.u], 1)
                    for b in chains:
                        ready(act, "q7", b.u, b.n(q, "q7", i, T - 1))
                        f(b.w[1], b.b, ACT.Relu, bias=one_col("b3")).then_inc(sig["c5r"][b.u], 1)
                    layer_norm(q, chains, i, 2)
                    for b in chains:
                        ready(act, "lin", b.u, b.n(q, "lin", i))
                        f(b.new, b.a, ACT.Relu, bias=one_col("lin0_b")).then_inc(sig["hn"][b.u], 1)
                    for k in range(STEPS):
                        for b in chains:
                            ready(act, "gr", b.u, b.n(q, "gr", i, k))
                            f(b.w[1], b.a, ACT.Sigmoid, bias=one_col("nr")).then_inc(sig["r"][b.u], 1)
                            ready(act, "gz", b.u, b.n(q, "gz", i, k))
                            f(b.w[2], b.b, ACT.Sigmoid, bias=one_col("nz")).then_inc(sig["z"][b.u], 1)
                        for b in chains:
                            ready(act, "rh", b.u, b.n(q, "rh", i, k))
                            f(b.w[1], b.w[3], ACT.Tanh, bias=one_col("nn")).then_inc(sig["n"][b.u], 1)
                    for c, b in enumerate(chains):
                        ready(act, "ot", b.u, b.n(q, "ot", i))
                        stored(act, "st_out", c, i + first)
                        f(b.out, b.a, ACT.Copy).then_inc(sig["oc"][b.u], 1)

            act.wait_ge(s_const, 16 * 10)
            q = p_["T_setup"]

            def body(i, par, j, q=q):
                ready(act, "tab_sum", par, q.n("tab_sum", par, j))
                spent(act, "deg_r", par, q.n("deg_r", par, j))
                f(w[0][par][:], tab_in[par][:], ACT.Sqrt, bias=one_col("two")).then_inc(sig["deg_sd"][par], 1)
                ready(act, "tab_t", par, q.n("tab_t", par, j))
                f(ends[:, bass.ds(i * TILES, TILES), 1:2],
                  pD[par].rearrange("p (k f) -> p k f", f=D)[:, :, 0:1], ACT.Identity, bias=one_col("one")
                  ).then_inc(sig["tab_rm"][par], 1)
            sweep(act, EB, body)
            for par in (0, 1):
                ready(act, "deg_r", par, p_["T_setup"].last("deg_r", par))
                stored(act, "st_d", par, p_["T_setup"].last("st_d", par) + 1)
            nodes("N_early", 0, EARLY)
            q = p_["ENDS"]
            act.wait_ge(s_pairs, EB + 2)

            def body(i, par, j, q=q):
                spent(act, "ends_bc", par, q.n("ends_bc", par, j))
                f(deg_small[par][:].rearrange("p (k a) -> p k a", a=1), src_ends[:, bass.ds(i * TILES, TILES), 1:2], ACT.Sqrt, bias=one_col("one")
                  ).then_inc(sig["ends_sd"][par], 1)
                ready(act, "ends_t", par, q.n("ends_t", par, j))
                stored(act, "st_d", par, q.n("st_d", par, j))
                f(w[1][par][:], pA[par], ACT.Copy).then_inc(sig["ends_d"][par], 1)
            sweep(act, EB, body)

            q = p_["P0"]
            for par in (0, 1):
                stored(act, "st_d", par, p_["ENDS"].last("st_d", par) + 1)

            def body(i, par, j, q=q, q2=p_["WE"]):
                for u in SPACES:
                    ready(act, "head", u, q.n("head", u, i))
                    stored(act, "st_x", u, q.n("st_x", u, i))
                    f(xb[u][:], pA[u], ACT.Copy).then_inc(sig["xb"][u], 1)
                layer_norm(q, space, i)
                def hidden(t):
                    ready(act, "ehp", t % 2, q2.n("ehp", t % 2, i, t // 2))
                    f(w[0][t % 2][:], pA[t % 2], ACT.Relu, bias=one_col("en1_b")).then_inc(sig["eh"][t % 2], 1)
                hidden(0)
                for t in range(T):
                    if t + 1 < T:
                        hidden(t + 1)
                    for k in (0, 2):
                        ready(act, "wep", 0, q2.n("wep", 0, i, 2 * t + k // 2))
                        stored(act, "st_we", k // 2, i * T + t)
                        f(ring[k // 2], ps[:, 1:3, :].rearrange("p a f -> p (a f)"), ACT.Copy).then_inc(sig["weo"][0], 1)
            sweep(act, EB, body)
            tables("T0")

            q = p_["P1"]

            def body(i, par, j, q=q):
                for u in SPACES:
                    ready(act, "head", u, q.n("head", u, i))
                    f(w[0][u][:], pA[u], ACT.Copy).then_inc(sig["agg"][u], 1)
                for u in SPACES:
                    sage(q, u, i)
            sweep(act, EB, body)
            tables("T1")

            q = p_["P2"]

            def body(i, par, j, q=q):
                layer_norm(q, space, i)
            sweep(act, EB, body)
            tables("T2")

            q = p_["T3"]
            for t in range(T):
                def hidden(i, par, j, t=t, q=q):
                    ready(act, "b1", par, q.n("b1", par, j, t * halves(EB)[par]))
                    f(w[1][par][:], pA[par], ACT.Relu, bias=one_col("b1")).then_inc(sig["b1r"][par], 1)

                def sums(i, par, j, t=t, q=q):
                    off = t * halves(EB)[par]
                    ready(act, "b3t", par, q.n("b3t", par, j, off))
                    stored(act, "st_tab4", par, q.n("st_tab4", par, j, off))
                    f(w[4][par][:], pD[par], ACT.Copy).then_inc(sig["b4"][par], 1)

                def body(i, par, j, par1, j1):
                    hidden(i + 1, par1, j1)
                    sums(i, par, j)
                sweep_ahead(act, lambda: hidden(0, 0, 0), body, sums)

            q = p_["P4"]

            def body(i, par, j, q=q):
                def first(u, t):
                    ready(act, "q1", u, q.n("q1", u, i, t))
                    f(w[1][u][:], pB[u], ACT.Relu, bias=one_col("b1")).then_inc(sig["q1r"][u], 1)

                def second(u, t):
                    ready(act, "q5", u, q.n("q5", u, i, t))
                    spent(act, "q7", u, q.n("q7", u, i, t))
                    f(w[3][u][:], pB[u], ACT.Relu, bias=one_col("b2")).then_inc(sig["q6"][u], 1)

                for t in range(T + 1):
                    if t < T:
                        first(S_, t)
                    if t:
                        second(D_, t - 1)
                    if t < T:
                        first(D_, t)
                        second(S_, t)
            sweep(act, EB, body)
            tables("T4")

            q = p_["P5"]

            def body(i, par, j, q=q):
                for u in SPACES:
                    ready(act, "c1b", u, q.n("c1b", u, i))
                    f(w[2][u][:], w[1][u][:], ACT.Relu, bias=one_col("b3")).then_inc(sig["c5r"][u], 1)
                layer_norm(q, space, i)
                for u in SPACES:
                    ready(act, "lin", u, q.n("lin", u, i))
                    f(hn[u], pD[u], ACT.Relu, bias=one_col("lin0_b")).then_inc(sig["hn"][u], 1)
                rows(q, i)
            sweep(act, EB, body)
            tables("T5")

            def gru_pass(q, more):
                def body(i, par, j):
                    for u in SPACES:
                        ready(act, "head", u, q.n("head", u, i))
                        f(w[0][u][:], pA[u], ACT.Relu, bias=one_col("conv_b")).then_inc(sig["m"][u], 1)
                        gru(q, u, i)
                    for u in SPACES:
                        gru_new(q, u, i)
                    more(i, par, j)
                sweep(act, EB, body)

            for k, name in enumerate(GRU_PASSES):
                def new_rows(i, par, j, q=p_[name]):
                    ready(act, "mt", S_, q.n("mt", S_, i))
                    spent(act, "pr", S_, q.n("pr", S_, i), TILES + 1)
                    f(state_rows[par][:], pB[S_], ACT.Copy).then_inc(sig["hrm"][S_], 1)
                gru_pass(p_[name], new_rows)
                tables(f"T{6 + k}")

            gru_pass(p_["P11"], lambda i, par, j: layer_norm(p_["P11"], space[:1], i))

            pass_over(act, "P11")

            def body(blocks, q=p_["R11"]):
                for c, i, j in blocks:
                    spent(act, "mt", c, q.n("mt", c, j))
                    f(hb[c], blk(h[S_], i), ACT.Copy).then_inc(sig["th"][c], 1)
                relation(q, blocks)
            sweep_pairs(act, body)
            tables("T11")

            def body(blocks, q=p_["P12"]):
                for c, i, j in blocks:
                    ready(act, "head", c, q.n("head", c, j))
                    f(hb[c], pA[c], ACT.Tanh).then_inc(sig["th"][c], 1)
                relation(q, blocks)
            sweep_pairs(act, body)
            tables("T12")

            nodes("N", EARLY, NP - EARLY)

            q = p_["P13"]
            stored(act, "st_out", D_, NP)

            def body(i, par, j, q=q):
                ready(act, "ot", D_, q.n("ot", D_, i))
                spent(act, "scattered", D_, q.n("scattered", D_, i))
                f(db[D_][:], pB[D_], ACT.Copy).then_inc(sig["oc"][D_], 1)
            sweep(act, EB, body)

        @block.vector
        def _(dve):
            v = nc.vector

            def rank3(ap, n):
                return ap.rearrange("p (a b) -> p a b", b=n)

            def layer_norm(q, bs, i, dsts, sub=0):
                for b in bs:
                    ready(dve, "ln_v", b.u, b.n(q, "ln_v", i, sub))
                    v.tensor_scalar(b.var, b.small[:, 0:TILES], 1e-5, None, ALU.add).then_inc(sig["ln_s"][b.u], 1)
                for b in bs:
                    ready(dve, "ln_sd", b.u, b.n(q, "ln_sd", i, sub))
                    v.reciprocal(b.root, b.root).then_inc(sig["ln_r0"][b.u], 1)
                for b in bs:
                    ready(dve, "ln_r0", b.u, b.n(q, "ln_r0", i, sub))
                    v.tensor_tensor(b.newton, b.root, b.root, ALU.mult).then_inc(sig["ln_a"][b.u], 1)
                for b in bs:
                    ready(dve, "ln_a", b.u, b.n(q, "ln_a", i, sub))
                    v.scalar_tensor_tensor(b.newton, b.newton, -0.5, b.var, ALU.mult, ALU.mult).then_inc(sig["ln_b"][b.u], 1)
                for b in bs:
                    ready(dve, "ln_b", b.u, b.n(q, "ln_b", i, sub))
                    v.scalar_tensor_tensor(b.root, b.newton, 1.5, b.root, ALU.add, ALU.mult).then_inc(sig["ln_y"][b.u], 1)
                for b in bs:
                    ready(dve, "ln_y", b.u, b.n(q, "ln_y", i, sub))
                    v.tensor_copy(rank3(b.w[2], D), b.root.rearrange("p (k a) -> p k a", a=1)
                                  .to_broadcast([P, TILES, D])).then_inc(sig["ln_r"][b.u], 1)
                for b, dst in zip(bs, dsts):
                    ready(dve, "ln_relu", b.u, b.n(q, "ln_relu", i, sub))
                    ready(dve, "ln_t", b.u, b.n(q, "ln_t", i, sub))
                    v.tensor_tensor(dst, b.w[1], b.spread, ALU.mult).then_inc(sig["ln"][b.u], 1)

            def run_sums(q, i, messages):
                spent(dve, "scan", S_, q.n("scan", S_, i))
                v.tensor_tensor_scan(scan[:, bass.ds(i * W + 1, W)], blk(keep, i), messages, scan[:, bass.ds(i * W, 1)],
                                     ALU.mult, ALU.add).then_inc(sig["scan"][S_], 1)

            def tables(name, after):
                q = p_[name]
                if after:
                    pass_over(dve, after)
                ready(dve, "tab_end", 0, q.n("tab_end", 0, 0))
                v.tensor_copy(carry[:], pA[0][:, 0:1]).then_inc(sig["carry"][0], 1)
                ready(dve, "carry", 0, q.n("carry", 0, 0))

                def body(i, par, j):
                    spent(dve, "tab_t", par, q.n("tab_t", par, j))
                    if name == "T_setup":
                        spent(dve, "deg_sd", par, q.n("deg_sd", par, j))
                    v.scalar_tensor_tensor(tab_in[par][:], blk(first, i), carry[:], scan[:, bass.ds(i * W + 1, W)],
                                           ALU.mult, ALU.add).then_inc(sig["tab_sum"][par], 1)
                    if name == "T_setup":
                        ready(dve, "deg_sd", par, q.n("deg_sd", par, j))
                        stored(dve, "st_d", par, q.n("st_d", par, j))
                        v.reciprocal(w[1][par][:], w[0][par][:]).then_inc(sig["deg_r"][par], 1)
                sweep(dve, EB, body)

            def gate(q, u, i):
                ready(dve, "ghn", u, q.n("ghn", u, i))
                ready(dve, "r", u, q.n("r", u, i))
                v.scalar_tensor_tensor(w[3][u][:], pD[u], one_col("hn"), w[1][u][:], ALU.add, ALU.mult
                                       ).then_inc(sig["rh"][u], 1)

            def sum_new(q, u, i):
                ready(dve, "rh", u, q.n("rh", u, i))
                ready(dve, "gin", u, q.n("gin", u, i))
                v.tensor_tensor(w[4][u][:], w[3][u][:], pA[u], ALU.add).then_inc(sig["npre"][u], 1)

            def gru(q, u, i):
                gate(q, u, i)
                sum_new(q, u, i)

            def blend_a(q, u, i, old):
                ready(dve, "n", u, q.n("n", u, i))
                v.tensor_tensor(w[3][u][:], old, w[1][u][:], ALU.subtract).then_inc(sig["u1"][u], 1)

            def blend_b(q, u, i):
                ready(dve, "u1", u, q.n("u1", u, i))
                ready(dve, "z", u, q.n("z", u, i))
                v.tensor_tensor(w[4][u][:], w[3][u][:], w[2][u][:], ALU.mult).then_inc(sig["u2"][u], 1)

            def blend_c(q, u, i, new, kind):
                ready(dve, "u2", u, q.n("u2", u, i))
                v.tensor_tensor(new, w[4][u][:], w[1][u][:], ALU.add).then_inc(sig[kind][u], 1)

            def gru_blend(q, u, i, old, new, kind):
                blend_a(q, u, i, old)
                blend_b(q, u, i)
                blend_c(q, u, i, new, kind)

            def edge_messages(q, i):
                edge_tiles(q, i, h_rows, msg_rows, {})

            def edge_tiles(q, i, h_rows, msg_rows, between):
                ready(dve, "hrm", S_, q.n("hrm", S_, i))
                for k in range(TILES + 1):
                    if k < TILES:
                        landed(dve, "ld_w", k % RING, q.n("ld_w", k % RING, i, k // RING))
                        tile = rank3(ring[k % RING], D)
                        state = h_rows[:, k * D:k * D + D].rearrange("p (a i) -> p a i", a=1).to_broadcast([P, D, D])
                        v.tensor_tensor(tile, tile, state, ALU.mult).then_inc(sig["pr"][S_], 1)
                    if k:
                        m = k - 1
                        ready(dve, "pr", S_, q.n("pr", S_, i, m))
                        v.tensor_reduce(msg_rows[:, m * D:m * D + D], rank3(ring[m % RING][:], D), AX_X, ALU.add
                                        ).then_inc(sig["rd"][S_], 1)
                    if k in between:
                        between[k]()
                ready(dve, "mf", S_, q.n("mf", S_, i))
                run_sums(q, i, pC[S_])

            def relation_messages(q, blocks):
                for c, i, j in blocks:
                    v.tensor_tensor(onehot[c][:], etype[:, bass.ds(i * TILES, TILES)].rearrange("p (k a) -> p k a", a=1)
                                    .to_broadcast([P, TILES, R]),
                                    rel_id[:].rearrange("p (a r) -> p a r", a=1).to_broadcast([P, TILES, R]),
                                    ALU.is_equal).then_inc(sig["oh"][c], 1)
                for c, i, j in blocks:
                    ready(dve, "oh", c, q.n("oh", c, j))
                    ready(dve, "hrm", c, q.n("hrm", c, j))
                    hot, truth = onehot[c][:], tv[:, bass.ds(i * TILES, TILES), :]
                    v.tensor_tensor(w[2][c][:].rearrange("p (k r q) -> p k r q", r=R, q=T),
                                    hot.rearrange("p k (r a) -> p k r a", a=1).to_broadcast([P, TILES, R, T]),
                                    truth.rearrange("p k (a q) -> p k a q", a=1).to_broadcast([P, TILES, R, T]),
                                    ALU.mult).then_inc(sig["ob"][c], 1)
                for g in range(Q + 1):
                    for c, i, j in blocks:
                        if g < Q:
                            spent(dve, "zt", c, q.n("zt", c, j, g), 2)
                            v.tensor_tensor(Z[c][g % 2].rearrange("p (t q i) -> p t q i", t=T, q=T),
                                            w[3][c][:, g * P:g * P + P].rearrange("p (t a i) -> p t a i", t=T, a=1)
                                            .to_broadcast([P, T, T, D]),
                                            tv[:, bass.ds(i * TILES + g * T, T), :].rearrange("p t (q b) -> p t q b", b=1)
                                            .to_broadcast([P, T, T, D]), ALU.mult).then_inc(sig["zz"][c], 1)
                    for c, i, j in blocks:
                        if g:
                            for half, bank in enumerate((pD, pA)):
                                m = 2 * (g - 1) + half
                                ready(dve, "rg", c, q.n("rg", c, j, m))
                                v.tensor_tensor(picked[c][half].rearrange("p (t o r) -> p t o r", t=2, r=R),
                                                bank[c].rearrange("p (t o r) -> p t o r", t=2, r=R),
                                                onehot[c][:, 2 * m:2 * m + 2, :].rearrange("p t (a r) -> p t a r", a=1)
                                                .to_broadcast([P, 2, D, R]), ALU.mult).then_inc(sig["rgm"][c], 1)
                                ready(dve, "rgm", c, q.n("rgm", c, j, m))
                                v.tensor_reduce(w[4][c][:, 2 * m * D:2 * (m + 1) * D], rank3(picked[c][half], R), AX_X, ALU.add
                                                ).then_inc(sig["rd"][c], 1)
                for c, i, j in blocks:
                    ready(dve, "mf", c, q.n("mf", c, j))
                    run_sums(q, i, pA[c])

            def nodes(name, first, groups):
                q = p_[name]
                with dve.Fori(0, groups) as i:
                    layer_norm(q, chains, i, [b.h for b in chains], 0)
                    for b in chains:
                        ready(dve, "l0x_mm", b.u, b.n(q, "l0x_mm", i))
                        v.scalar_tensor_tensor(b.x, b.a, one_col("b_out"), b.x, ALU.add, ALU.add).then_inc(sig["xb"][b.u], 1)
                    layer_norm(q, chains, i, [b.h for b in chains], 1)
                    for b in chains:
                        ready(dve, "c5r", b.u, b.n(q, "c5r", i))
                        v.tensor_tensor(b.x, b.x, b.w[1], ALU.add).then_inc(sig["xb"][b.u], 1)
                    layer_norm(q, chains, i, [b.h for b in chains], 2)
                    for k in range(STEPS):
                        for b in chains:
                            ready(dve, "ghn", b.u, b.n(q, "ghn", i, k))
                            ready(dve, "r", b.u, b.n(q, "r", i, k))
                            v.scalar_tensor_tensor(b.w[3], b.a, one_col("hn"), b.w[1], ALU.add, ALU.mult
                                                   ).then_inc(sig["rh"][b.u], 1)
                        for b in chains:
                            ready(dve, "n", b.u, b.n(q, "n", i, k))
                            v.tensor_tensor(b.w[3], b.new, b.w[1], ALU.subtract).then_inc(sig["u1"][b.u], 1)
                            ready(dve, "u1", b.u, b.n(q, "u1", i, k))
                            ready(dve, "z", b.u, b.n(q, "z", i, k))
                            v.tensor_tensor(b.w[3], b.w[3], b.w[2], ALU.mult).then_inc(sig["u2"][b.u], 1)
                            ready(dve, "u2", b.u, b.n(q, "u2", i, k))
                            v.tensor_tensor(b.new, b.w[3], b.w[1], ALU.add).then_inc(sig["hn"][b.u], 1)
                    for b in chains:
                        ready(dve, "hn", b.u, b.n(q, "hn", i, STEPS))
                        v.tensor_tensor(b.w[0], b.x, b.new, ALU.add).then_inc(sig["of"][b.u], 1)

            v.memset(scan[:], 0.0).then_inc(s_set, 1)
            dve.wait_ge(s_bd, 16 * 2 * T)
            v.tensor_tensor(keep[:], h[0][:].bitcast(I32), h[1][:].bitcast(I32), ALU.is_equal).then_inc(s_set, 1)
            dve.wait_ge(s_set, 2)
            v.tensor_tensor_scan(first[:], keep[:], keep[:], 1.0, ALU.min, ALU.min).then_inc(s_set, 1)
            dve.wait_ge(s_start, 48)
            dve.wait_ge(s_set, 3)
            v.tensor_tensor_scan(scan[:, 1:EC + 1], keep[:], keep[:], 0.0, ALU.mult, ALU.add).then_inc(s_set, 1)
            dve.wait_ge(s_const, 16 * 10)
            dve.wait_ge(s_idx, 16 * 3)
            v.tensor_copy(first_end[:], first[:, EC - 1:EC]).then_inc(s_own, 1)
            dve.wait_ge(s_own, 1)
            v.tensor_scalar(w[0][0][:, 0:P], mat["next_quarter"], first_end[:], None, ALU.mult).then_inc(s_set, 1)
            dve.wait_ge(s_pset, 1)
            dve.wait_ge(s_set, 5)
            v.scalar_tensor_tensor(w[1][0][:, 0:P], pA[0][:, 0:P], first_end[:], w[0][0][:, 0:P], ALU.mult, ALU.add
                                   ).then_inc(s_set, 1)
            dve.wait_ge(s_pset, 2)
            v.tensor_tensor(carry_mat[:], pB[0][:, 0:P], mat["next_quarter"], ALU.add).then_inc(s_set, 1)
            v.tensor_tensor(one_col("r"), one_col("ir"), one_col("hr"), ALU.add).then_inc(s_set, 1)
            v.tensor_tensor(one_col("z"), one_col("iz"), one_col("hz"), ALU.add).then_inc(s_set, 1)
            v.tensor_scalar(w[2][0][:, 0:1], one_col("conv_b"), 0.0, None, ALU.max).then_inc(s_set, 1)
            dve.wait_ge(s_set, 10)
            dve.wait_ge(s_pset, 5)
            for k, (name, part) in enumerate((("nr", "r"), ("nz", "z"), ("nn", "in"))):
                v.tensor_tensor(one_col(name), pC[0][:, k:k + 1], one_col(part), ALU.add).then_inc(s_set, 1)
            v.tensor_tensor(run_a, idx["dst"][:], idx["row"][:], ALU.not_equal).then_inc(s_set, 1)
            dve.wait_ge(s_set, 14)
            v.tensor_scalar(run_b, run_a, -float(BIG), float(BIG), ALU.mult, ALU.add).then_inc(s_set, 1)
            dve.wait_ge(s_set, 15)
            v.tensor_tensor(idx["run_end"][:], run_b, idx["dst"][:], ALU.add).then_inc(s_set, 1)
            v.tensor_copy(ends[:, :, 0:1], slot_row.rearrange("p (k a) -> p k a", a=1)).then_inc(s_set, 1)
            for t in range(T):
                last = v.tensor_copy(spread_bf[:, t, :], mat[f"spread{t}"])
            last.then_inc(s_set, 1)
            tables("T_setup", None)
            for par in (0, 1):
                ready(dve, "tab_rm", par, p_["T_setup"].last("tab_rm", par))
            nodes("N_early", 0, EARLY)
            pass_over(dve, "N_early")
            for c in range(CHAINS):
                stored(dve, "st_out", c, EARLY)
            q = p_["ENDS"]
            dve.wait_ge(s_pairs, EB + 2)
            settle(dve)

            def body(i, par, j, q=q):
                v.tensor_copy(idx["row"][:, bass.ds(i * TILES, TILES)].rearrange("p (k a) -> p k a", a=1),
                              src_ends[:, bass.ds(i * TILES, TILES), 0:1]).then_inc(sig["ends_row"][par], 1)
                ready(dve, "ends_sd", par, q.n("ends_sd", par, j))
                v.reciprocal(deg_small[par][:], deg_small[par][:]).then_inc(sig["ends_r"][par], 1)
                ready(dve, "ends_r", par, q.n("ends_r", par, j))
                spent(dve, "ends_t", par, q.n("ends_t", par, j))
                v.tensor_copy(rank3(w[0][par][:], D), deg_small[par][:].rearrange("p (k a) -> p k a", a=1)
                              .to_broadcast([P, TILES, D])).then_inc(sig["ends_bc"][par], 1)
            sweep(dve, EB, body)

            q = p_["P0"]

            def body(i, par, j, q=q, q2=p_["WE"]):
                layer_norm(q, space, i, [blk(h[u], i) for u in SPACES])
                ready(dve, "ln", S_, q.n("ln", S_, i))
                run_sums(q, i, blk(h[S_], i))
                for t in range(T):
                    for k in (1, 3):
                        ready(dve, "wep", 1, q2.n("wep", 1, i, 2 * t + k // 2))
                        stored(dve, "st_we", 2 + k // 2, i * T + t)
                        v.tensor_copy(ring[2 + k // 2], ps[:, 5:7, :].rearrange("p a f -> p (a f)")
                                      ).then_inc(sig["weo"][1], 1)
            sweep(dve, EB, body)
            tables("T0", "P0")

            q = p_["P1"]

            def sage(q, u, i, sub, kind):
                ready(dve, "l0x_mm", u, q.n("l0x_mm", u, i))
                v.scalar_tensor_tensor(xb[u][:], pD[u], one_col("b_out"), xb[u][:], ALU.add, ALU.add
                                       ).then_inc(sig[kind][u], 1)

            def body(i, par, j, q=q):
                for u in SPACES:
                    landed(dve, "ld_x", u, q.n("ld_x", u, i))
                    sage(q, u, i, 0, "l0x")
                ready(dve, "l0y", S_, q.n("l0y", S_, i))
                run_sums(q, i, pA[S_])
            sweep(dve, EB, body)
            tables("T1", "P1")

            q = p_["P2"]

            def body(i, par, j, q=q):
                for u in SPACES:
                    ready(dve, "head", u, q.n("head", u, i))
                    landed(dve, "ld_x", u, q.n("ld_x", u, i))
                    v.tensor_tensor(xb[u][:], xb[u][:], pA[u], ALU.add).then_inc(sig["xb"][u], 1)
                layer_norm(q, space, i, hb)
                for u in SPACES:
                    ready(dve, "ln", u, q.n("ln", u, i))
                    landed(dve, "ld_d", u, q.n("ld_d", u, i))
                    v.tensor_tensor(blk(h[u], i), hb[u], db[u][:], ALU.mult).then_inc(sig["g"][u], 1)
                ready(dve, "g", S_, q.n("g", S_, i))
                run_sums(q, i, blk(h[S_], i))
            sweep(dve, EB, body)
            tables("T2", "P2")

            q = p_["P3"]

            def body(i, par, j, q=q):
                for u in SPACES:
                    ready(dve, "head", u, q.n("head", u, i))
                    v.tensor_tensor(w[0][u][:], blk(h[u], i), pA[u], ALU.add).then_inc(sig["c1a"][u], 1)
                for u in SPACES:
                    ready(dve, "c1a", u, q.n("c1a", u, i))
                    landed(dve, "ld_d", u, q.n("ld_d", u, i))
                    v.tensor_tensor(blk(h[u], i), w[0][u][:], db[u][:], ALU.mult).then_inc(sig["g"][u], 1)
            sweep(dve, EB, body)

            v.memset(carry[:], 0.0).then_inc(s_end4, 1)
            q = p_["T3"]
            for t in range(T):
                def body(i, par, j, t=t, q=q):
                    off = t * halves(EB)[par]
                    ready(dve, "b1r", par, q.n("b1r", par, j, off))
                    ready(dve, "bd", par, q.n("bd", par, j, off))
                    v.tensor_tensor(w[2][par][:], w[1][par][:], pB[par], ALU.mult).then_inc(sig["bm"][par], 1)
                    ready(dve, "bm", par, q.n("bm", par, j, off))
                    ready(dve, "bk", par, q.n("bk", par, j, off))
                    dve.wait_ge(s_end4, i + (t * EB + 1))
                    v.tensor_tensor_scan(w[3][par][:], pC[par], w[2][par][:], carry[:], ALU.mult, ALU.add
                                         ).then_inc(sig["b3"][par], 1)
                    ready(dve, "b3", par, q.n("b3", par, j, off))
                    v.tensor_copy(carry[:], w[3][par][:, W - 1:W]).then_inc(s_end4, 1)
                sweep(dve, EB, body)

            q = p_["P4"]

            def body(i, par, j, q=q):
                for t in range(T):
                    for u in SPACES:
                        ready(dve, "q1r", u, q.n("q1r", u, i, t))
                        ready(dve, "qd", u, q.n("qd", u, i, t))
                        v.tensor_tensor(w[2][u][:], w[1][u][:], pC[u], ALU.mult).then_inc(sig["q2"][u], 1)
                        ready(dve, "q2", u, q.n("q2", u, i, t))
                        ready(dve, "q_head", u, q.n("q_head", u, i, t))
                        v.tensor_tensor(w[4][u][:], w[2][u][:], pA[u], ALU.add).then_inc(sig["q3"][u], 1)
                        ready(dve, "q3", u, q.n("q3", u, i, t))
                        v.tensor_tensor(w[2][u][:], w[4][u][:], pC[u], ALU.mult).then_inc(sig["q4"][u], 1)
                for u in SPACES:
                    ready(dve, "q7", u, q.n("q7", u, i, T - 1))
                    v.tensor_tensor(blk(h[u], i), pD[u], db[u][:], ALU.mult).then_inc(sig["g"][u], 1)
                ready(dve, "g", S_, q.n("g", S_, i))
                run_sums(q, i, blk(h[S_], i))
            sweep(dve, EB, body)
            tables("T4", "P4")

            q = p_["P5"]

            def body(i, par, j, q=q):
                for u in SPACES:
                    ready(dve, "head", u, q.n("head", u, i))
                    v.tensor_tensor(w[0][u][:], blk(h[u], i), pA[u], ALU.add).then_inc(sig["c1a"][u], 1)
                for u in SPACES:
                    ready(dve, "c1a", u, q.n("c1a", u, i))
                    landed(dve, "ld_d", u, q.n("ld_d", u, i))
                    v.tensor_tensor(w[1][u][:], w[0][u][:], db[u][:], ALU.mult).then_inc(sig["c1b"][u], 1)
                for u in SPACES:
                    ready(dve, "c5r", u, q.n("c5r", u, i))
                    landed(dve, "ld_x", u, q.n("ld_x", u, i))
                    v.tensor_tensor(xb[u][:], xb[u][:], w[2][u][:], ALU.add).then_inc(sig["xb"][u], 1)
                layer_norm(q, space, i, hb)
                for u in SPACES:
                    ready(dve, "hn", u, q.n("hn", u, i))
                    settle(dve)
                    v.tensor_copy(blk(h[u], i), hn[u]).then_inc(sig["hs"][u], 1)
                edge_messages(q, i)
            sweep(dve, EB, body)
            tables("T5", "P5")

            for k, name in enumerate(GRU_PASSES):
                q = p_[name]

                def own_state(q, i):
                    ready(dve, "hn", S_, q.n("hn", S_, i))
                    settle(dve)
                    v.tensor_copy(blk(h[S_], i), hn[S_]).then_inc(sig["hs"][S_], 1)

                def stages(q, i):
                    return {2: lambda: gate(q, S_, i), 3: lambda: sum_new(q, S_, i),
                            4: lambda: gate(q, D_, i), 5: lambda: sum_new(q, D_, i),
                            6: lambda: blend_a(q, S_, i, blk(h[S_], i)), 7: lambda: blend_b(q, S_, i),
                            8: lambda: blend_c(q, S_, i, hn[S_], "hn"), 9: lambda: own_state(q, i),
                            TILES: lambda: gru_blend(q, D_, i, blk(h[D_], i), blk(h[D_], i), "hs")}

                def start(q=q):
                    for run in stages(q, 0).values():
                        run()

                def body(i, par, j, par1, j1, q=q):
                    edge_tiles(q, i, state_rows[par], sum_rows[par], stages(q, i + 1))

                def last(i, par, j, q=q):
                    edge_tiles(q, i, state_rows[par], sum_rows[par], {})
                sweep_ahead(dve, start, body, last)
                tables(f"T{6 + k}", name)

            q = p_["P11"]

            def body(i, par, j, q=q):
                for u in SPACES:
                    gru(q, u, i)
                for u in SPACES:
                    gru_blend(q, u, i, blk(h[u], i), hn[u], "hn")
                for u in SPACES:
                    ready(dve, "hn", u, q.n("hn", u, i))
                    landed(dve, "ld_x", u, q.n("ld_x", u, i))
                    v.tensor_tensor(xb[u][:], xb[u][:], hn[u], ALU.add).then_inc(sig["xb"][u], 1)
                layer_norm(q, space[:1], i, [blk(h[S_], i)])
            sweep(dve, EB, body)

            pass_over(dve, "P11")
            stored(dve, "st_x", D_, q.last("st_x", D_) + 1)
            sweep_pairs(dve, lambda blocks: relation_messages(p_["R11"], blocks))
            tables("T11", "R11")
            sweep_pairs(dve, lambda blocks: relation_messages(p_["P12"], blocks))
            tables("T12", "P12")

            nodes("N", EARLY, NP - EARLY)

            q = p_["P13"]

            def body(i, par, j, q=q):
                ready(dve, "head", D_, q.n("head", D_, i))
                landed(dve, "ld_x", D_, q.n("ld_x", D_, i))
                v.tensor_tensor(w[0][D_][:], xb[D_][:], pA[D_], ALU.add).then_inc(sig["of"][D_], 1)
            sweep(dve, EB, body)


def kernel(**inputs):
    import numpy as _np
    import concourse.bacc as _bacc
    from concourse import mybir as _mybir
    from concourse.bass_utils import run_bass_kernel_spmd as _run

    a = {k: _np.asarray(v) for k, v in inputs.items()}
    f32, i32 = _np.float32, _np.int32
    nodes, edges = a["x"].shape[0], a["src"].shape[0]
    NP = -(-(nodes + 2) // (CHAINS * W * T))
    EB = -(-edges // (W * T))
    NR, EC = NP * CHAINS * W, EB * W
    NODES, GE = NR * T, EC * T

    def rows_of(flat):
        v = flat.reshape((T, EC // P, P) + flat.shape[1:])
        v = v.transpose((2, 1, 0) + tuple(range(3, v.ndim)))
        return _np.ascontiguousarray(v.reshape((P, GE // P) + flat.shape[1:]))

    def pad(v, n, fill=0):
        return _np.concatenate([v, _np.full((n - v.shape[0],) + v.shape[1:], fill, v.dtype)])

    src = pad(a["src"], GE, nodes + 1)
    dst = pad(a["dst"], GE, nodes)
    before = _np.concatenate([_np.full((1,), -1, dst.dtype), dst[:-1]])
    after = _np.concatenate([dst[1:], _np.full((1,), -1, dst.dtype)])

    def quarters(v):
        return _np.ascontiguousarray(v.reshape(T, EC))

    def four(m, rows, cols, r_step=None, c_step=None, ts=range(T)):
        z = _np.zeros((P, P), m.dtype)
        for j, t in enumerate(ts):
            r, c = rows(j, t), cols(j, t)
            z[r:r + m.shape[0], c:c + m.shape[1]] = m
        return z

    own, pair, zero = (lambda j, t: t * D), (lambda j, t: j * H0), (lambda j, t: 0)
    g = {k: a["L2_gnn_" + k] for k in ("gru_wih", "gru_whh", "gru_bih", "gru_bhh")}
    wts = {}
    for k in (0, 1):
        ts = (2 * k, 2 * k + 1)
        wts[f"l0_l{k}"] = four(a["L0_gnn_W_l_in"].T, own, pair, ts=ts)
        wts[f"l0_r{k}"] = four(a["L0_gnn_W_r_in"].T, own, pair, ts=ts)
        wts[f"l0_ol{k}"] = four(a["L0_gnn_W_l_out"].T, pair, own, ts=ts)
        wts[f"l0_or{k}"] = four(a["L0_gnn_W_r_out"].T, pair, own, ts=ts)
    for t in range(T):
        wts[f"w1_{t}"] = four(a["L1_gnn_W1"], own, zero, ts=(t,))
        wts[f"w3_{t}"] = four(a["L1_gnn_W3"], zero, own, ts=(t,))
    wts["w2"] = a["L1_gnn_W2"]
    wts["lin0"] = four(a["L2_gnn_lin0_w"].T, own, own)
    for k, name in enumerate("rzn"):
        wts["i" + name] = four(g["gru_wih"][k * D:k * D + D].T, own, own)
        wts["h" + name] = four(g["gru_whh"][k * D:k * D + D].T, own, own)
    wts["en2b"] = four(a["L2_gnn_en2_b"].reshape(D, D), own, own)
    for k in (0, 1):
        wts[f"rel_b{k}"] = four(a[f"L3_gnn_b{k + 1}"].reshape(R * T, D), own, own)
    tile = lambda v: _np.concatenate([v] * (P // v.shape[0]))
    cols = {"b_in": a["L0_gnn_b_l_in"], "b_out": a["L0_gnn_b_l_out"], "b1": a["L1_gnn_b1"], "b2": a["L1_gnn_b2"],
            "b3": a["L1_gnn_b3"], "lin0_b": a["L2_gnn_lin0_b"], "en1_b": a["L2_gnn_en1_b"], "conv_b": a["L2_gnn_conv_bias"],
            "zero": _np.zeros(1, f32), "eps": _np.full(1, 1e-5, f32), "one": _np.ones(1, f32), "two": _np.full(1, 2, f32)}
    for k, name in enumerate("rzn"):
        cols["i" + name] = g["gru_bih"][k * D:k * D + D]
        cols["h" + name] = g["gru_bhh"][k * D:k * D + D]
    slot = _np.arange(GE)
    data = {
        "x": pad(a["x"], NODES).reshape(NR, P),
        "src": rows_of(src), "dst": rows_of(dst), "dst_after": rows_of(after),
        "dst_fm": quarters(dst), "dst_before_fm": quarters(before),
        "edge_attr_T": _np.ascontiguousarray(pad(a["edge_attr_32"], GE).T),
        "tv": rows_of(pad(a["edge_attr_4"], GE)), "etype": rows_of(pad(a["edge_type_8"], GE)),
        "mats": shape_matrices(), "weights": _np.stack([wts[k] for k in WEIGHTS], 1),
        "biases": _np.stack([tile(cols[k]) for k in BIASES[:NB_LOADED]], 1),
        "en1": _np.ascontiguousarray(a["L2_gnn_en1_w"].T),
        "en2": _np.ascontiguousarray(a["L2_gnn_en2_w"].reshape(D, D, P).transpose(2, 1, 0).reshape(P, D * D)),
        "rel_w": _np.ascontiguousarray(_np.stack([a[f"L3_gnn_W{k}"].transpose(1, 2, 3, 0).reshape(P, D * R) for k in (1, 2)], 1)),
        "rel_id": _np.ascontiguousarray(_np.broadcast_to(_np.arange(R, dtype=f32), (P, R))),
        "slot_row": rows_of(((slot % EC + 1) * T + slot // EC).astype(f32)),
    }
    nc = _bacc.Bacc("TRN2", target_bir_lowering=False, num_devices=1)
    arrays, ins = {}, {}
    for name, v in data.items():
        v = _np.ascontiguousarray(v)
        arrays[f"in_{name}_dram"] = v
        ins[name] = nc.dram_tensor(f"in_{name}_dram", v.shape, _mybir.dt.from_np(v.dtype), kind="ExternalInput").ap()
    out = nc.dram_tensor("out_0_dram", (NR, P), _mybir.dt.float32, kind="ExternalOutput").ap()
    gnn_kernel(nc, ins, out)
    r = _run(nc, [arrays], core_ids=[0])
    return _np.asarray(r.results[0]["out_0_dram"]).reshape(NODES, D)[:nodes]
```
